# Optimizing a Trainium2 kernel written in Bass

```python
import numpy as np
import jax
import jax.numpy as jnp

def _softmax(x, axis=-1):
    return jax.nn.softmax(x, axis=axis)

def _gelu(x):
    return jax.nn.gelu(x, approximate=True)

def _silu(x):
    return jax.nn.silu(x)

def _sigmoid(x):
    return jax.nn.sigmoid(x)

def _layernorm(x, axis=-1, eps=1e-05):
    m = jnp.mean(x, axis=axis, keepdims=True)
    v = jnp.var(x, axis=axis, keepdims=True)
    return (x - m) / jnp.sqrt(v + eps)

def _scatter_add(tgt, idx, src, axis=0):
    return tgt.at[idx].add(src)

def _segment_sum(src, seg, n):
    return jax.ops.segment_sum(src, seg, n)
kernel_name = 'mk_gnn_resnorm_d4_gnn_r32_caafef'

def setup_inputs(seed: int=0):
    np.random.seed(seed)
    _w = jnp.asarray

    def _rec_inputs():
        import jax
        import jax.numpy as jnp
        _gk = jax.random.key(seed)
        x = -0.0005121 + 1.001 * jax.random.normal(jax.random.fold_in(_gk, 1), (3125, 32), jnp.float32)
        src = jax.random.randint(jax.random.fold_in(_gk, 2), (50000,), 0, 3125, jnp.int32)
        dst = jnp.minimum((3125 * jax.random.uniform(jax.random.fold_in(_gk, 3), (50000,)) ** 2.0).astype(jnp.int32), 99999)
        _o = jnp.argsort(dst, stable=True)
        src = src[_o]
        dst = dst[_o]
        edge_attr_32 = -5.3897e-05 + 0.999841 * jax.random.normal(jax.random.fold_in(_gk, 13), (50000, 32), jnp.float32)
        return (x, src, dst, edge_attr_32)
    x, src, dst, edge_attr_32 = _rec_inputs()

    def _L0_gnn_setup():
        import jax, jax.numpy as jnp
        import numpy as np
        N = 3125
        E = 25000
        H = 4
        D = 32
        NL = 3
        DN = 32
        DE = 32

        def _egat_layer(nf, ef, src, dst, W_ni, W_nj, W_fij, W_node, attn, bias):
            f_ni = nf @ W_ni
            f_nj = nf @ W_nj
            f_fij = ef @ W_fij
            f_out = f_ni[src] + f_nj[dst] + f_fij + bias
            f_out = jax.nn.leaky_relu(f_out, 0.2).reshape(-1, H, D)
            e = jnp.einsum('ehd,hd->eh', f_out, attn)
            emax = jax.ops.segment_max(e, dst, num_segments=N)
            a = jnp.exp(e - emax[dst])
            denom = jax.ops.segment_sum(a, dst, num_segments=N)
            a = a / denom[dst]
            h = (nf @ W_node).reshape(-1, H, D)
            m = h[src] * a[:, :, None]
            h_out = jax.ops.segment_sum(m, dst, num_segments=N)
            return (h_out, f_out)
        key = jax.random.key(seed)
        ks = jax.random.split(key, 10)
        s = 1.0 / np.sqrt(DN)
        inp = {'nf': jax.random.normal(ks[0], (N, DN), jnp.float32), 'ef': jax.random.normal(ks[1], (E, DE), jnp.float32), 'src': jax.random.randint(ks[2], (E,), 0, N, jnp.int32), 'dst': jax.random.randint(ks[3], (E,), 0, N, jnp.int32), 'W_ni': jax.random.normal(ks[4], (NL, DN, H * D), jnp.float32) * s, 'W_nj': jax.random.normal(ks[5], (NL, DN, H * D), jnp.float32) * s, 'W_fij': jax.random.normal(ks[6], (NL, DE, H * D), jnp.float32) * s, 'W_node': jax.random.normal(ks[7], (NL, DN, H * D), jnp.float32) * s, 'attn': jax.random.normal(ks[8], (NL, H, D), jnp.float32) * s, 'bias': jnp.zeros((NL, H * D), jnp.float32)}
        return inp
    _L0_gnn_all = _L0_gnn_setup()
    _L0_gnn_in = {k: v for k, v in _L0_gnn_all.items() if k in ('W_ni', 'W_nj', 'W_fij', 'W_node', 'attn', 'bias')}
    del _L0_gnn_all

    def _L1_gnn_setup():
        import jax, jax.numpy as jnp
        import numpy as np
        N_NODES = 3125
        N_EDGES = 50000
        IN_CH = 32
        HID = 128
        OUT_CH = 32

        def _glorot(key, shape):
            fan_in, fan_out = (shape[1], shape[0])
            lim = (6.0 / (fan_in + fan_out)) ** 0.5
            return jax.random.uniform(key, shape, jnp.float32, -lim, lim)

        def _sage_conv(x, src, dst, W_l, W_r, b):
            agg = jax.ops.segment_sum(x[src], dst, num_segments=N_NODES)
            deg = jax.ops.segment_sum(jnp.ones((src.shape[0],), x.dtype), dst, num_segments=N_NODES)
            agg = agg / jnp.maximum(deg, 1.0)[:, None]
            return agg @ W_l.T + x @ W_r.T + b
        key = jax.random.key(seed)
        ks = jax.random.split(key, 8)
        x = jax.random.normal(ks[0], (N_NODES, IN_CH), jnp.float32)
        edge_index = jax.random.randint(ks[1], (2, N_EDGES), 0, N_NODES, jnp.int64)
        W1_l = _glorot(ks[2], (HID, IN_CH))
        W1_r = _glorot(ks[3], (HID, IN_CH))
        b1 = jnp.zeros((HID,), jnp.float32)
        W2_l = _glorot(ks[4], (OUT_CH, HID))
        W2_r = _glorot(ks[5], (OUT_CH, HID))
        b2 = jnp.zeros((OUT_CH,), jnp.float32)
        return {'x': x, 'edge_index': edge_index, 'W1_l': W1_l, 'W1_r': W1_r, 'b1': b1, 'W2_l': W2_l, 'W2_r': W2_r, 'b2': b2}
    _L1_gnn_all = _L1_gnn_setup()
    _L1_gnn_in = {k: v for k, v in _L1_gnn_all.items() if k in ('W1_l', 'W1_r', 'b1', 'W2_l', 'W2_r', 'b2')}
    del _L1_gnn_all

    def _L2_gnn_setup():
        import jax, jax.numpy as jnp
        import numpy as np
        N, D, E = (3125, 32, 50000)
        EH, NH = (32, 16)
        TAU = 0.1
        key = jax.random.key(seed)
        ks = jax.random.split(key, 12)
        x = jax.random.normal(ks[0], (N, D), dtype=jnp.float32)
        edge_index = jax.random.randint(ks[1], (2, E), 0, N, dtype=jnp.int32)
        hsd = jax.random.normal(ks[2], (N,), dtype=jnp.float32)
        s_e1 = 1.0 / np.sqrt(D + 2)
        s_e2 = 1.0 / np.sqrt(EH)
        s_n2 = 1.0 / np.sqrt(NH)
        We1 = jax.random.uniform(ks[3], (D + 2, EH), jnp.float32, -s_e1, s_e1)
        be1 = jax.random.uniform(ks[4], (EH,), jnp.float32, -s_e1, s_e1)
        We2 = jax.random.uniform(ks[5], (EH, 1), jnp.float32, -s_e2, s_e2)
        be2 = jax.random.uniform(ks[6], (1,), jnp.float32, -s_e2, s_e2)
        Wn1 = jax.random.uniform(ks[7], (1, NH), jnp.float32, -1.0, 1.0)
        bn1 = jax.random.uniform(ks[8], (NH,), jnp.float32, -1.0, 1.0)
        Wn2 = jax.random.uniform(ks[9], (NH, 1), jnp.float32, -s_n2, s_n2)
        bn2 = jax.random.uniform(ks[10], (1,), jnp.float32, -s_n2, s_n2)
        return {'x': x, 'hsd': hsd, 'We1': We1, 'be1': be1, 'We2': We2, 'be2': be2, 'Wn1': Wn1, 'bn1': bn1, 'Wn2': Wn2, 'bn2': bn2, 'edge_index': edge_index}
    _L2_gnn_all = _L2_gnn_setup()
    _L2_gnn_in = {k: v for k, v in _L2_gnn_all.items() if k in ('We1', 'be1', 'We2', 'be2', 'Wn1', 'bn1', 'Wn2', 'bn2')}
    del _L2_gnn_all

    def _L3_gnn_setup():
        import jax, jax.numpy as jnp
        import numpy as np
        N = 3125
        E = 50000
        H = 4
        D = 32
        IN = 32
        NEG_SLOPE = 0.2
        key = jax.random.key(seed)
        ks = jax.random.split(key, 9)
        h = jax.random.normal(ks[0], (N, IN), jnp.float32)
        src = jax.random.randint(ks[1], (E,), 0, N, jnp.int32)
        dst = jax.random.randint(ks[2], (E,), 0, N, jnp.int32)
        W_fc = jax.random.normal(ks[3], (IN, H * D), jnp.float32) / np.sqrt(IN).astype(np.float32)
        attn_l = jax.random.normal(ks[4], (H, D), jnp.float32) * 0.1
        attn_r = jax.random.normal(ks[5], (H, D), jnp.float32) * 0.1
        bias_gat = jnp.zeros((H * D,), jnp.float32)
        W_out = jax.random.normal(ks[6], (H * D, D), jnp.float32) / np.sqrt(H * D).astype(np.float32)
        b_out = jnp.zeros((D,), jnp.float32)
        return {'h': h, 'src': src, 'dst': dst, 'W_fc': W_fc, 'attn_l': attn_l, 'attn_r': attn_r, 'bias_gat': bias_gat, 'W_out': W_out, 'b_out': b_out}
    _L3_gnn_all = _L3_gnn_setup()
    _L3_gnn_in = {k: v for k, v in _L3_gnn_all.items() if k in ('W_fc', 'attn_l', 'attn_r', 'bias_gat', 'W_out', 'b_out')}
    del _L3_gnn_all
    return {'x': x, 'src': src, 'dst': dst, 'edge_attr_32': edge_attr_32, 'L0_gnn_W_ni': _L0_gnn_in['W_ni'], 'L0_gnn_W_nj': _L0_gnn_in['W_nj'], 'L0_gnn_W_fij': _L0_gnn_in['W_fij'], 'L0_gnn_W_node': _L0_gnn_in['W_node'], 'L0_gnn_attn': _L0_gnn_in['attn'], 'L0_gnn_bias': _L0_gnn_in['bias'], 'L1_gnn_W1_l': _L1_gnn_in['W1_l'], 'L1_gnn_W1_r': _L1_gnn_in['W1_r'], 'L1_gnn_b1': _L1_gnn_in['b1'], 'L1_gnn_W2_l': _L1_gnn_in['W2_l'], 'L1_gnn_W2_r': _L1_gnn_in['W2_r'], 'L1_gnn_b2': _L1_gnn_in['b2'], 'L2_gnn_We1': _L2_gnn_in['We1'], 'L2_gnn_be1': _L2_gnn_in['be1'], 'L2_gnn_We2': _L2_gnn_in['We2'], 'L2_gnn_be2': _L2_gnn_in['be2'], 'L2_gnn_Wn1': _L2_gnn_in['Wn1'], 'L2_gnn_bn1': _L2_gnn_in['bn1'], 'L2_gnn_Wn2': _L2_gnn_in['Wn2'], 'L2_gnn_bn2': _L2_gnn_in['bn2'], 'L3_gnn_W_fc': _L3_gnn_in['W_fc'], 'L3_gnn_attn_l': _L3_gnn_in['attn_l'], 'L3_gnn_attn_r': _L3_gnn_in['attn_r'], 'L3_gnn_bias_gat': _L3_gnn_in['bias_gat'], 'L3_gnn_W_out': _L3_gnn_in['W_out'], 'L3_gnn_b_out': _L3_gnn_in['b_out']}

def reference(x, src, dst, edge_attr_32, L0_gnn_W_ni, L0_gnn_W_nj, L0_gnn_W_fij, L0_gnn_W_node, L0_gnn_attn, L0_gnn_bias, L1_gnn_W1_l, L1_gnn_W1_r, L1_gnn_b1, L1_gnn_W2_l, L1_gnn_W2_r, L1_gnn_b2, L2_gnn_We1, L2_gnn_be1, L2_gnn_We2, L2_gnn_be2, L2_gnn_Wn1, L2_gnn_bn1, L2_gnn_Wn2, L2_gnn_bn2, L3_gnn_W_fc, L3_gnn_attn_l, L3_gnn_attn_r, L3_gnn_bias_gat, L3_gnn_W_out, L3_gnn_b_out):
    import jax
    import jax.numpy as jnp

    def _L0_gnn_ref(nf, ef, src, dst, W_ni, W_nj, W_fij, W_node, attn, bias):
        import jax, jax.numpy as jnp
        import numpy as np
        N = 3125
        E = 25000
        H = 4
        D = 32
        NL = 3
        DN = 32
        DE = 32

        def _egat_layer(nf, ef, src, dst, W_ni, W_nj, W_fij, W_node, attn, bias):
            f_ni = nf @ W_ni
            f_nj = nf @ W_nj
            f_fij = ef @ W_fij
            f_out = f_ni[src] + f_nj[dst] + f_fij + bias
            f_out = jax.nn.leaky_relu(f_out, 0.2).reshape(-1, H, D)
            e = jnp.einsum('ehd,hd->eh', f_out, attn)
            emax = jax.ops.segment_max(e, dst, num_segments=N)
            a = jnp.exp(e - emax[dst])
            denom = jax.ops.segment_sum(a, dst, num_segments=N)
            a = a / denom[dst]
            h = (nf @ W_node).reshape(-1, H, D)
            m = h[src] * a[:, :, None]
            h_out = jax.ops.segment_sum(m, dst, num_segments=N)
            return (h_out, f_out)
        for l in range(NL):
            nfh, efh = _egat_layer(nf, ef, src, dst, W_ni[l], W_nj[l], W_fij[l], W_node[l], attn[l], bias[l])
            nf = nfh.mean(axis=1)
            ef = efh.mean(axis=1)
        return nf

    def _L1_gnn_ref(x, edge_index, W1_l, W1_r, b1, W2_l, W2_r, b2):
        import jax, jax.numpy as jnp
        import numpy as np
        N_NODES = 3125
        N_EDGES = 50000
        IN_CH = 32
        HID = 128
        OUT_CH = 32

        def _glorot(key, shape):
            fan_in, fan_out = (shape[1], shape[0])
            lim = (6.0 / (fan_in + fan_out)) ** 0.5
            return jax.random.uniform(key, shape, jnp.float32, -lim, lim)

        def _sage_conv(x, src, dst, W_l, W_r, b):
            agg = jax.ops.segment_sum(x[src], dst, num_segments=N_NODES)
            deg = jax.ops.segment_sum(jnp.ones((src.shape[0],), x.dtype), dst, num_segments=N_NODES)
            agg = agg / jnp.maximum(deg, 1.0)[:, None]
            return agg @ W_l.T + x @ W_r.T + b
        src, dst = (edge_index[0], edge_index[1])
        h = _sage_conv(x, src, dst, W1_l, W1_r, b1)
        h = jax.nn.relu(h)
        out = _sage_conv(h, src, dst, W2_l, W2_r, b2)
        return out

    def _L2_gnn_ref(x, hsd, We1, be1, We2, be2, Wn1, bn1, Wn2, bn2, edge_index):
        import jax, jax.numpy as jnp
        import numpy as np
        N, D, E = (3125, 32, 50000)
        EH, NH = (32, 16)
        TAU = 0.1
        row, col = (edge_index[0], edge_index[1])
        n = x.shape[0]
        hsd_norm = (hsd - hsd.mean()) / (jnp.std(hsd, ddof=1) + 1e-08)
        diff_abs = jnp.abs(x[row] - x[col])
        edge_in = jnp.concatenate([hsd_norm[row][:, None], hsd_norm[col][:, None], diff_abs], axis=1)
        h = jax.nn.relu(edge_in @ We1 + be1)
        e_uv = (h @ We2 + be2)[:, 0]
        logits = e_uv / TAU
        seg_max = jax.ops.segment_max(logits, col, num_segments=n)
        seg_max = jnp.where(jnp.isfinite(seg_max), seg_max, 0.0)
        ex = jnp.exp(logits - seg_max[col])
        denom = jax.ops.segment_sum(ex, col, num_segments=n)
        alpha_uv = (ex / (denom[col] + 1e-16))[:, None]
        gh = jax.nn.relu(hsd_norm[:, None] @ Wn1 + bn1)
        alpha_bar = jax.nn.sigmoid(gh @ Wn2 + bn2)
        ones = jnp.ones(row.shape[0], dtype=x.dtype)
        src_deg = jnp.sqrt(jnp.clip(jax.ops.segment_sum(ones, row, num_segments=n), 1.0))
        dst_deg = jnp.sqrt(jnp.clip(jax.ops.segment_sum(ones, col, num_segments=n), 1.0))
        edge_w = 1.0 / (src_deg[row] * dst_deg[col])
        low_pass = jax.ops.segment_sum(edge_w[:, None] * x[row], col, num_segments=n)
        high_pass = jax.ops.segment_sum(alpha_uv * (x[col] - x[row]), col, num_segments=n)
        return (1.0 - alpha_bar) * low_pass + alpha_bar * high_pass

    def _L3_gnn_ref(h, src, dst, W_fc, attn_l, attn_r, bias_gat, W_out, b_out):
        import jax, jax.numpy as jnp
        import numpy as np
        N = 3125
        E = 50000
        H = 4
        D = 32
        IN = 32
        NEG_SLOPE = 0.2
        feat = (h @ W_fc).reshape(N, H, D)
        el = jnp.einsum('nhd,hd->nh', feat, attn_l)
        er = jnp.einsum('nhd,hd->nh', feat, attn_r)
        e = el[src] + er[dst]
        e = jnp.where(e > 0, e, NEG_SLOPE * e)
        emax = jax.ops.segment_max(e, dst, num_segments=N)
        ex = jnp.exp(e - emax[dst])
        denom = jax.ops.segment_sum(ex, dst, num_segments=N)
        alpha = ex / jnp.maximum(denom[dst], 1e-09)
        msg = feat[src] * alpha[:, :, None]
        rst = jax.ops.segment_sum(msg, dst, num_segments=N)
        rst = rst.reshape(N, H * D) + bias_gat
        out = rst @ W_out + b_out
        out = jnp.where(out > 0, out, jnp.expm1(out))
        return h + out
    edge_index = jnp.stack([src, dst])
    deg = jnp.maximum(jax.ops.segment_sum(jnp.ones(dst.shape, jnp.float32), dst, num_segments=3125), 1.0)
    x = _layernorm(x + _L0_gnn_ref(x, edge_attr_32, src, dst, L0_gnn_W_ni, L0_gnn_W_nj, L0_gnn_W_fij, L0_gnn_W_node, L0_gnn_attn, L0_gnn_bias), axis=-1)
    x = _layernorm(x + _L1_gnn_ref(x, edge_index, L1_gnn_W1_l, L1_gnn_W1_r, L1_gnn_b1, L1_gnn_W2_l, L1_gnn_W2_r, L1_gnn_b2), axis=-1)
    x = _layernorm(x + _L2_gnn_ref(x, deg, L2_gnn_We1, L2_gnn_be1, L2_gnn_We2, L2_gnn_be2, L2_gnn_Wn1, L2_gnn_bn1, L2_gnn_Wn2, L2_gnn_bn2, edge_index), axis=-1)
    x = _layernorm(x + _L3_gnn_ref(x, src, dst, L3_gnn_W_fc, L3_gnn_attn_l, L3_gnn_attn_r, L3_gnn_bias_gat, L3_gnn_W_out, L3_gnn_b_out), axis=-1)
    return x

_drawn_inputs = setup_inputs


def setup_inputs(seed=0):
    import zlib

    import numpy as np

    out = dict(_drawn_inputs(seed))
    spreads = {'L0_gnn_bias': (0.0, 0.8),
     'L1_gnn_b1': (0.0, 0.1),
     'L1_gnn_b2': (0.0, 0.1),
     'L3_gnn_bias_gat': (0.0, 0.299),
     'L3_gnn_b_out': (0.0, 0.1)}
    factors = {'edge_attr_32': 8.0,
     'L0_gnn_W_ni': 3.817,
     'L0_gnn_W_nj': 8.0,
     'L0_gnn_W_fij': 8.0,
     'L0_gnn_W_node': 3.312,
     'L0_gnn_attn': 5.544,
     'L2_gnn_Wn1': 23.593,
     'L2_gnn_bn1': 3.076,
     'L3_gnn_attn_r': 3.069,
     'L2_gnn_be1': 2.982}
    for name, (base, spread) in spreads.items():
        noise = np.random.default_rng([zlib.crc32(name.encode()), seed]).standard_normal(out[name].shape)
        drawn = base * np.exp(spread * noise) if base else spread * noise
        out[name] = jnp.asarray(drawn.astype(out[name].dtype))
    for name, factor in factors.items():
        out[name] = (out[name] * factor).astype(out[name].dtype)
    return out
```

```python
import concourse.bass as bass
from concourse import mybir
from contextlib import ExitStack

N, E, C, H = 3125, 50000, 32, 4
P = 125
T = E // P
J = N // P
TC = 40
NCH = T // TC
GT = 4
NG = TC // GT
HB = 10
NHB = T // HB
CW = C + 1
ROW = H * CW + H
SW = 100
GW = 37
BIG = 1.0e30
MAGIC = 12582912.0
LN_EPS = 1e-5
NEG_SLOPE = 0.2
EDGE_SPLIT = 112

W_OFF = {}


def _w_layout():
    at = 0
    for name, n in (("edge", 3 * 128), ("att", 3 * H), ("node", 3 * C), ("sage1", 128), ("sage2", 2 * C),
                    ("filt1", 32), ("filt2", 1), ("wfc", 128), ("wfc_row", 128), ("attn_lr", 2 * 128),
                    ("wout", C), ("bias_gat", 1), ("be1", 1), ("be2", 1), ("b2", C), ("bout", C),
                    ("wn1", 16), ("bn1", 16), ("wn2", 16), ("bn2", 1)):
        W_OFF[name] = (at, n)
        at += n
    return at


WCOLS = _w_layout()
C_OFF = {"ident": (0, 128), "ones": (128, 128), "tri": (256, 128), "triT": (384, 128), "mean": (512, 32),
         "iota": (544, 128), "col": (672, 1)}
CCOLS = 673

PASSES = ("egat", "egat", "egat", "sage", "sage", "filter", "gat")
KIND = {
    "egat": dict(src_w=C, src_at=0, dst_w=C, dst_at=65, heads=H, plain=0, feat=97, hid=128, le=36),
    "sage": dict(src_w=C, src_at=0, dst_w=0, dst_at=0, heads=0, plain=C, plain_at=0, feat=0),
    "filter": dict(src_w=35, src_at=33, dst_w=33, dst_at=0, heads=1, x_at=34, plain=C, plain_at=68,
                   feat=34, hid=32, le=1),
    "gat": dict(src_w=37, src_at=0, dst_w=H, dst_at=40, heads=H, plain=0, feat=0),
}
NP = len(PASSES)


def before(i, test):
    return sum(1 for k in PASSES[:i] if test(KIND[k]))


def graph_kernel(nc, x, src, dst, edge_attr, wpack, cpack, out):
    f32, i32, bf16 = mybir.dt.float32, mybir.dt.int32, mybir.dt.bfloat16
    ALU, ACT, AX = mybir.AluOpType, mybir.ActivationFunctionType, mybir.AxisListType.X

    def dram(name, shape):
        return nc.dram_tensor(name, shape, f32).ap()

    run_start_rows = dram("run_start_rows", (E, CW))
    dst_table = dram("dst_table", (N, CW))
    message_rows = {k: dram(f"message_rows_{k}", (E, ROW if k in ("egat", "gat") else C if k == "sage" else 66))
                    for k in KIND}
    src_tables = [x] + [dram(f"src_table_{i}", (N, KIND[PASSES[i]]["src_w"])) for i in range(1, NP)]
    carry_owner_d = dram("carry_owner_d", (N,))

    ctx = ExitStack()
    with ctx:
        def sb(name, shape, dt=f32):
            return ctx.enter_context(nc.sbuf_tensor(name, shape, dt))

        def pb(name):
            return ctx.enter_context(nc.psum_tensor(name, [128, 512], f32))

        def sem(name):
            return ctx.enter_context(nc.semaphore(name))

        W = sb("W", [128, WCOLS])
        CS = sb("CS", [128, CCOLS])

        def w(name, rows=128):
            a, n = W_OFF[name]
            return W[0:rows, a:a + n]

        def cst(name, rows=P, cols=None):
            a, n = C_OFF[name]
            return CS[0:rows, a:a + (cols or n)]

        src_i = sb("src_i", [P, T + 2 * TC], i32)
        src_ring = sb("src_ring", [P, 2, TC], i32)
        first_i = sb("first_i", [P, 1], i32)
        prev_i = sb("prev_i", [P, 1], i32)
        same = sb("same", [P, T])
        same_neg = sb("same_neg", [P, T])
        edge_feat = sb("edge_feat", [P, T, C])
        gathered = sb("gathered", [P, 2, TC * GW])
        stage = sb("stage", [P, 2, TC, SW])
        dst_in = sb("dst_in", [P, 2, TC, CW])
        dst_first = sb("dst_first", [P, CW])
        featT = sb("featT", [128, 2, GT * P])
        hidT = sb("hidT", [128, 2, GT * P])
        hid_negT = sb("hid_negT", [128, 2, GT * P])
        logits = sb("logits", [P, 2, TC * H])
        run_max = sb("run_max", [P, TC + 1, H])
        w_arg = sb("w_arg", [P, TC * H])
        d_arg = sb("d_arg", [P, TC * H])
        decay = sb("decay", [P, TC * H])
        msg = sb("msg", [P, 2, TC * ROW])
        att = sb("att", [128, 3, 36])
        att_neg = sb("att_neg", [128, 3, 36])
        wlr = sb("wlr", [C, 2 * H])
        X = sb("X", [P, J, C])
        nf = sb("nf", [P, J, CW])
        sdeg = sb("sdeg", [P, J])
        nd = sb("nd", [P, 10, J])
        end_i = sb("end_i", [P, J], i32)
        start_i = sb("start_i", [P, J], i32)
        owner = sb("owner", [P, N])
        tail = sb("tail", [P, ROW])
        carry = sb("carry", [P, ROW])
        carry_max = sb("carry_max", [P, H])
        cont01 = sb("cont01", [P, P])
        cont_neg = sb("cont_neg", [P, P])
        contT_neg = sb("contT_neg", [P, P])
        sm = sb("sm", [P, 8, J])
        deg = sm[:, 4, :]
        hw = sb("hw", [P, 5, J * H])
        yt = sb("yt", [P, J, C])
        rr = sb("rr", [P, J, C])
        lr_tmp = rr[0:C, :, :].rearrange("p j c -> p (j c)")[:, 0:128]
        dst_last = sb("dst_last", [P, CW])
        be2s = sb("be2s", [P, 1])
        tot = sb("tot", [P, 2])

        dst_in_flat = dst_in[:, :, :, :].rearrange("p a t c -> p (a t c)")
        id_f, hi_f, lo_f = (dst_in_flat[:, n * T:(n + 1) * T] for n in range(3))
        dst_i = dst_in_flat[:, 3 * T:4 * T].bitcast(i32)
        dst_f = dst_in_flat[:, 4 * T:5 * T]

        def hot(slot):
            b = (featT, hidT)[slot][0:P, :, :].rearrange("p a b -> p (a b)").bitcast(bf16)
            return (b[:, 0:HB * P].rearrange("p (t n) -> p t n", n=P),
                    b[:, HB * P:HB * (P + J)].rearrange("p (t n) -> p t n", n=J))

        def ends_view(width):
            return msg[:, 0, 0:J * width].rearrange("p (j c) -> p j c", c=width)

        aggregate = msg[:, 1, 0:J * 128].rearrange("p (j c) -> p j c", c=128)
        stage_flat = stage[:, 0, :, :].rearrange("p t c -> p (t c)")

        def carried_view(width):
            return stage_flat[:, 0:J * width].rearrange("p (j c) -> p j c", c=width)

        pair = stage[:, 1, :, :].rearrange("p t c -> p (t c)")
        diag = featT[0:P, :, :].rearrange("p a b -> p (a b)")[:, 0:H * P]
        seen = hidT[0:P, :, :].rearrange("p a b -> p (a b)")[:, 0:H * P]
        weights_pq = featT[0:P, :, :].rearrange("p a b -> p (a b)")[:, H * P:2 * H * P]

        bank = [pb(f"bank{i}") for i in range(8)]
        ps_featT, ps_hid, ps_le, ps_w, ps_misc = bank[0:2], bank[2:4], bank[4:6], bank[6], bank[7]

        s_const = sem("s_const")
        s_apart = sem("s_apart")
        s_idx_in = sem("s_idx_in")
        s_dst_in = sem("s_dst_in")
        s_ef_in = sem("s_ef_in")
        s_x_in = sem("s_x_in")
        s_zero = sem("s_zero")
        s_zeroed = sem("s_zeroed")
        s_ones_col = sem("s_ones_col")
        s_v = sem("s_v")
        s_a = sem("s_a")
        s_att = sem("s_att")
        s_hot = sem("s_hot")
        s_hist = sem("s_hist")
        s_tot = sem("s_tot")
        s_off = sem("s_off")
        s_rows = sem("s_rows")
        s_rowsd = sem("s_rowsd")
        s_wlr = sem("s_wlr")
        s_setup = sem("s_setup")
        s_place = sem("s_place")
        s_owner_w = sem("s_owner_w")
        s_owner_r = sem("s_owner_r")
        s_ring = sem("s_ring")
        s_gather = [sem("s_gather0"), sem("s_gather1")]
        s_staged = sem("s_staged")
        s_ef = sem("s_ef")
        s_free = sem("s_free")
        s_dstrow = [sem("s_dstrow0"), sem("s_dstrow1")]
        s_filled = sem("s_filled")
        s_fscan = sem("s_fscan")
        s_fsub = sem("s_fsub")
        s_T = sem("s_T")
        s_featT = sem("s_featT")
        s_main = sem("s_main")
        s_hid = sem("s_hid")
        s_le = sem("s_le")
        s_lec = sem("s_lec")
        s_mcar = sem("s_mcar")
        s_lg = sem("s_lg")
        s_max = sem("s_max")
        s_max2 = sem("s_max2")
        s_arg = sem("s_arg")
        s_exp = sem("s_exp")
        s_mult = sem("s_mult")
        s_scan = sem("s_scan")
        s_store = [sem("s_store0"), sem("s_store1")]
        s_scatter = sem("s_scatter")
        s_first = sem("s_first")
        s_diag = sem("s_diag")
        s_bcast = sem("s_bcast")
        s_carg = sem("s_carg")
        s_cexp = sem("s_cexp")
        s_carry_mm = sem("s_carry_mm")
        s_carry = sem("s_carry")
        s_sel = sem("s_sel")
        s_selc = sem("s_selc")
        s_ends = sem("s_ends")
        s_narg = sem("s_narg")
        s_nexp = sem("s_nexp")
        s_agg = sem("s_agg")
        s_nT = sem("s_nT")
        s_nTc = sem("s_nTc")
        s_nh = sem("s_nh")
        s_nhc = sem("s_nhc")
        s_xT = sem("s_xT")
        s_no = sem("s_no")
        s_noc = sem("s_noc")
        s_var = sem("s_var")
        s_std = sem("s_std")
        s_sq = sem("s_sq")
        s_sqd = sem("s_sqd")
        s_gate = sem("s_gate")
        s_gated = sem("s_gated")
        s_elu = sem("s_elu")
        s_elud = sem("s_elud")
        s_table = sem("s_table")
        s_table_w = sem("s_table_w")
        s_out = sem("s_out")

        block = ctx.enter_context(nc.Block())

        def wait(eng, s, value):
            if isinstance(value, int) and value <= 0:
                return
            eng.wait_ge(s, value)

        def apart(eng):
            eng.sem_inc(s_apart, 1)

        def chunk_no(i, c):
            return i * NCH + c

        def dst_chunk_no(i, c):
            return before(i, lambda k: k["dst_w"]) * NCH + c

        def soft_chunk_no(i, c):
            return before(i, lambda k: k["heads"]) * NCH + c

        def group_no(i, c, g):
            return (before(i, lambda k: k["feat"]) * NCH + c) * NG + g

        def cols(c):
            return bass.ds(c * TC, TC)

        def slot_turn(i, c, slot):
            return i * (NCH // 2) + ((c - slot) // 2 if isinstance(c, int) else c)

        def chunks(eng, body):
            for slot in range(2):
                body(slot, slot, 0)
            with eng.Fori(1, NCH // 2) as k:
                for slot in range(2):
                    body(2 * k + slot, slot, k)

        NSEL = 3
        SEL = [(j, min(NSEL, J - j)) for j in range(0, J, NSEL)]
        NT = [(j, min(4, J - j)) for j in range(0, J, 4)]
        TPASS = [i for i in range(NP) if PASSES[i] == "egat"] + [3, 6]
        PROD = {"egat": dict(k=128, hid=None, m=C), "sage": dict(k=65, hid="sage1", m=2 * C),
                "gat": dict(k=128, hid="wfc", m=C)}

        def prod_no(i):
            return sum(1 for t in TPASS if t < i)

        def hid_no(i):
            return sum(1 for t in TPASS if t < i and PROD[PASSES[t]]["hid"])

        def width(i):
            return {"egat": ROW, "gat": ROW, "filter": 66, "sage": C}[PASSES[i]]

        @block.sync
        def _(sp):
            sp.dma_start(src_i[:, 0:T], src.rearrange("(p t) -> p t", t=T)).then_inc(s_idx_in, 16)
            sp.dma_start(src_i[:, T:T + 2 * TC], src.rearrange("(p t) -> p t", t=T)[:, 0:2 * TC]).then_inc(s_idx_in, 16)
            sp.dma_start(dst_i, dst.rearrange("(p t) -> p t", t=T)).then_inc(s_dst_in, 16)
            sp.dma_start(prev_i[1:P, :], dst.rearrange("(p t) -> p t", t=T)[0:P - 1, T - 1:T],
                         allow_slow_non_contiguous=True).then_inc(s_dst_in, 16)
            sp.dma_start(W[:, :], wpack).then_inc(s_const, 16)
            sp.dma_start(CS[:, :], cpack).then_inc(s_const, 16)
            sp.dma_start(X[:, :, :], x.rearrange("(p j) c -> p j c", j=J)).then_inc(s_x_in, 16)
            ea = edge_attr.rearrange("(p t) c -> p t c", t=T)
            sp.dma_start(edge_feat[0:EDGE_SPLIT, :, :], ea[0:EDGE_SPLIT]).then_inc(s_ef_in, 16)
            sp.dma_start(edge_feat[EDGE_SPLIT:P, :, :], ea[EDGE_SPLIT:P]).then_inc(s_ef_in, 16)
            sp.wait_ge(s_zero, 1)
            rs = run_start_rows.rearrange("(p t) c -> p t c", t=T)
            for c in range(NCH):
                sp.dma_start(rs[:, c * TC:(c + 1) * TC, :],
                             msg[:, 0, 0:TC * CW].rearrange("p (t c) -> p t c", c=CW)).then_inc(s_zeroed, 16)
            sp.wait_ge(s_place, 1)
            sp.dma_start(carry_owner_d.rearrange("(p j) -> p j", j=J), nd[:, 6, :]).then_inc(s_owner_w, 16)
            sp.wait_ge(s_owner_w, 16)
            sp.dma_start(owner[:, :], carry_owner_d.rearrange("(a n) -> a n", a=1).broadcast_to([P, N])).then_inc(s_owner_r, 16)

            for i in range(NP):
                k = KIND[PASSES[i]]
                wd = width(i)
                rows = message_rows[PASSES[i]].rearrange("(p t) c -> p t c", t=T)
                if i == 0:
                    sp.wait_ge(s_rows, 1)
                    sp.dma_start(dst_table.rearrange("(p j) c -> p j c", j=J), nf[:, :, :]).then_inc(s_table_w, 16)
                else:
                    sp.wait_ge(s_table, i)
                    tw = k["src_w"]
                    from_ = (yt[:, :, :] if PASSES[i] == "egat" or i == 4 else X[:, :, :] if i == 3 else
                             pair[:, 0:J * tw].rearrange("p (j c) -> p j c", c=tw))
                    sp.dma_start(src_tables[i].rearrange("(p j) c -> p j c", j=J), from_).then_inc(s_table_w, 16)
                    if k["dst_w"]:
                        sp.dma_start(dst_table.rearrange("(p j) c -> p j c", j=J), nf[:, :, :]).then_inc(s_table_w, 16)
                if k["dst_w"]:
                    sp.wait_ge(s_scatter, 16 * J * (before(i, lambda k: k["dst_w"]) + 1))

                def load_dst(c, slot, turn):
                    wait(sp, s_filled, dst_chunk_no(i, c) - 1)
                    sp.dma_start(dst_in[:, slot, :, :], rs[:, cols(c), :]).then_inc(s_dstrow[slot], 16)

                def store(c, slot, turn):
                    sp.wait_ge(s_scan, chunk_no(i, c) + 1)
                    m = msg[:, slot, 0:TC * wd].rearrange("p (t c) -> p t c", c=wd)
                    sp.dma_start(rows[0:EDGE_SPLIT, cols(c), :], m[0:EDGE_SPLIT]).then_inc(s_store[slot], 16)
                    sp.dma_start(rows[EDGE_SPLIT:P, cols(c), :], m[EDGE_SPLIT:P]).then_inc(s_store[slot], 16)

                if k["dst_w"]:
                    if i == 0:
                        sp.wait_ge(s_setup, 1)
                    load_dst(0, 0, 0)
                    load_dst(1, 1, 0)
                    store(0, 0, 0)
                    load_dst(2, 0, 1)
                    store(1, 1, 0)
                    load_dst(3, 1, 1)
                    with sp.Fori(1, NCH // 2 - 1) as kk:
                        for slot in range(2):
                            store(2 * kk + slot, slot, kk)
                            load_dst(2 * kk + 2 + slot, slot, kk + 1)
                    store(NCH - 2, 0, NCH // 2 - 1)
                    store(NCH - 1, 1, NCH // 2 - 1)
                else:
                    chunks(sp, store)
            sp.wait_ge(s_table, NP)
            sp.dma_start(out.rearrange("(p j) c -> p j c", j=J), X[:, :, :]).then_inc(s_out, 16)
            sp.wait_ge(s_out, 16)

        @block.gpsimd
        def _(pool):
            at = bass.IndirectOffsetOnAxis
            tables = 0
            for i in range(NP):
                k = KIND[PASSES[i]]
                wd, tw = width(i), k["src_w"]
                if i:
                    tables += 1
                    pool.wait_ge(s_table_w, 16 * (tables + (1 if k["dst_w"] else 0)))
                if k["dst_w"]:
                    tables += 1

                def gather(c, slot, turn):
                    pool.wait_ge(s_ring, chunk_no(i, c) + 1)
                    wait(pool, s_staged, chunk_no(i, c) - 1)
                    apart(pool)
                    for t in range(TC):
                        pool.indirect_dma_start(gathered[:, slot, t * tw:(t + 1) * tw], None, src_tables[i],
                                                at(src_ring[:, slot, t:t + 1], 0)).then_inc(s_gather[slot], 16)

                def place():
                    if i == 0:
                        pool.wait_ge(s_place, 1)
                        pool.wait_ge(s_zeroed, 16 * NCH)
                        pool.wait_ge(s_table_w, 16)
                    if i:
                        pool.wait_ge(s_filled, dst_chunk_no(i, 0))
                    for j in range(J):
                        pool.indirect_dma_start(run_start_rows, at(start_i[:, j:j + 1], 0), nf[:, j, :], None,
                                                bounds_check=E - 1, oob_is_err=False).then_inc(s_scatter, 16)
                    pool.indirect_dma_start(dst_first[:, :], None, dst_table, at(first_i[:, 0:1], 0)).then_inc(s_first, 16)

                gather(0, 0, 0)
                if k["dst_w"] and i:
                    place()
                gather(1, 1, 0)
                if k["dst_w"] and not i:
                    place()
                with pool.Fori(1, NCH // 2) as kk:
                    for slot in range(2):
                        gather(2 * kk + slot, slot, kk)
                for slot in range(2):
                    pool.wait_ge(s_store[slot], 32 * (i + 1) * (NCH // 2))
                ends = ends_view(wd)
                for j in range(J):
                    pool.indirect_dma_start(ends[:, j, :], None, message_rows[PASSES[i]],
                                            at(end_i[:, j:j + 1], 0)).then_inc(s_ends, 16)

        @block.scalar
        def _(act):
            act.wait_ge(s_idx_in, 32)
            for slot in range(2):
                act.copy(src_ring[:, slot, :], src_i[:, slot * TC:(slot + 1) * TC]).then_inc(s_ring, 1)
            act.wait_ge(s_const, 32)
            act.wait_ge(s_ef_in, 32)
            act.wait_ge(s_ones_col, 1)
            for i in range(NP):
                kind = PASSES[i]
                k = KIND[kind]
                nh = k["heads"]

                def arrive(c, slot, turn):
                    act.wait_ge(s_gather[slot], 16 * TC * (i * (NCH // 2) + turn + 1))
                    apart(act)
                    act.copy(src_ring[:, slot, :], src_i[:, bass.ds((c + 2) * TC, TC)]).then_inc(s_ring, 1)
                    wait(act, s_free, chunk_no(i, c) - 1)
                    tw = k["src_w"]
                    act.copy(stage[:, slot, :, k["src_at"]:k["src_at"] + tw],
                             gathered[:, slot, 0:TC * tw].rearrange("p (t c) -> p t c", c=tw)).then_inc(s_staged, 1)
                    if kind == "egat":
                        act.copy(stage[:, slot, :, 33:65], edge_feat[:, cols(c), :]).then_inc(s_ef, 1)

                def feat_copy(c, g):
                    act.wait_ge(s_T, group_no(i, c, g) + 1)
                    wait(act, s_main, group_no(i, c, g) - 1)
                    act.copy(featT[0:k["feat"], g % 2, 0:GT * P], ps_featT[g % 2][0:k["feat"], 0:GT * P]).then_inc(s_featT, 1)

                def hidden(c, g):
                    act.wait_ge(s_main, group_no(i, c, g) + 1)
                    wait(act, s_le, group_no(i, c, g) - 1)
                    o, n = hidT[0:k["hid"], g % 2, 0:GT * P], ps_hid[g % 2][0:k["hid"], 0:GT * P]
                    if kind == "egat":
                        act.activation(o, n, ACT.Relu)
                        act.activation(hid_negT[0:k["hid"], g % 2, 0:GT * P], n, ACT.Relu, scale=-1.0).then_inc(s_hid, 1)
                    else:
                        act.activation(o, n, ACT.Relu, bias=w("be1", 32)).then_inc(s_hid, 1)

                def logit_copy(c, slot, g):
                    act.wait_ge(s_le, group_no(i, c, g) + 1)
                    le = ps_le[g % 2][0:P, 0:GT * k["le"]].rearrange("p (t c) -> p t c", c=k["le"])
                    lg = logits[:, slot, 0:TC * nh].rearrange("p (t h) -> p t h", h=nh)[:, g * GT:(g + 1) * GT, :]
                    if kind == "egat":
                        last = act.copy(lg, le[:, :, 0:H])
                        if i < 2:
                            last = act.copy(edge_feat[:, bass.ds(c * TC + g * GT, GT), :], le[:, :, H:36])
                        last.then_inc(s_lec, 1)
                    else:
                        act.activation(lg, le, ACT.Identity, scale=10.0, bias=be2s[:, 0:1]).then_inc(s_lec, 1)

                def chunk(c, slot, turn):
                    arrive(c, slot, turn)
                    if k["feat"]:
                        if kind == "filter" and isinstance(c, int) and c == 0:
                            act.wait_ge(s_place, 1)
                        for g in range(NG + 2):
                            if g < NG:
                                feat_copy(c, g)
                            if 1 <= g <= NG:
                                hidden(c, g - 1)
                            if g >= 2:
                                logit_copy(c, slot, g - 2)
                    if nh:
                        act.wait_ge(s_arg, soft_chunk_no(i, c) + 1)
                        act.activation(decay[:, 0:TC * nh], d_arg[:, 0:TC * nh], ACT.Exp)
                        act.activation(ps_w[0:P, 0:TC * nh], w_arg[:, 0:TC * nh], ACT.Exp).then_inc(s_exp, 1)

                chunks(act, chunk)

                if nh:
                    a = before(i, lambda k: k["heads"])
                    act.wait_ge(s_carg, a + 1)
                    for h in range(nh):
                        last = act.activation(weights_pq[:, h * P:(h + 1) * P], seen[:, h * P:(h + 1) * P], ACT.Exp,
                                              bias=tail[:, width(i) - nh + h:width(i) - nh + h + 1])
                    last.then_inc(s_cexp, 1)
                cv = carried_view(width(i))
                for n, (j, m) in enumerate(SEL):
                    act.wait_ge(s_sel, i * len(SEL) + n + 1)
                    act.copy(cv[:, j:j + m, :], bank[n % 2][0:P, 0:m * width(i)].rearrange("p (j c) -> p j c", c=width(i)))\
                       .then_inc(s_selc, 1)
                if nh:
                    act.wait_ge(s_narg, a + 1)
                    act.activation(hw[:, 2:4, 0:J * nh], hw[:, 0:2, 0:J * nh], ACT.Exp).then_inc(s_nexp, 1)
                if i in TPASS:
                    pr = PROD[kind]
                    b = prod_no(i) * len(NT)
                    hb = hid_no(i) * len(NT)
                    for n, (j, m) in enumerate(NT):
                        act.wait_ge(s_nT, b + n + 1)
                        act.copy(featT[0:pr["k"], n % 2, 0:m * P], bank[4 + n % 2][0:pr["k"], 0:m * P]).then_inc(s_nTc, 1)
                        if pr["hid"]:
                            act.wait_ge(s_nh, hb + n + 1)
                            o, v = hidT[:, n % 2, 0:m * P], bank[6][:, 0:m * P]
                            if kind == "sage":
                                act.activation(o, v, ACT.Relu).then_inc(s_nhc, 1)
                            else:
                                act.activation(o, v, ACT.Identity, bias=w("bias_gat")).then_inc(s_nhc, 1)
                if kind == "gat":
                    act.wait_ge(s_elu, 1)
                    act.activation(rr[:, :, :], rr[:, :, :], ACT.Exp).then_inc(s_elud, 1)
                if i == 4:
                    act.wait_ge(s_sq, 1)
                    act.activation(tot[:, 1:2], tot[:, 1:2], ACT.Sqrt)
                    act.activation(sm[:, 6:8, :], sm[:, 6:8, :], ACT.Sqrt).then_inc(s_sqd, 1)
                    act.wait_ge(s_gate, 1)
                    act.activation(nd[:, 0, :], nd[:, 0, :], ACT.Exp, scale=-1.0).then_inc(s_gated, 1)
                if i in (2, 4, 5, 6):
                    r = (2, 4, 5, 6).index(i)
                    act.wait_ge(s_var, r + 1)
                    act.activation(sm[:, 2, :], sm[:, 2, :], ACT.Sqrt).then_inc(s_std, 1)

        @block.tensor
        def _(pe):
            ident = cst("ident", P, P)
            ones = cst("ones", P, P)
            pe.wait_ge(s_const, 32)

            def histogram(turn):
                def count(b, slot, start=False, stop=False):
                    pe.wait_ge(s_hot, turn * NHB + b + 1)
                    for t in range(HB):
                        last = pe.matmul(ps_misc[0:P, 0:J], hot(slot)[0][:, t, :], hot(slot)[1][:, t, :],
                                         start=start and t == 0, stop=stop and t == HB - 1)
                    last.then_inc(s_hist, 1)

                count(0, 0, start=True)
                count(1, 1)
                with pe.Fori(1, NHB // 2 - 1) as kk:
                    for slot in range(2):
                        count(2 * kk + slot, slot)
                count(NHB - 2, 0)
                count(NHB - 1, 1, stop=True)

            histogram(0)
            pe.wait_ge(s_tot, 1)
            pe.matmul(ps_misc[0:P, 64:65], cst("tri", P, P), tot[:, 0:1], start=True, stop=True).then_inc(s_off, 1)
            pe.wait_ge(s_rowsd, 1)
            pe.matmul(bank[2][0:P, 0:2 * P], ones, diag[:, 0:2 * P], start=True, stop=True).then_inc(s_bcast, 1)

            for i in range(NP):
                kind = PASSES[i]
                k = KIND[kind]
                nh, wd = k["heads"], width(i)

                def transposes(c, slot, g):
                    wait(pe, s_featT, group_no(i, c, g) - 1)
                    if kind == "filter":
                        apart(pe)
                    for t in range(GT):
                        last = pe.transpose(ps_featT[g % 2][0:k["feat"], t * P:(t + 1) * P],
                                            stage[:, slot, g * GT + t, 0:k["feat"]], ident)
                    last.then_inc(s_T, 1)

                def main(c, g):
                    pe.wait_ge(s_featT, group_no(i, c, g) + 1)
                    wait(pe, s_hid, group_no(i, c, g) - 1)
                    if kind == "filter":
                        apart(pe)
                    lhs = w("edge", 97)[:, i * 128:(i + 1) * 128] if kind == "egat" else w("filt1", 34)
                    pe.matmul(ps_hid[g % 2][0:k["hid"], 0:GT * P], lhs, featT[0:k["feat"], g % 2, 0:GT * P],
                              start=True, stop=True).then_inc(s_main, 1)

                def logit(c, g):
                    pe.wait_ge(s_hid, group_no(i, c, g) + 1)
                    wait(pe, s_lec, group_no(i, c, g) - 1)
                    n = k["le"]
                    rhs = att[:, i, :] if kind == "egat" else w("filt2", 32)
                    for t in range(GT):
                        o = ps_le[g % 2][0:P, t * n:(t + 1) * n]
                        last = pe.matmul(o, hidT[0:k["hid"], g % 2, t * P:(t + 1) * P], rhs, start=True,
                                         stop=kind != "egat")
                        if kind == "egat":
                            last = pe.matmul(o, hid_negT[:, g % 2, t * P:(t + 1) * P], att_neg[:, i, :],
                                             start=False, stop=True)
                    last.then_inc(s_le, 1)

                def chunk(c, slot, turn):
                    pe.wait_ge(s_filled, dst_chunk_no(i, c) + 1)
                    if kind == "egat":
                        pe.wait_ge(s_ef, before(i, lambda k: k["feat"] == 97) * NCH + c + 1)
                    else:
                        pe.wait_ge(s_staged, chunk_no(i, c) + 1)
                    for g in range(NG + 2):
                        if g < NG:
                            transposes(c, slot, g)
                        if 1 <= g <= NG:
                            main(c, g - 1)
                        if g >= 2:
                            logit(c, g - 2)

                if k["feat"]:
                    if i == 0:
                        pe.wait_ge(s_att, 1)
                    chunks(pe, chunk)
                if i == 3:
                    histogram(1)

                if nh:
                    a = before(i, lambda k: k["heads"])
                    for r in range(2):
                        pe.wait_ge(s_diag, 2 * a + r + 1)
                        pe.matmul(bank[2][0:P, 0:nh * P], ones, diag[:, 0:nh * P], start=True, stop=True).then_inc(s_bcast, 1)
                    pe.wait_ge(s_cexp, a + 1)
                    for h in range(nh):
                        last = pe.matmul(bank[3][0:P, h * CW:(h + 1) * CW], weights_pq[:, h * P:(h + 1) * P],
                                         tail[:, h * CW:(h + 1) * CW], start=True, stop=True)
                else:
                    pe.wait_ge(s_scan, chunk_no(i, NCH))
                if k["plain"]:
                    p0 = nh * CW
                    src_rows = tail[:, p0:p0 + C] if nh else msg[:, 1, (TC - 1) * wd:(TC - 1) * wd + C]
                    last = pe.matmul(bank[3][0:P, p0:p0 + C], cont01[:, :], src_rows, start=True, stop=True)
                last.then_inc(s_carry_mm, 1)
                pe.wait_ge(s_carry, i + 1)
                own = owner[:, :].rearrange("q (p j) -> q j p", j=J)
                for n, (j, m) in enumerate(SEL):
                    wait(pe, s_selc, i * len(SEL) + n - 1)
                    for e in range(m):
                        last = pe.matmul(bank[n % 2][0:P, e * wd:(e + 1) * wd], own[:, j + e, :], carry[:, 0:wd],
                                         start=True, stop=True)
                    last.then_inc(s_sel, 1)
                if i in TPASS:
                    pr = PROD[kind]
                    b, hb = prod_no(i) * len(NT), hid_no(i) * len(NT)
                    pe.wait_ge(s_agg, i + 1)
                    out_w = pr["m"]
                    per = 512 // out_w
                    for n, (j, m) in enumerate(NT):
                        wait(pe, s_nTc, b + n - 1)
                        for e in range(m):
                            last = pe.transpose(bank[4 + n % 2][0:pr["k"], e * P:(e + 1) * P],
                                                aggregate[:, j + e, 0:pr["k"]], ident)
                        last.then_inc(s_nT, 1)
                        pe.wait_ge(s_nTc, b + n + 1)
                        lhs = featT
                        if pr["hid"]:
                            wait(pe, s_nhc, hb + n)
                            pe.matmul(bank[6][:, 0:m * P], w(pr["hid"], pr["k"]), featT[0:pr["k"], n % 2, 0:m * P],
                                      start=True, stop=True).then_inc(s_nh, 1)
                            pe.wait_ge(s_nhc, hb + n + 1)
                            lhs = hidT
                        rhs = {"egat": w("node")[:, i * C:(i + 1) * C] if kind == "egat" else None,
                               "sage": w("sage2"), "gat": w("wout")}[kind]
                        for e in range(m):
                            q = j + e
                            bk = {32: (2, 3), 64: (0, 1, 2, 3)}[out_w][q // per]
                            last = pe.matmul(bank[bk][0:P, (q % per) * out_w:(q % per + 1) * out_w],
                                             lhs[:, n % 2, e * P:(e + 1) * P], rhs, start=True, stop=True)
                    last.then_inc(s_no, 1)
                if i == 4:
                    pe.wait_ge(s_wlr, 1)
                    pe.matmul(ps_misc[0:P, 64:65], ones, tot[:, 0:1], start=True, stop=True).then_inc(s_off, 1)
                    pe.wait_ge(s_wlr, 2)
                    pe.matmul(ps_misc[0:P, 65:66], ones, tot[:, 1:2], start=True, stop=True).then_inc(s_off, 1)
                if i == 5:
                    b = 3 * len(NT)
                    pe.wait_ge(s_agg, 6)
                    for n, (j, m) in enumerate(NT):
                        wait(pe, s_noc, n - 1)
                        for e in range(m):
                            last = pe.transpose(bank[4 + n % 2][0:C, e * P:(e + 1) * P], X[:, j + e, :], ident)
                        last.then_inc(s_xT, 1)
                        pe.wait_ge(s_noc, n + 1)
                        for e in range(m):
                            last = pe.matmul(bank[2][0:P, (j + e) * 8:(j + e) * 8 + 8], featT[0:C, n % 2, e * P:(e + 1) * P],
                                             wlr[:, :], start=True, stop=True)
                    last.then_inc(s_no, 1)

        @block.vector
        def _(dve):
            chain = [0]

            def link(ins):
                chain[0] += 1
                ins.then_inc(s_v, 1)
                dve.wait_ge(s_v, chain[0])

            tt, ts, stt = dve.tensor_tensor, dve.tensor_scalar, dve.scalar_tensor_tensor
            IDENT = cst("ident", P, P)

            def bc(ap, n):
                s = [int(d) for d in ap.shape]
                return ap.unsqueeze(len(s)).broadcast_to(s + [n])

            dve.memset(msg[:, 0, 0:TC * CW], 0.0).then_inc(s_zero, 1)
            dve.memset(prev_i[0:1, :], -1)
            dve.memset(stage[:, :, :, 32:33], 1.0).then_inc(s_ones_col, 1)
            dve.wait_ge(s_dst_in, 32)
            dve.wait_ge(s_const, 32)
            dve.tensor_copy(first_i[:, :], dst_i[:, 0:1])
            link(dve.tensor_copy(dst_f, dst_i[:, :]))

            def histogram(turn, ids):
                link(ts(hi_f, ids, 1.0 / J, 0.5 / J - 0.5, ALU.mult, ALU.add))
                link(ts(hi_f, hi_f, MAGIC, MAGIC, ALU.add, ALU.subtract))
                link(stt(lo_f, hi_f, -float(J), ids, ALU.mult, ALU.add))

                def build(b, slot):
                    wait(dve, s_hist, turn * NHB + b - 1)
                    hi, lo = hi_f[:, bass.ds(b * HB, HB)], lo_f[:, bass.ds(b * HB, HB)]
                    io = cst("iota")
                    tt(hot(slot)[0], bc(hi, P), io[:, 0:P].unsqueeze(1).broadcast_to([P, HB, P]), ALU.is_equal)
                    tt(hot(slot)[1], bc(lo, J), io[:, 0:J].unsqueeze(1).broadcast_to([P, HB, J]), ALU.is_equal)\
                        .then_inc(s_hot, 1)

                build(0, 0)
                build(1, 1)
                with dve.Fori(1, NHB // 2) as kk:
                    for slot in range(2):
                        build(2 * kk + slot, slot)
                dve.wait_ge(s_hist, (turn + 1) * NHB)

            histogram(0, dst_f)
            link(dve.tensor_copy(deg, ps_misc[0:P, 0:J]))
            START, ENDP, HAS, PEND, CROSS, INCL, OWN, CNEG, RDEG, DEG1 = range(10)
            GATE, RS_DST, HN, RS_SRC = START, ENDP, PEND, INCL

            def ndc(r):
                return nd[:, r, :]

            link(dve.tensor_tensor_scan(ndc(INCL), cst("ones", P, J), deg, 0.0, ALU.mult, ALU.add))
            dve.tensor_copy(tot[:, 0:1], nd[:, INCL, J - 1:J]).then_inc(s_tot, 1)
            link(ts(ndc(HAS), deg, 1.0, None, ALU.min))
            link(ts(ndc(DEG1), deg, 1.0, None, ALU.max))
            link(dve.reciprocal(ndc(RDEG), ndc(DEG1)))
            link(tt(ndc(START), ndc(INCL), deg, ALU.subtract))
            dve.wait_ge(s_off, 1)
            link(ts(ndc(START), ndc(START), ps_misc[0:P, 64:65], None, ALU.add))
            link(stt(ndc(ENDP), ndc(START), -1.0, deg, ALU.add, ALU.add))
            link(ts(ndc(PEND), ndc(ENDP), 1.0 / T, 0.5 / T - 0.5, ALU.mult, ALU.add))
            link(ts(ndc(PEND), ndc(PEND), MAGIC, MAGIC, ALU.add, ALU.subtract))
            link(ts(ndc(CROSS), ndc(PEND), float(T), None, ALU.mult))
            link(tt(ndc(CROSS), ndc(START), ndc(CROSS), ALU.is_lt))
            link(tt(ndc(CROSS), ndc(CROSS), ndc(HAS), ALU.mult))
            link(stt(ndc(OWN), ndc(PEND), 1.0, ndc(CROSS), ALU.add, ALU.mult))
            link(ts(ndc(OWN), ndc(OWN), -1.0, None, ALU.add))
            link(ts(ndc(CNEG), ndc(CROSS), -1.0, BIG, ALU.add, ALU.mult))
            link(ts(ndc(ENDP), ndc(ENDP), 0.0, None, ALU.max))
            link(dve.tensor_copy(end_i[:, :], ndc(ENDP)))
            link(ts(ndc(INCL), ndc(HAS), -1.0, -1.0e6, ALU.add, ALU.mult))
            link(tt(ndc(INCL), ndc(INCL), ndc(START), ALU.add))
            link(dve.tensor_copy(start_i[:, :], ndc(INCL)))
            link(ts(be2s[:, :], w("be2", P), 10.0, None, ALU.mult))
            dve.wait_ge(s_x_in, 16)
            dve.memset(nf[:, :, C:CW], 0.0)
            dve.tensor_copy(nf[:, :, 0:C], X[:, :, :]).then_inc(s_rows, 1)
            dve.tensor_copy(same_neg[:, 0:1], prev_i[:, :]).then_inc(s_place, 1)
            dve.wait_ge(s_place, 1)
            tt(same[:, 0:1], dst_f[:, 0:1], same_neg[:, 0:1], ALU.is_equal)
            link(tt(same[:, 1:T], dst_f[:, 1:T], dst_f[:, 0:T - 1], ALU.is_equal))
            link(ts(same_neg[:, :], same[:, :], -1.0, BIG, ALU.add, ALU.mult))
            ts(diag[:, 0:P], IDENT, dst_f[:, T - 1:T], None, ALU.mult)
            ts(diag[:, P:2 * P], IDENT, dst_f[:, 0:1], None, ALU.mult).then_inc(s_rowsd, 1)
            for l in range(3):
                dve.tensor_copy(att[:, l, 0:H], w("att")[:, l * H:(l + 1) * H])
                last = dve.tensor_copy(att[:, l, H:36], cst("mean", 128))
            link(last)
            ts(att_neg[:, :, :], att[:, :, :], -NEG_SLOPE, None, ALU.mult).then_inc(s_att, 1)
            dve.wait_ge(s_bcast, 1)
            link(ts(cont01[:, :], bank[2][0:P, P:2 * P], dst_f[:, T - 1:T], None, ALU.is_equal))
            link(tt(cont01[:, :], cont01[:, :], cst("tri", P, P), ALU.mult))
            ts(cont_neg[:, :], cont01[:, :], -1.0, 1.0e36, ALU.add, ALU.mult)
            link(ts(contT_neg[:, :], bank[2][0:P, 0:P], dst_f[:, 0:1], None, ALU.is_equal))
            link(tt(contT_neg[:, :], contT_neg[:, :], cst("triT", P, P), ALU.mult))
            link(ts(contT_neg[:, :], contT_neg[:, :], -1.0, BIG, ALU.add, ALU.mult))
            dve.sem_inc(s_setup, 1)
            dve.wait_ge(s_owner_r, 16)
            link(ts(owner[:, :], owner[:, :], cst("col", P), None, ALU.is_equal))

            for i in range(NP):
                kind = PASSES[i]
                k = KIND[kind]
                nh, wd, dw = k["heads"], width(i), k["dst_w"]
                plain = k["plain"]

                def msg3(slot):
                    return msg[:, slot, 0:TC * wd].rearrange("p (t c) -> p t c", c=wd)

                def fill(c, slot, turn):
                    dve.wait_ge(s_dstrow[slot], 16 * (before(i, lambda k: k["dst_w"]) * (NCH // 2) + turn + 1))
                    wait(dve, s_free, chunk_no(i, c) - 1)
                    first = isinstance(c, int) and c == 0
                    if first:
                        dve.wait_ge(s_first, 16 * (before(i, lambda k: k["dst_w"]) + 1))
                    if kind == "filter":
                        dve.wait_ge(s_staged, chunk_no(i, c) + 1)
                    for ch in range(dw):
                        at = k["dst_at"] + ch
                        init = dst_first[:, ch:ch + 1] if first else dst_last[:, ch:ch + 1]
                        last = dve.tensor_tensor_scan(stage[:, slot, :, at], same[:, cols(c)], dst_in[:, slot, :, ch],
                                                      init, ALU.mult, ALU.add)
                    last.then_inc(s_fscan, 1)
                    dve.wait_ge(s_fscan, dst_chunk_no(i, c) + 1)
                    last = dve.tensor_copy(dst_last[:, 0:dw], stage[:, slot, TC - 1, k["dst_at"]:k["dst_at"] + dw])
                    if kind == "filter":
                        last.then_inc(s_fsub, 1)
                        dve.wait_ge(s_fsub, 2 * c + 1)
                        tt(stage[:, slot, :, 0:C], stage[:, slot, :, 0:C], stage[:, slot, :, 34:34 + C], ALU.subtract)\
                            .then_inc(s_fsub, 1)
                        dve.wait_ge(s_fsub, 2 * c + 2)
                        tt(stage[:, slot, :, 68:68 + C], stage[:, slot, :, 34:34 + C], bc(stage[:, slot, :, 67], C), ALU.mult)
                        last = stt(stage[:, slot, :, 0:C], stage[:, slot, :, 0:C], -1.0, stage[:, slot, :, 0:C], ALU.mult, ALU.max)
                    last.then_inc(s_filled, 1)

                def head_view(buf):
                    return buf.rearrange("p (t h) -> p t h", h=nh)

                def maxima(c, slot, turn):
                    first = isinstance(c, int) and c == 0
                    sc = soft_chunk_no(i, c)
                    lg = head_view(logits[:, slot, 0:TC * nh])
                    if first:
                        dve.memset(run_max[:, 0, 0:nh], -BIG).then_inc(s_mcar, 1)
                    else:
                        dve.tensor_copy(run_max[:, 0, 0:nh], run_max[:, TC, 0:nh]).then_inc(s_mcar, 1)
                    if kind == "gat":
                        dve.wait_ge(s_staged, chunk_no(i, c) + 1)
                        dve.wait_ge(s_filled, dst_chunk_no(i, c) + 1)
                        tt(head_view(w_arg[:, 0:TC * nh]), stage[:, slot, :, 33:37], stage[:, slot, :, 40:44], ALU.add)\
                            .then_inc(s_lg, 1)
                        dve.wait_ge(s_lg, 2 * c + 1)
                        stt(lg, head_view(w_arg[:, 0:TC * nh]), NEG_SLOPE, head_view(w_arg[:, 0:TC * nh]), ALU.mult, ALU.max)\
                            .then_inc(s_lg, 1)
                        dve.wait_ge(s_lg, 2 * c + 2)
                    else:
                        dve.wait_ge(s_lec, group_no(i, c, NG))
                    dve.wait_ge(s_mcar, sc + 1)
                    for h in range(nh):
                        last = dve.tensor_tensor_scan(run_max[:, 1:TC + 1, h], same_neg[:, cols(c)], lg[:, :, h],
                                                      run_max[:, 0, h:h + 1], ALU.add, ALU.max)
                    last.then_inc(s_max, 1)
                    dve.wait_ge(s_max, sc + 1)
                    wait(dve, s_exp, sc)
                    tt(head_view(w_arg[:, 0:TC * nh]), lg, run_max[:, 1:TC + 1, 0:nh], ALU.subtract)
                    tt(head_view(d_arg[:, 0:TC * nh]), run_max[:, 0:TC, 0:nh], run_max[:, 1:TC + 1, 0:nh], ALU.subtract)\
                        .then_inc(s_max2, 1)
                    dve.wait_ge(s_max2, sc + 1)
                    tt(head_view(d_arg[:, 0:TC * nh]), head_view(d_arg[:, 0:TC * nh]), bc(same_neg[:, cols(c)], nh), ALU.add)\
                        .then_inc(s_arg, 1)

                def weigh(c, slot, turn):
                    if not (isinstance(c, int) and i == 0 and c < 2):
                        dve.wait_ge(s_store[slot], 32 * (i * (NCH // 2) + turn))
                    m3 = msg3(slot)
                    xa = k.get("x_at", 0)
                    dve.wait_ge(s_exp, soft_chunk_no(i, c) + 1)
                    dve.tensor_copy(m3[:, :, wd - nh:wd], run_max[:, 1:TC + 1, 0:nh])
                    if nh > 1:
                        o = m3[:, :, 0:nh * CW].rearrange("p t (h c) -> p t h c", c=CW)
                        wgt = bc(head_view(ps_w[0:P, 0:TC * nh]), CW)
                        row = stage[:, slot, :, xa:xa + CW].unsqueeze(2).broadcast_to([P, TC, nh, CW])
                    else:
                        o = m3[:, :, 0:CW]
                        wgt = bc(ps_w[0:P, 0:TC], CW)
                        row = stage[:, slot, :, xa:xa + CW]
                    tt(o, wgt, row, ALU.mult).then_inc(s_mult, 1)

                def sums(c, slot, turn):
                    first = isinstance(c, int) and c == 0
                    m3, p3 = msg3(slot), msg3(1 - slot)
                    if nh:
                        dve.wait_ge(s_mult, soft_chunk_no(i, c) + 1)
                    else:
                        dve.wait_ge(s_staged, chunk_no(i, c) + 1)
                        if not (isinstance(c, int) and i == 0 and c < 2):
                            dve.wait_ge(s_store[slot], 32 * (i * (NCH // 2) + turn))
                    dv = head_view(decay[:, 0:TC * nh]) if nh else None
                    for h in range(nh):
                        for ch in range(CW):
                            q = h * CW + ch
                            last = dve.tensor_tensor_scan(m3[:, :, q], dv[:, :, h], m3[:, :, q],
                                                          0.0 if first else p3[:, TC - 1, q:q + 1], ALU.mult, ALU.add)
                    for ch in range(plain):
                        q = nh * CW + ch
                        last = dve.tensor_tensor_scan(m3[:, :, q], same[:, cols(c)], stage[:, slot, :, k["plain_at"] + ch],
                                                      0.0 if first else p3[:, TC - 1, q:q + 1], ALU.mult, ALU.add)
                    last.then_inc(s_scan, 1)
                    dve.wait_ge(s_scan, chunk_no(i, c) + 1)
                    dve.sem_inc(s_free, 1)

                if kind == "egat" and i:
                    link(dve.memset(stage[:, :, :, 32:33], 1.0))
                if nh:
                    def step(c, slot, turn):
                        fill(c, slot, turn)
                        if not (isinstance(c, int) and c == 0):
                            sums(c - 1, 1 - slot, turn - 1 + slot)
                        maxima(c, slot, turn)
                        weigh(c, slot, turn)
                    chunks(dve, step)
                    sums(NCH - 1, 1, NCH // 2 - 1)
                else:
                    if i == 3:
                        link(dve.tensor_copy(id_f, src_i[:, 0:T]))
                        histogram(1, id_f)
                        link(dve.tensor_copy(sdeg[:, :], ps_misc[0:P, 0:J]))
                    chunks(dve, sums)

                a = before(i, lambda k: k["heads"])
                if nh:
                    m0 = wd - nh
                    link(dve.tensor_copy(tail[:, 0:wd], msg[:, 1, (TC - 1) * wd:TC * wd]))
                    for h in range(nh):
                        last = ts(diag[:, h * P:(h + 1) * P], IDENT, tail[:, m0 + h:m0 + h + 1], None, ALU.mult)
                    last.then_inc(s_diag, 1)
                    dve.wait_ge(s_bcast, 1 + 2 * a + 1)
                    v3 = seen[:, 0:nh * P].rearrange("p (h q) -> p h q", q=P)
                    b3 = bank[2][0:P, 0:nh * P].rearrange("p (h q) -> p h q", q=P)
                    link(tt(v3, b3, contT_neg[:, :].unsqueeze(1).broadcast_to([P, nh, P]), ALU.add))
                    link(dve.tensor_reduce(carry_max[:, 0:nh], v3, AX, ALU.max))
                    for h in range(nh):
                        last = ts(diag[:, h * P:(h + 1) * P], IDENT, carry_max[:, h:h + 1], None, ALU.mult)
                    last.then_inc(s_diag, 1)
                    dve.wait_ge(s_bcast, 1 + 2 * a + 2)
                    tt(v3, cont_neg[:, :].unsqueeze(1).broadcast_to([P, nh, P]), b3, ALU.subtract).then_inc(s_carg, 1)
                dve.wait_ge(s_carry_mm, i + 1)
                if nh:
                    dve.tensor_copy(carry[:, m0:wd], carry_max[:, 0:nh])
                dve.tensor_copy(carry[:, 0:nh * CW + plain], bank[3][0:P, 0:nh * CW + plain]).then_inc(s_carry, 1)
                dve.wait_ge(s_ends, 16 * J * (i + 1))
                dve.wait_ge(s_selc, (i + 1) * len(SEL))
                en, cv = ends_view(wd), carried_view(wd)

                def hv(r):
                    return hw[:, r, 0:J * nh].rearrange("p (j h) -> p j h", h=nh)

                def bj(ap, n):
                    return bc(ap, n)

                if nh:
                    link(tt(cv[:, :, m0:wd], cv[:, :, m0:wd], bj(ndc(CNEG), nh), ALU.add))
                    link(tt(hv(4), en[:, :, m0:wd], cv[:, :, m0:wd], ALU.max))
                    tt(hv(0), en[:, :, m0:wd], hv(4), ALU.subtract)
                    tt(hv(1), cv[:, :, m0:wd], hv(4), ALU.subtract).then_inc(s_narg, 1)
                    dve.wait_ge(s_nexp, a + 1)
                    den_e = en[:, :, C:nh * CW:CW]
                    den_c = cv[:, :, C:nh * CW:CW]
                    tt(hv(0), hv(2), den_e, ALU.mult)
                    link(tt(hv(1), hv(3), den_c, ALU.mult))
                    link(tt(hv(4), hv(0), hv(1), ALU.add))
                    if kind == "filter":
                        link(ts(hv(0), hv(4), 1e-16, None, ALU.add))
                        link(dve.reciprocal(hv(0), hv(0)))
                        link(tt(hv(0), hv(0), bj(ndc(HAS), nh), ALU.mult))
                    else:
                        if kind == "gat":
                            link(ts(hv(4), hv(4), 1e-9, None, ALU.max))
                        link(dve.reciprocal(hv(0), hv(4)))
                        link(tt(hv(0), hv(0), bj(ndc(HAS), nh), ALU.mult))
                    tt(hv(2), hv(2), hv(0), ALU.mult)
                    link(tt(hv(3), hv(3), hv(0), ALU.mult))

                    def chans(v):
                        return v[:, :, 0:nh * CW].rearrange("p j (h c) -> p j h c", c=CW)[:, :, :, 0:C] if nh > 1 else v[:, :, 0:C]

                    ag = aggregate[:, :, 0:nh * C].rearrange("p j (h c) -> p j h c", c=C) if nh > 1 else aggregate[:, :, 0:C]
                    we = bc(hv(2), C) if nh > 1 else bc(hw[:, 2, 0:J], C)
                    wc = bc(hv(3), C) if nh > 1 else bc(hw[:, 3, 0:J], C)
                    link(tt(chans(cv), chans(cv), wc, ALU.mult))
                    link(tt(ag, chans(en), we, ALU.mult))
                    ins = tt(ag, ag, chans(cv), ALU.add)
                    if kind != "filter":
                        ins.then_inc(s_agg, 1)
                    else:
                        link(ins)

                def product_out(cols_out):
                    per = 512 // cols_out
                    for n in range((J + per - 1) // per):
                        j = n * per
                        m = min(per, J - j)
                        bk = bank[{32: (2, 3), 64: (0, 1, 2, 3)}[cols_out][n]]
                        yield j, m, bk[0:P, 0:m * cols_out].rearrange("p (j c) -> p j c", c=cols_out)

                def layer_norm(y, r):
                    link(dve.tensor_reduce(sm[:, 0, :], y, AX, ALU.add))
                    link(ts(sm[:, 0, :], sm[:, 0, :], 1.0 / C, None, ALU.mult))
                    link(tt(y, y, bj(sm[:, 0, :], C), ALU.subtract))
                    link(tt(rr[:, :, :], y, y, ALU.mult))
                    link(dve.tensor_reduce(sm[:, 1, :], rr[:, :, :], AX, ALU.add))
                    ts(sm[:, 2, :], sm[:, 1, :], 1.0 / C, LN_EPS, ALU.mult, ALU.add).then_inc(s_var, 1)
                    dve.wait_ge(s_std, r + 1)
                    link(dve.reciprocal(sm[:, 3, :], sm[:, 2, :]))
                    link(tt(X[:, :, :], y, bj(sm[:, 3, :], C), ALU.mult))

                if kind == "egat":
                    dve.wait_ge(s_no, prod_no(i) + 1)
                    for j, m, v in product_out(C):
                        last = ts(yt[:, j:j + m, :], v, 1.0 / H, None, ALU.mult)
                    link(last)
                    if i < 2:
                        dve.tensor_copy(nf[:, :, 0:C], yt[:, :, :]).then_inc(s_table, 1)
                    else:
                        link(tt(yt[:, :, :], yt[:, :, :], X[:, :, :], ALU.add))
                        layer_norm(yt[:, :, :], 0)
                        dve.sem_inc(s_table, 1)
                if i == 3:
                    tt(cv, cv, bj(ndc(CROSS), C), ALU.mult)
                    link(tt(en, en, bj(ndc(HAS), C), ALU.mult))
                    link(tt(en, en, cv, ALU.add))
                    tt(aggregate[:, :, 0:C], en, bj(ndc(RDEG), C), ALU.mult)
                    dve.memset(aggregate[:, :, 64:65], 1.0)
                    dve.tensor_copy(aggregate[:, :, C:2 * C], X[:, :, :]).then_inc(s_agg, 1)
                    dve.wait_ge(s_no, 4)
                    for j, m, v in product_out(2 * C):
                        dve.tensor_copy(rr[:, j:j + m, :], v[:, :, C:2 * C])
                        last = dve.tensor_copy(yt[:, j:j + m, :], v[:, :, 0:C])
                    last.then_inc(s_table, 1)
                if i == 4:
                    link(tt(en, en, bj(ndc(HAS), C), ALU.mult))
                    link(tt(en, en, cv, ALU.add))
                    link(tt(en, en, bj(ndc(RDEG), C), ALU.mult))
                    link(tt(en, en, rr[:, :, :], ALU.add))
                    link(tt(en, en, w("b2", P).unsqueeze(1).broadcast_to([P, J, C]), ALU.add))
                    link(tt(yt[:, :, :], en, X[:, :, :], ALU.add))
                    dve.sem_inc(s_agg, 1)
                    link(dve.tensor_reduce(tot[:, 0:1], ndc(DEG1), AX, ALU.add))
                    dve.sem_inc(s_wlr, 1)
                    dve.wait_ge(s_off, 2)
                    link(ts(tot[:, 0:1], ps_misc[0:P, 64:65], 1.0 / N, None, ALU.mult))
                    link(ts(ndc(HN), ndc(DEG1), tot[:, 0:1], None, ALU.subtract))
                    link(tt(sm[:, 5, :], ndc(HN), ndc(HN), ALU.mult))
                    dve.tensor_reduce(tot[:, 1:2], sm[:, 5, :], AX, ALU.add).then_inc(s_wlr, 1)
                    dve.wait_ge(s_off, 3)
                    ts(tot[:, 1:2], ps_misc[0:P, 65:66], 1.0 / (N - 1), None, ALU.mult)
                    dve.tensor_copy(sm[:, 6, :], ndc(DEG1))
                    ts(sm[:, 7, :], sdeg[:, :], 1.0, None, ALU.max).then_inc(s_sq, 1)
                    dve.wait_ge(s_sqd, 1)
                    link(ts(tot[:, 1:2], tot[:, 1:2], 1e-8, None, ALU.add))
                    link(dve.reciprocal(tot[:, 1:2], tot[:, 1:2]))
                    link(ts(ndc(HN), ndc(HN), tot[:, 1:2], None, ALU.mult))
                    dve.reciprocal(ndc(RS_DST), sm[:, 6, :])
                    link(dve.reciprocal(ndc(RS_SRC), sm[:, 7, :]))
                    gw = pair[:, 2000:2000 + J * 16].rearrange("p (j c) -> p j c", c=16)
                    w16 = lambda n: w(n, P).unsqueeze(1).broadcast_to([P, J, 16])
                    link(tt(gw, bc(ndc(HN), 16), w16("wn1"), ALU.mult))
                    link(tt(gw, gw, w16("bn1"), ALU.add))
                    link(ts(gw, gw, 0.0, None, ALU.max))
                    link(tt(gw, gw, w16("wn2"), ALU.mult))
                    link(dve.tensor_reduce(ndc(GATE), gw, AX, ALU.add))
                    ts(ndc(GATE), ndc(GATE), w("bn2", P), None, ALU.add).then_inc(s_gate, 1)
                    dve.wait_ge(s_gated, 1)
                    link(ts(ndc(GATE), ndc(GATE), 1.0, None, ALU.add))
                    link(dve.reciprocal(ndc(GATE), ndc(GATE)))
                    layer_norm(yt[:, :, :], 1)
                    tb = pair[:, 0:J * 35].rearrange("p (j c) -> p j c", c=35)
                    dve.tensor_copy(tb[:, :, 0:1], nd[:, HN, :].unsqueeze(2))
                    dve.tensor_copy(tb[:, :, 1:33], X[:, :, :])
                    dve.memset(tb[:, :, 33:34], 1.0)
                    dve.tensor_copy(tb[:, :, 34:35], nd[:, RS_SRC, :].unsqueeze(2))
                    dve.tensor_copy(nf[:, :, 0:C], X[:, :, :])
                    dve.tensor_copy(nf[:, :, C:CW], nd[:, HN, :].unsqueeze(2)).then_inc(s_table, 1)
                if kind == "filter":
                    low_e, low_c = en[:, :, CW:CW + C], cv[:, :, CW:CW + C]
                    link(tt(low_e, low_e, bj(ndc(HAS), C), ALU.mult))
                    link(tt(low_e, low_e, low_c, ALU.add))
                    link(tt(low_e, low_e, bj(ndc(RS_DST), C), ALU.mult))
                    link(tt(hw[:, 4, 0:J], hw[:, 4, 0:J], hw[:, 0, 0:J], ALU.mult))
                    link(tt(yt[:, :, :], X[:, :, :], bj(hw[:, 4, 0:J], C), ALU.mult))
                    link(tt(yt[:, :, :], yt[:, :, :], aggregate[:, :, 0:C], ALU.subtract))
                    link(tt(yt[:, :, :], yt[:, :, :], low_e, ALU.subtract))
                    link(tt(yt[:, :, :], yt[:, :, :], bj(ndc(GATE), C), ALU.mult))
                    link(tt(yt[:, :, :], yt[:, :, :], low_e, ALU.add))
                    link(tt(yt[:, :, :], yt[:, :, :], X[:, :, :], ALU.add))
                    layer_norm(yt[:, :, :], 2)
                    for s in range(2):
                        link(tt(lr_tmp, w("wfc_row", C), w("attn_lr", C)[:, s * 128:(s + 1) * 128], ALU.mult))
                        link(dve.tensor_reduce(wlr[:, s * H:(s + 1) * H], lr_tmp.rearrange("c (h d) -> c h d", d=C), AX, ALU.add))
                    dve.sem_inc(s_agg, 1)
                    for n, (j, m) in enumerate(NT):
                        dve.wait_ge(s_xT, n + 1)
                        dve.tensor_copy(featT[0:C, n % 2, 0:m * P], bank[4 + n % 2][0:C, 0:m * P]).then_inc(s_noc, 1)
                    dve.wait_ge(s_no, 5)
                    lr = bank[2][0:P, 0:J * 8].rearrange("p (j c) -> p j c", c=8)
                    tb = pair[:, 0:J * 37].rearrange("p (j c) -> p j c", c=37)
                    dve.tensor_copy(tb[:, :, 0:C], X[:, :, :])
                    dve.memset(tb[:, :, C:CW], 1.0)
                    dve.tensor_copy(tb[:, :, 33:37], lr[:, :, 0:H])
                    dve.tensor_copy(nf[:, :, 0:H], lr[:, :, H:2 * H]).then_inc(s_table, 1)
                if kind == "gat":
                    dve.wait_ge(s_no, 6)
                    for j, m, v in product_out(C):
                        last = tt(yt[:, j:j + m, :], v, w("bout", P).unsqueeze(1).broadcast_to([P, m, C]), ALU.add)
                    link(last)
                    ts(rr[:, :, :], yt[:, :, :], 0.0, None, ALU.min).then_inc(s_elu, 1)
                    link(ts(yt[:, :, :], yt[:, :, :], 0.0, None, ALU.max))
                    dve.wait_ge(s_elud, 1)
                    link(stt(rr[:, :, :], rr[:, :, :], -1.0, yt[:, :, :], ALU.add, ALU.add))
                    link(stt(yt[:, :, :], X[:, :, :], 2.0, rr[:, :, :], ALU.mult, ALU.add))
                    layer_norm(yt[:, :, :], 3)
                    dve.sem_inc(s_table, 1)


def pack_weights(np, a):
    wp = np.zeros((128, WCOLS), np.float32)

    def put(name, rows, block, col=0, row=0):
        wp[row:row + rows, W_OFF[name][0] + col:W_OFF[name][0] + col + block.shape[1]] = block

    for l in range(3):
        put("edge", C, a["L0_gnn_W_ni"][l], l * 128, 0)
        put("edge", 1, a["L0_gnn_bias"][l][None], l * 128, 32)
        put("edge", C, a["L0_gnn_W_fij"][l], l * 128, 33)
        put("edge", C, a["L0_gnn_W_nj"][l], l * 128, 65)
        for h in range(H):
            put("att", C, a["L0_gnn_attn"][l, h][:, None], l * H + h, h * C)
            put("node", C, a["L0_gnn_W_node"][l][:, h * C:(h + 1) * C], l * C, h * C)
    put("sage1", C, a["L1_gnn_W1_l"].T)
    put("sage1", C, a["L1_gnn_W1_r"].T, 0, C)
    put("sage1", 1, a["L1_gnn_b1"][None], 0, 2 * C)
    put("sage2", 128, a["L1_gnn_W2_l"].T)
    put("sage2", 128, a["L1_gnn_W2_r"].T, C)
    put("filt1", C, a["L2_gnn_We1"][2:])
    put("filt1", 1, a["L2_gnn_We1"][1:2], 0, C)
    put("filt1", 1, a["L2_gnn_We1"][0:1], 0, C + 1)
    put("filt2", 32, a["L2_gnn_We2"])
    for h in range(H):
        put("wfc", C, a["L3_gnn_W_fc"][:, h * C:(h + 1) * C], h * C, h * C)
    put("wfc_row", C, a["L3_gnn_W_fc"])
    put("attn_lr", C, np.tile(a["L3_gnn_attn_l"].reshape(1, -1), (C, 1)))
    put("attn_lr", C, np.tile(a["L3_gnn_attn_r"].reshape(1, -1), (C, 1)), 128)
    put("wout", 128, a["L3_gnn_W_out"])
    put("bias_gat", 128, a["L3_gnn_bias_gat"][:, None])
    put("be1", 32, a["L2_gnn_be1"][:, None])
    for name, v in (("be2", a["L2_gnn_be2"]), ("b2", a["L1_gnn_b2"]), ("bout", a["L3_gnn_b_out"]),
                    ("wn1", a["L2_gnn_Wn1"]), ("bn1", a["L2_gnn_bn1"]), ("wn2", a["L2_gnn_Wn2"]),
                    ("bn2", a["L2_gnn_bn2"])):
        put(name, 128, np.tile(v.reshape(1, -1), (128, 1)))
    return wp


def pack_constants(np):
    c = np.zeros((128, CCOLS), np.float32)
    c[:, 0:128] = np.eye(128)
    c[:, 128:256] = 1.0
    c[:, 256:384] = np.triu(np.ones((128, 128)), 1)
    c[:, 384:512] = np.tril(np.ones((128, 128)), -1)
    c[:, 512:544] = np.tile(np.eye(C), (H, 1)) / H
    c[:, 544:672] = np.arange(128)[None]
    c[:, 672] = np.arange(128)
    return c


def build(nc):
    f32, i32 = mybir.dt.float32, mybir.dt.int32
    shapes = {"x": ((N, C), f32), "src": ((E,), i32), "dst": ((E,), i32), "edge_attr": ((E, C), f32),
              "wpack": ((128, WCOLS), f32), "cpack": ((128, CCOLS), f32)}
    ins = [nc.dram_tensor(n, s, d, kind="ExternalInput").ap() for n, (s, d) in shapes.items()]
    out = nc.dram_tensor("out", (N, C), f32, kind="ExternalOutput").ap()
    graph_kernel(nc, *ins, out)


def kernel(**inputs):
    import numpy as np
    import concourse.bacc as bacc
    from concourse.bass_utils import run_bass_kernel_spmd

    a = {n: np.ascontiguousarray(v) for n, v in inputs.items()}
    nc = bacc.Bacc("TRN2", target_bir_lowering=False, num_devices=1)
    build(nc)
    arrays = {"x": a["x"], "src": a["src"], "dst": a["dst"], "edge_attr": a["edge_attr_32"],
              "wpack": pack_weights(np, a), "cpack": pack_constants(np)}
    r = run_bass_kernel_spmd(nc, [arrays], core_ids=[0])
    return r.results[0]["out"]
```

```python
import concourse.bass as bass
from concourse import mybir
from contextlib import ExitStack

N, E, C, H = 3125, 50000, 32, 4
P = 125
T = E // P
J = N // P
TC = 40
NCH = T // TC
GT = 4
NG = TC // GT
HB = 10
NHB = T // HB
CW = C + 1
ROW = H * CW + H
SW = 100
GW = 37
BIG = 1.0e30
MAGIC = 12582912.0
LN_EPS = 1e-5
NEG_SLOPE = 0.2
EDGE_SPLIT = 112

W_OFF = {}


def _w_layout():
    at = 0
    for name, n in (("edge", 3 * 128), ("att", 3 * H), ("node", 3 * C), ("sage1", 128), ("sage2", 2 * C),
                    ("filt1", 64), ("filt2", 2), ("wfc", 128), ("wfc_row", 128), ("attn_lr", 2 * 128),
                    ("wout", C), ("bias_gat", 1), ("be1", 1), ("be2", 1), ("b2", C), ("bout", C),
                    ("wn1", 16), ("bn1", 16), ("wn2", 16), ("bn2", 1)):
        W_OFF[name] = (at, n)
        at += n
    return at


WCOLS = _w_layout()
C_OFF = {"ident": (0, 128), "ones": (128, 128), "tri": (256, 128), "triT": (384, 128), "mean": (512, 32),
         "col": (544, 1)}
CCOLS = 545

PASSES = ("egat", "egat", "egat", "sage", "sage", "filter", "gat")
KIND = {
    "egat": dict(src_w=C, dst_w=C, dst_at=65, heads=H, plain=0, feat=97, hid=128, le=36, pair=1),
    "sage": dict(src_w=C, dst_w=0, dst_at=0, heads=0, plain=C, feat=0),
    "filter": dict(src_w=35, dst_w=33, dst_at=0, heads=1, plain=C,
                   feat=68, hid=64, le=1, pair=2),
    "gat": dict(src_w=37, dst_w=H, dst_at=40, heads=H, plain=0, feat=0),
}
NP = len(PASSES)


def before(i, test):
    return sum(1 for k in PASSES[:i] if test(KIND[k]))


def graph_kernel(nc, x, src, dst, edge_attr, wpack, cpack, out):
    f32, i32, bf16 = mybir.dt.float32, mybir.dt.int32, mybir.dt.bfloat16
    ALU, ACT, AX = mybir.AluOpType, mybir.ActivationFunctionType, mybir.AxisListType.X

    def dram(name, shape):
        return nc.dram_tensor(name, shape, f32).ap()

    run_start_rows = dram("run_start_rows", (E, CW))
    dst_table = dram("dst_table", (N, CW))
    message_rows = {k: dram(f"message_rows_{k}", (E, ROW if k in ("egat", "gat") else C if k == "sage" else 66))
                    for k in KIND}
    src_tables = [x] + [dram(f"src_table_{i}", (N, KIND[PASSES[i]]["src_w"])) for i in range(1, NP)]
    carry_owner_d = dram("carry_owner_d", (N,))

    ctx = ExitStack()
    with ctx:
        def sb(name, shape, dt=f32):
            return ctx.enter_context(nc.sbuf_tensor(name, shape, dt))

        def pb(name):
            return ctx.enter_context(nc.psum_tensor(name, [128, 512], f32))

        def sem(name):
            return ctx.enter_context(nc.semaphore(name))

        W = sb("W", [128, WCOLS])
        CS = sb("CS", [128, CCOLS])

        def w(name, rows=128):
            a, n = W_OFF[name]
            return W[0:rows, a:a + n]

        def cst(name, rows=P, cols=None):
            a, n = C_OFF[name]
            return CS[0:rows, a:a + (cols or n)]

        src_i = sb("src_i", [P, T + 2 * TC], i32)
        src_ring = sb("src_ring", [P, 2, TC], i32)
        first_i = sb("first_i", [P, 1], i32)
        prev_i = sb("prev_i", [P, 1], i32)
        same = sb("same", [P, T])
        same_neg = sb("same_neg", [P, T])
        edge_feat = sb("edge_feat", [P, T, C])
        gathered = sb("gathered", [P, 2, TC * GW])
        stage = sb("stage", [P, 2, TC, SW])
        dst_in = sb("dst_in", [P, 2, TC, CW])
        dst_first = sb("dst_first", [P, CW])
        featT = sb("featT", [128, 2, GT * P])
        hidT = sb("hidT", [128, 2, GT * P])
        hid_negT = sb("hid_negT", [128, 2, GT * P])
        logits = sb("logits", [P, 2, TC * H])
        run_max = sb("run_max", [P, TC + 1, H])
        w_arg = sb("w_arg", [P, TC * H])
        d_arg = sb("d_arg", [P, TC * H])
        decay = sb("decay", [P, TC * H])
        msg = sb("msg", [P, 2, TC * ROW])
        att = sb("att", [128, 3, 36])
        att_neg = sb("att_neg", [128, 3, 36])
        wlr = sb("wlr", [C, 2 * H])
        X = sb("X", [P, J, C])
        nf = sb("nf", [P, J, CW])
        sdeg = sb("sdeg", [P, J])
        nd = sb("nd", [P, 10, J])
        end_i = sb("end_i", [P, J], i32)
        start_i = sb("start_i", [P, J], i32)
        owner = sb("owner", [P, N])
        tail = sb("tail", [P, ROW])
        carry = sb("carry", [P, ROW])
        carry_max = sb("carry_max", [P, H])
        cont01 = sb("cont01", [P, P])
        cont_neg = sb("cont_neg", [P, P])
        contT_neg = sb("contT_neg", [P, P])
        sm = sb("sm", [P, 8, J])
        deg = sm[:, 4, :]
        hw = sb("hw", [P, 5, J * H])
        yt = sb("yt", [P, J, C])
        rr = sb("rr", [P, J, C])
        lr_tmp = rr[0:C, :, :].rearrange("p j c -> p (j c)")[:, 0:128]
        iota_b = sb("iota_b", [P, 128], bf16)
        dst_last = sb("dst_last", [P, CW])
        be2s = sb("be2s", [P, 1])
        tot = sb("tot", [P, 2])

        def filter_stage(slot):
            flat = stage[:, slot, :, :].rearrange("p t c -> p (t c)")
            return (flat[:, 0:TC * 34].rearrange("p (t c) -> p t c", c=34),
                    flat[:, TC * 34:TC * 68].rearrange("p (t c) -> p t c", c=34))

        dst_in_flat = dst_in[:, :, :, :].rearrange("p a t c -> p (a t c)")
        id_f, hi_f = (dst_in_flat[:, n * T:(n + 1) * T] for n in range(2))
        dst_i = dst_in_flat[:, 3 * T:4 * T].bitcast(i32)
        dst_f = dst_in_flat[:, 4 * T:5 * T]
        iota_f = dst_in_flat[:, 6 * T:6 * T + 128]
        hi_lo = dst_in_flat[:, 5 * T:6 * T].bitcast(bf16)

        def hot(slot):
            b = (featT, hidT)[slot][0:P, :, :].rearrange("p a b -> p (a b)").bitcast(bf16)
            return (b[:, 0:HB * P].rearrange("p (t n) -> p t n", n=P),
                    b[:, HB * P:HB * (P + J)].rearrange("p (t n) -> p t n", n=J))

        def ends_view(width):
            return msg[:, 0, 0:J * width].rearrange("p (j c) -> p j c", c=width)

        aggregate = msg[:, 1, 0:J * 128].rearrange("p (j c) -> p j c", c=128)
        stage_flat = stage[:, 0, :, :].rearrange("p t c -> p (t c)")

        def carried_view(width):
            return stage_flat[:, 0:J * width].rearrange("p (j c) -> p j c", c=width)

        pair = stage[:, 1, :, :].rearrange("p t c -> p (t c)")
        diag = featT[0:P, :, :].rearrange("p a b -> p (a b)")[:, 0:H * P]
        seen = hidT[0:P, :, :].rearrange("p a b -> p (a b)")[:, 0:H * P]
        weights_pq = featT[0:P, :, :].rearrange("p a b -> p (a b)")[:, H * P:2 * H * P]

        bank = [pb(f"bank{i}") for i in range(8)]
        ps_featT, ps_hid, ps_le, ps_w, ps_misc = bank[0:2], bank[2:4], bank[4:6], bank[6], bank[7]

        s_const = sem("s_const")
        s_apart = sem("s_apart")
        s_idx_in = sem("s_idx_in")
        s_dst_in = sem("s_dst_in")
        s_ef_in = sem("s_ef_in")
        s_x_in = sem("s_x_in")
        s_zero = sem("s_zero")
        s_zeroed = sem("s_zeroed")
        s_ones_col = sem("s_ones_col")
        s_v = sem("s_v")
        s_a = sem("s_a")
        s_att = sem("s_att")
        s_hot = sem("s_hot")
        s_hist = sem("s_hist")
        s_tot = sem("s_tot")
        s_off = sem("s_off")
        s_rows = sem("s_rows")
        s_rowsd = sem("s_rowsd")
        s_wlr = sem("s_wlr")
        s_setup = sem("s_setup")
        s_place = sem("s_place")
        s_owner_w = sem("s_owner_w")
        s_owner_r = sem("s_owner_r")
        s_ring = sem("s_ring")
        s_gather = [sem("s_gather0"), sem("s_gather1")]
        s_staged = sem("s_staged")
        s_ef = sem("s_ef")
        s_free = sem("s_free")
        s_dstrow = [sem("s_dstrow0"), sem("s_dstrow1")]
        s_filled = sem("s_filled")
        s_fscan = sem("s_fscan")
        s_fsub = sem("s_fsub")
        s_T = sem("s_T")
        s_featT = sem("s_featT")
        s_main = sem("s_main")
        s_hid = sem("s_hid")
        s_le = sem("s_le")
        s_lec = sem("s_lec")
        s_mcar = sem("s_mcar")
        s_lg = sem("s_lg")
        s_max = sem("s_max")
        s_max2 = sem("s_max2")
        s_arg = sem("s_arg")
        s_exp = sem("s_exp")
        s_mult = sem("s_mult")
        s_scan = sem("s_scan")
        s_store = [sem("s_store0"), sem("s_store1")]
        s_scatter = sem("s_scatter")
        s_first = sem("s_first")
        s_diag = sem("s_diag")
        s_bcast = sem("s_bcast")
        s_carg = sem("s_carg")
        s_cexp = sem("s_cexp")
        s_carry_mm = sem("s_carry_mm")
        s_carry = sem("s_carry")
        s_sel = sem("s_sel")
        s_selc = sem("s_selc")
        s_ends = [sem(f"s_ends{b}") for b in range(3)]
        s_narg = sem("s_narg")
        s_nexp = sem("s_nexp")
        s_agg = sem("s_agg")
        s_nT = sem("s_nT")
        s_nTc = sem("s_nTc")
        s_nh = sem("s_nh")
        s_nhc = sem("s_nhc")
        s_lr = sem("s_lr")
        s_xT = sem("s_xT")
        s_xTc = sem("s_xTc")
        s_no = sem("s_no")
        s_noc = sem("s_noc")
        s_var = sem("s_var")
        s_std = sem("s_std")
        s_sq = sem("s_sq")
        s_sqd = sem("s_sqd")
        s_gate = sem("s_gate")
        s_gated = sem("s_gated")
        s_elu = sem("s_elu")
        s_elud = sem("s_elud")
        s_table = sem("s_table")
        s_table_w = sem("s_table_w")
        s_out = sem("s_out")

        block = ctx.enter_context(nc.Block())

        def wait(eng, s, value):
            if isinstance(value, int) and value <= 0:
                return
            eng.wait_ge(s, value)

        def apart(eng):
            eng.sem_inc(s_apart, 1)

        def chunk_no(i, c):
            return i * NCH + c

        def dst_chunk_no(i, c):
            return before(i, lambda k: k["dst_w"]) * NCH + c

        def soft_chunk_no(i, c):
            return before(i, lambda k: k["heads"]) * NCH + c

        def group_no(i, c, g):
            return (before(i, lambda k: k["feat"]) * NCH + c) * NG + g

        def cols(c):
            return bass.ds(c * TC, TC)

        def slot_turn(i, c, slot):
            return i * (NCH // 2) + ((c - slot) // 2 if isinstance(c, int) else c)

        def chunks(eng, body):
            for slot in range(2):
                body(slot, slot, 0)
            with eng.Fori(1, NCH // 2) as k:
                for slot in range(2):
                    body(2 * k + slot, slot, k)

        NSEL = 3
        SEL = [(j, min(NSEL, J - j)) for j in range(0, J, NSEL)]
        BLOCKS = [(0, 8), (8, 8), (16, J - 16)]
        NBL = len(BLOCKS)
        GROUPS = [[(j, min(4, j0 + m0 - j)) for j in range(j0, j0 + m0, 4)] for j0, m0 in BLOCKS]
        NGR = sum(len(g) for g in GROUPS)

        def groups(b):
            at = sum(len(g) for g in GROUPS[:b])
            return [(at + n, j, m) for n, (j, m) in enumerate(GROUPS[b])]

        TPASS = [i for i in range(NP) if PASSES[i] == "egat"] + [3, 6]
        PROD = {"egat": dict(k=128, hid=None, m=C), "sage": dict(k=65, hid="sage1", m=2 * C),
                "gat": dict(k=128, hid="wfc", m=C)}

        def product_at(j, m, width):
            b = 0 if j < 8 else 1 if j < 16 else 2
            at = j - BLOCKS[b][0]
            per = 512 // width
            if at + m <= per:
                return [(j, m, (2, 3, 7)[b], at * width)]
            return ([(j, per - at, (2, 3, 7)[b], at * width)] if at < per else []) + \
                   [(max(j, BLOCKS[b][0] + per), at + m - max(per, at), 0, 0)]

        def prod_no(i):
            return sum(1 for t in TPASS if t < i)

        def hid_no(i):
            return sum(1 for t in TPASS if t < i and PROD[PASSES[t]]["hid"])

        def width(i):
            return {"egat": ROW, "gat": ROW, "filter": 66, "sage": C}[PASSES[i]]

        @block.sync
        def _(sp):
            sp.dma_start(src_i[:, 0:T], src.rearrange("(p t) -> p t", t=T)).then_inc(s_idx_in, 16)
            sp.dma_start(src_i[:, T:T + 2 * TC], src.rearrange("(p t) -> p t", t=T)[:, 0:2 * TC]).then_inc(s_idx_in, 16)
            sp.dma_start(dst_i, dst.rearrange("(p t) -> p t", t=T)).then_inc(s_dst_in, 16)
            sp.dma_start(prev_i[1:P, :], dst.rearrange("(p t) -> p t", t=T)[0:P - 1, T - 1:T],
                         allow_slow_non_contiguous=True).then_inc(s_dst_in, 16)
            sp.dma_start(W[:, :], wpack).then_inc(s_const, 16)
            sp.dma_start(CS[:, :], cpack[:, 0:CCOLS]).then_inc(s_const, 16)
            sp.dma_start(iota_f, cpack[0:P, CCOLS:CCOLS + 128]).then_inc(s_dst_in, 16)
            sp.dma_start(X[:, :, :], x.rearrange("(p j) c -> p j c", j=J)).then_inc(s_x_in, 16)
            ea = edge_attr.rearrange("(p t) c -> p t c", t=T)
            sp.dma_start(edge_feat[0:EDGE_SPLIT, :, :], ea[0:EDGE_SPLIT]).then_inc(s_ef_in, 16)
            sp.dma_start(edge_feat[EDGE_SPLIT:P, :, :], ea[EDGE_SPLIT:P]).then_inc(s_ef_in, 16)
            sp.wait_ge(s_zero, 1)
            rs = run_start_rows.rearrange("(p t) c -> p t c", t=T)
            for c in range(NCH):
                sp.dma_start(rs[:, c * TC:(c + 1) * TC, :],
                             msg[:, 0, 0:TC * CW].rearrange("p (t c) -> p t c", c=CW)).then_inc(s_zeroed, 16)
            sp.wait_ge(s_place, 1)
            sp.dma_start(carry_owner_d.rearrange("(p j) -> p j", j=J), nd[:, 6, :]).then_inc(s_owner_w, 16)
            sp.wait_ge(s_owner_w, 16)
            sp.dma_start(owner[:, :], carry_owner_d.rearrange("(a n) -> a n", a=1).broadcast_to([P, N])).then_inc(s_owner_r, 16)

            for i in range(NP):
                k = KIND[PASSES[i]]
                wd = width(i)
                rows = message_rows[PASSES[i]].rearrange("(p t) c -> p t c", t=T)
                if i == 0:
                    sp.wait_ge(s_rows, 1)
                    sp.dma_start(dst_table.rearrange("(p j) c -> p j c", j=J), nf[:, :, :]).then_inc(s_table_w, 16)
                else:
                    tw = k["src_w"]
                    from_ = (yt[:, :, :] if PASSES[i] == "egat" or i == 4 else X[:, :, :] if i == 3 else
                             pair[:, 0:J * tw].rearrange("p (j c) -> p j c", c=tw))
                    for b, (j, m) in enumerate(BLOCKS):
                        sp.wait_ge(s_table, (i - 1) * NBL + b + 1)
                        sp.dma_start(src_tables[i].rearrange("(p j) c -> p j c", j=J)[:, j:j + m, :],
                                     from_[:, j:j + m, :]).then_inc(s_table_w, 16)
                        if k["dst_w"]:
                            sp.dma_start(dst_table.rearrange("(p j) c -> p j c", j=J)[:, j:j + m, :],
                                         nf[:, j:j + m, :]).then_inc(s_table_w, 16)
                if k["dst_w"]:
                    sp.wait_ge(s_scatter, 16 * J * (before(i, lambda k: k["dst_w"]) + 1))

                def load_dst(c, slot, turn):
                    wait(sp, s_filled, dst_chunk_no(i, c) - 1)
                    sp.dma_start(dst_in[:, slot, :, :], rs[:, cols(c), :]).then_inc(s_dstrow[slot], 16)

                def store(c, slot, turn):
                    sp.wait_ge(s_scan, chunk_no(i, c) + 1)
                    m = msg[:, slot, 0:TC * wd].rearrange("p (t c) -> p t c", c=wd)
                    sp.dma_start(rows[0:EDGE_SPLIT, cols(c), :], m[0:EDGE_SPLIT]).then_inc(s_store[slot], 16)
                    sp.dma_start(rows[EDGE_SPLIT:P, cols(c), :], m[EDGE_SPLIT:P]).then_inc(s_store[slot], 16)

                if k["dst_w"]:
                    if i == 0:
                        sp.wait_ge(s_setup, 1)
                    for c in range(4):
                        load_dst(c, c % 2, c // 2)
                    for c in range(2):
                        store(c, c, 0)
                        load_dst(c + 4, c, 2)
                    with sp.Fori(1, NCH // 2 - 2) as kk:
                        for slot in range(2):
                            store(2 * kk + slot, slot, kk)
                            load_dst(2 * kk + 4 + slot, slot, kk + 2)
                    for c in range(NCH - 4, NCH):
                        store(c, c % 2, c // 2)
                else:
                    chunks(sp, store)
            for b, (j, m) in enumerate(BLOCKS):
                sp.wait_ge(s_table, (NP - 1) * NBL + b + 1)
                sp.dma_start(out.rearrange("(p j) c -> p j c", j=J)[:, j:j + m, :], X[:, j:j + m, :]).then_inc(s_out, 16)
            sp.wait_ge(s_out, 16 * NBL)

        @block.gpsimd
        def _(pool):
            at = bass.IndirectOffsetOnAxis
            tables = 0
            for i in range(NP):
                k = KIND[PASSES[i]]
                wd, tw = width(i), k["src_w"]
                def gather(c, slot, turn):
                    pool.wait_ge(s_ring, chunk_no(i, c) + 1)
                    wait(pool, s_staged, chunk_no(i, c) - 1)
                    apart(pool)
                    for t in range(TC):
                        pool.indirect_dma_start(gathered[:, slot, t * tw:(t + 1) * tw], None, src_tables[i],
                                                at(src_ring[:, slot, t:t + 1], 0)).then_inc(s_gather[slot], 16)

                def place(j):
                    pool.indirect_dma_start(run_start_rows, at(start_i[:, j:j + 1], 0), nf[:, j, :], None,
                                            bounds_check=E - 1, oob_is_err=False).then_inc(s_scatter, 16)

                def place_first():
                    pool.indirect_dma_start(dst_first[:, :], None, dst_table, at(first_i[:, 0:1], 0)).then_inc(s_first, 16)

                if i:
                    if k["dst_w"]:
                        pool.wait_ge(s_filled, dst_chunk_no(i, 0))
                        for b, (j0, m) in enumerate(BLOCKS):
                            pool.wait_ge(s_table, (i - 1) * NBL + b + 1)
                            for j in range(j0, j0 + m):
                                place(j)
                    tables += NBL * (2 if k["dst_w"] else 1)
                    pool.wait_ge(s_table_w, 16 * tables)
                    if k["dst_w"]:
                        place_first()
                    gather(0, 0, 0)
                    gather(1, 1, 0)
                else:
                    gather(0, 0, 0)
                    gather(1, 1, 0)
                    tables = 1
                    pool.wait_ge(s_place, 1)
                    pool.wait_ge(s_zeroed, 16 * NCH)
                    for j in range(J):
                        place(j)
                    pool.wait_ge(s_table_w, 16)
                    place_first()
                with pool.Fori(1, NCH // 2) as kk:
                    for slot in range(2):
                        gather(2 * kk + slot, slot, kk)
                for slot in range(2):
                    pool.wait_ge(s_store[slot], 32 * (i + 1) * (NCH // 2))
                ends = ends_view(wd)
                for b, (j0, m) in enumerate(BLOCKS):
                    for j in range(j0, j0 + m):
                        pool.indirect_dma_start(ends[:, j, :], None, message_rows[PASSES[i]],
                                                at(end_i[:, j:j + 1], 0)).then_inc(s_ends[b], 16)

        @block.scalar
        def _(act):
            act.wait_ge(s_idx_in, 32)
            for slot in range(2):
                act.copy(src_ring[:, slot, :], src_i[:, slot * TC:(slot + 1) * TC]).then_inc(s_ring, 1)
            act.wait_ge(s_const, 32)
            act.wait_ge(s_ef_in, 32)
            act.wait_ge(s_ones_col, 1)
            for i in range(NP):
                kind = PASSES[i]
                k = KIND[kind]
                nh = k["heads"]
                if i == 4:
                    act.wait_ge(s_sq, 1)
                    act.activation(tot[:, 1:2], tot[:, 1:2], ACT.Sqrt)
                    act.activation(sm[:, 6:8, :], sm[:, 6:8, :], ACT.Sqrt).then_inc(s_sqd, 1)
                    act.wait_ge(s_gate, 1)
                    act.activation(nd[:, 0, :], nd[:, 0, :], ACT.Exp, scale=-1.0).then_inc(s_gated, 1)

                def arrive(c, slot, turn):
                    act.wait_ge(s_gather[slot], 16 * TC * (i * (NCH // 2) + turn + 1))
                    apart(act)
                    act.copy(src_ring[:, slot, :], src_i[:, bass.ds((c + 2) * TC, TC)]).then_inc(s_ring, 1)
                    wait(act, s_free, chunk_no(i, c) - 1)
                    tw = k["src_w"]
                    rows = gathered[:, slot, 0:TC * tw].rearrange("p (t c) -> p t c", c=tw)
                    if kind == "filter":
                        features, rest = filter_stage(slot)
                        act.copy(features[:, :, 33:34], rows[:, :, 0:1])
                        act.copy(rest, rows[:, :, 1:tw]).then_inc(s_staged, 1)
                    else:
                        act.copy(stage[:, slot, :, 0:tw], rows).then_inc(s_staged, 1)
                    if kind == "egat":
                        act.copy(stage[:, slot, :, 33:65], edge_feat[:, cols(c), :]).then_inc(s_ef, 1)

                def feat_copy(c, g):
                    act.wait_ge(s_T, group_no(i, c, g) + 1)
                    wait(act, s_main, group_no(i, c, g) - 1)
                    n = GT // k["pair"] * P
                    act.copy(featT[0:k["feat"], g % 2, 0:n], ps_featT[g % 2][0:k["feat"], 0:n]).then_inc(s_featT, 1)

                def hidden(c, g):
                    act.wait_ge(s_main, group_no(i, c, g) + 1)
                    wait(act, s_le, group_no(i, c, g) - 1)
                    m = GT // k["pair"] * P
                    o, n = hidT[0:k["hid"], g % 2, 0:m], ps_hid[g % 2][0:k["hid"], 0:m]
                    if kind == "egat":
                        act.activation(o, n, ACT.Relu)
                        act.activation(hid_negT[0:k["hid"], g % 2, 0:GT * P], n, ACT.Relu, scale=-1.0).then_inc(s_hid, 1)
                    else:
                        act.activation(o, n, ACT.Relu, bias=w("be1", k["hid"])).then_inc(s_hid, 1)

                def logit_copy(c, slot, g):
                    act.wait_ge(s_le, group_no(i, c, g) + 1)
                    le = ps_le[g % 2][0:P, 0:GT * k["le"]].rearrange("p (t c) -> p t c", c=k["le"])
                    lg = logits[:, slot, 0:TC * nh].rearrange("p (t h) -> p t h", h=nh)[:, g * GT:(g + 1) * GT, :]
                    if kind == "egat":
                        last = act.copy(lg, le[:, :, 0:H])
                        if i < 2:
                            last = act.copy(edge_feat[:, bass.ds(c * TC + g * GT, GT), :], le[:, :, H:36])
                        last.then_inc(s_lec, 1)
                    else:
                        act.activation(lg, le, ACT.Identity, scale=10.0, bias=be2s[:, 0:1]).then_inc(s_lec, 1)

                def chunk(c, slot, turn):
                    arrive(c, slot, turn)
                    if k["feat"]:
                        if kind == "filter" and isinstance(c, int) and c == 0:
                            act.wait_ge(s_place, 1)
                        for g in range(NG + 2):
                            if g < NG:
                                feat_copy(c, g)
                            if 1 <= g <= NG:
                                hidden(c, g - 1)
                            if g >= 2:
                                logit_copy(c, slot, g - 2)
                    if nh:
                        act.wait_ge(s_arg, soft_chunk_no(i, c) + 1)
                        act.activation(decay[:, 0:TC * nh], d_arg[:, 0:TC * nh], ACT.Exp)
                        act.activation(ps_w[0:P, 0:TC * nh], w_arg[:, 0:TC * nh], ACT.Exp).then_inc(s_exp, 1)

                chunks(act, chunk)

                if nh:
                    a = before(i, lambda k: k["heads"])
                    act.wait_ge(s_carg, a + 1)
                    for h in range(nh):
                        last = act.activation(weights_pq[:, h * P:(h + 1) * P], seen[:, h * P:(h + 1) * P], ACT.Exp,
                                              bias=tail[:, width(i) - nh + h:width(i) - nh + h + 1])
                    last.then_inc(s_cexp, 1)
                cv = carried_view(width(i))
                for n, (j, m) in enumerate(SEL):
                    act.wait_ge(s_sel, i * len(SEL) + n + 1)
                    act.copy(cv[:, j:j + m, :], bank[n % 2][0:P, 0:m * width(i)].rearrange("p (j c) -> p j c", c=width(i)))\
                       .then_inc(s_selc, 1)
                def end_weights(b):
                    if nh:
                        j, m = BLOCKS[b]
                        act.wait_ge(s_narg, a * NBL + b + 1)
                        act.activation(hw[:, 2:4, j * nh:(j + m) * nh], hw[:, 0:2, j * nh:(j + m) * nh], ACT.Exp)\
                           .then_inc(s_nexp, 1)

                def products(b):
                    if i not in TPASS:
                        return
                    pr = PROD[kind]
                    for n, j, m in groups(b):
                        g, hg = prod_no(i) * NGR + n, hid_no(i) * NGR + n
                        act.wait_ge(s_nT, g + 1)
                        act.copy(featT[0:pr["k"], n % 2, 0:m * P], bank[4 + n % 2][0:pr["k"], 0:m * P]).then_inc(s_nTc, 1)
                        if pr["hid"]:
                            act.wait_ge(s_nh, hg + 1)
                            o, v = hidT[:, n % 2, 0:m * P], bank[6][:, 0:m * P]
                            if kind == "sage":
                                act.activation(o, v, ACT.Relu).then_inc(s_nhc, 1)
                            else:
                                act.activation(o, v, ACT.Identity, bias=w("bias_gat")).then_inc(s_nhc, 1)

                def finish(b):
                    j, m = BLOCKS[b]
                    if kind == "gat":
                        act.wait_ge(s_elu, b + 1)
                        act.activation(rr[:, j:j + m, :], rr[:, j:j + m, :], ACT.Exp).then_inc(s_elud, 1)
                    if i in (2, 4, 5, 6):
                        act.wait_ge(s_var, (2, 4, 5, 6).index(i) * NBL + b + 1)
                        act.activation(sm[:, 2, j:j + m], sm[:, 2, j:j + m], ACT.Sqrt).then_inc(s_std, 1)
                    if kind == "filter":
                        for n, j, m in groups(b):
                            act.wait_ge(s_xT, n + 1)
                            act.copy(featT[0:C, n % 2, 0:m * P], bank[4 + n % 2][0:C, 0:m * P]).then_inc(s_xTc, 1)

                end_weights(0)
                products(0)
                end_weights(1)
                finish(0)
                products(1)
                end_weights(2)
                finish(1)
                products(2)
                finish(2)

        @block.tensor
        def _(pe):
            ident = cst("ident", P, P)
            ones = cst("ones", P, P)
            pe.wait_ge(s_const, 32)

            def histogram(turn):
                def count(b, slot, start=False, stop=False):
                    pe.wait_ge(s_hot, turn * NHB + b + 1)
                    for t in range(HB):
                        last = pe.matmul(ps_misc[0:P, 0:J], hot(slot)[0][:, t, :], hot(slot)[1][:, t, :],
                                         start=start and t == 0, stop=stop and t == HB - 1)
                    last.then_inc(s_hist, 1)

                count(0, 0, start=True)
                count(1, 1)
                with pe.Fori(1, NHB // 2 - 1) as kk:
                    for slot in range(2):
                        count(2 * kk + slot, slot)
                count(NHB - 2, 0)
                count(NHB - 1, 1, stop=True)

            histogram(0)
            pe.wait_ge(s_tot, 1)
            pe.matmul(ps_misc[0:P, 64:65], cst("tri", P, P), tot[:, 0:1], start=True, stop=True).then_inc(s_off, 1)
            pe.wait_ge(s_rowsd, 1)
            pe.matmul(bank[2][0:P, 0:2 * P], ones, diag[:, 0:2 * P], start=True, stop=True).then_inc(s_bcast, 1)

            for i in range(NP):
                kind = PASSES[i]
                k = KIND[kind]
                nh, wd = k["heads"], width(i)

                two = k.get("pair", 1)

                def transposes(c, slot, g):
                    wait(pe, s_featT, group_no(i, c, g) - 1)
                    for u in range(GT // two):
                        t = g * GT + two * u
                        last = pe.transpose(ps_featT[g % 2][0:k["feat"], u * P:(u + 1) * P],
                                            filter_stage(slot)[0][:, t:t + two, :].rearrange("p t c -> p (t c)")
                                            if kind == "filter" else stage[:, slot, t, 0:k["feat"]], ident)
                    last.then_inc(s_T, 1)

                def main(c, g):
                    pe.wait_ge(s_featT, group_no(i, c, g) + 1)
                    wait(pe, s_hid, group_no(i, c, g) - 1)
                    lhs = w("edge", 97)[:, i * 128:(i + 1) * 128] if kind == "egat" else w("filt1", k["feat"])
                    n = GT // two * P
                    pe.matmul(ps_hid[g % 2][0:k["hid"], 0:n], lhs, featT[0:k["feat"], g % 2, 0:n],
                              start=True, stop=True).then_inc(s_main, 1)

                def logit(c, g):
                    pe.wait_ge(s_hid, group_no(i, c, g) + 1)
                    wait(pe, s_lec, group_no(i, c, g) - 1)
                    n = k["le"]
                    if kind == "egat":
                        for t in range(GT):
                            o = ps_le[g % 2][0:P, t * n:(t + 1) * n]
                            pe.matmul(o, hidT[:, g % 2, t * P:(t + 1) * P], att[:, i, :], start=True, stop=False)
                            last = pe.matmul(o, hid_negT[:, g % 2, t * P:(t + 1) * P], att_neg[:, i, :],
                                             start=False, stop=True)
                    else:
                        for u in range(GT // two):
                            last = pe.matmul(ps_le[g % 2][0:P, u * two:(u + 1) * two],
                                             hidT[0:k["hid"], g % 2, u * P:(u + 1) * P], w("filt2", k["hid"]),
                                             start=True, stop=True)
                    last.then_inc(s_le, 1)

                def chunk(c, slot, turn):
                    pe.wait_ge(s_filled, dst_chunk_no(i, c) + 1)
                    if kind == "egat":
                        pe.wait_ge(s_ef, before(i, lambda k: k["feat"] == 97) * NCH + c + 1)
                    else:
                        pe.wait_ge(s_staged, chunk_no(i, c) + 1)
                    for g in range(NG + 2):
                        if g < NG:
                            transposes(c, slot, g)
                        if 1 <= g <= NG:
                            main(c, g - 1)
                        if g >= 2:
                            logit(c, g - 2)

                if k["feat"]:
                    if i == 0:
                        pe.wait_ge(s_att, 1)
                    chunks(pe, chunk)
                if i == 3:
                    histogram(1)
                if i == 4:
                    pe.wait_ge(s_wlr, 1)
                    pe.matmul(ps_misc[0:P, 64:65], ones, tot[:, 0:1], start=True, stop=True).then_inc(s_off, 1)
                    pe.wait_ge(s_wlr, 2)
                    pe.matmul(ps_misc[0:P, 65:66], ones, tot[:, 1:2], start=True, stop=True).then_inc(s_off, 1)

                if nh:
                    a = before(i, lambda k: k["heads"])
                    for r in range(2):
                        pe.wait_ge(s_diag, 2 * a + r + 1)
                        pe.matmul(bank[2][0:P, 0:nh * P], ones, diag[:, 0:nh * P], start=True, stop=True).then_inc(s_bcast, 1)
                    pe.wait_ge(s_cexp, a + 1)
                    for h in range(nh):
                        last = pe.matmul(bank[3][0:P, h * CW:(h + 1) * CW], weights_pq[:, h * P:(h + 1) * P],
                                         tail[:, h * CW:(h + 1) * CW], start=True, stop=True)
                else:
                    pe.wait_ge(s_scan, chunk_no(i, NCH))
                if k["plain"]:
                    p0 = nh * CW
                    src_rows = tail[:, p0:p0 + C] if nh else msg[:, 1, (TC - 1) * wd:(TC - 1) * wd + C]
                    last = pe.matmul(bank[3][0:P, p0:p0 + C], cont01[:, :], src_rows, start=True, stop=True)
                last.then_inc(s_carry_mm, 1)
                pe.wait_ge(s_carry, i + 1)
                own = owner[:, :].rearrange("q (p j) -> q j p", j=J)
                for n, (j, m) in enumerate(SEL):
                    wait(pe, s_selc, i * len(SEL) + n - 1)
                    for e in range(m):
                        last = pe.matmul(bank[n % 2][0:P, e * wd:(e + 1) * wd], own[:, j + e, :], carry[:, 0:wd],
                                         start=True, stop=True)
                    last.then_inc(s_sel, 1)
                def transposed(src_, rows, g, n, j, m, done, copied):
                    wait(pe, copied, g - 1)
                    for e in range(m):
                        last = pe.transpose(bank[4 + n % 2][0:rows, e * P:(e + 1) * P], src_[:, j + e, 0:rows], ident)
                    last.then_inc(done, 1)
                    pe.wait_ge(copied, g + 1)

                for b in range(NBL):
                    if i in TPASS:
                        pr = PROD[kind]
                        out_w = pr["m"]
                        pe.wait_ge(s_agg, (i if i < 4 else i - 1) * NBL + b + 1)
                        for n, j, m in groups(b):
                            g, hg = prod_no(i) * NGR + n, hid_no(i) * NGR + n
                            transposed(aggregate, pr["k"], g, n, j, m, s_nT, s_nTc)
                            lhs = featT
                            if pr["hid"]:
                                wait(pe, s_nhc, hg)
                                pe.matmul(bank[6][:, 0:m * P], w(pr["hid"], pr["k"]), featT[0:pr["k"], n % 2, 0:m * P],
                                          start=True, stop=True).then_inc(s_nh, 1)
                                pe.wait_ge(s_nhc, hg + 1)
                                lhs = hidT
                            rhs = w("node")[:, i * C:(i + 1) * C] if kind == "egat" else w({"sage": "sage2", "gat": "wout"}[kind])
                            for e in range(m):
                                (_, _, bk, at), = product_at(j + e, 1, out_w)
                                last = pe.matmul(bank[bk][0:P, at:at + out_w], lhs[:, n % 2, e * P:(e + 1) * P], rhs,
                                                 start=True, stop=True)
                        last.then_inc(s_no, 1)
                    if kind == "filter":
                        pe.wait_ge(s_agg, (i - 1) * NBL + b + 1)
                        for n, j, m in groups(b):
                            transposed(X, C, n, n, j, m, s_xT, s_xTc)
                            for e in range(m):
                                (_, _, bk, at), = product_at(j + e, 1, 2 * H)
                                last = pe.matmul(bank[bk][0:P, at:at + 2 * H], featT[0:C, n % 2, e * P:(e + 1) * P],
                                                 wlr[:, :], start=True, stop=True)
                        last.then_inc(s_lr, 1)
        @block.vector
        def _(dve):
            chain = [0]

            def link(ins):
                chain[0] += 1
                ins.then_inc(s_v, 1)
                dve.wait_ge(s_v, chain[0])

            tt, ts, stt = dve.tensor_tensor, dve.tensor_scalar, dve.scalar_tensor_tensor
            IDENT = cst("ident", P, P)

            def bc(ap, n):
                s = [int(d) for d in ap.shape]
                return ap.unsqueeze(len(s)).broadcast_to(s + [n])

            dve.memset(msg[:, 0, 0:TC * CW], 0.0).then_inc(s_zero, 1)
            dve.memset(prev_i[0:1, :], -1)
            dve.memset(stage[:, :, :, 32:33], 1.0).then_inc(s_ones_col, 1)
            dve.wait_ge(s_dst_in, 48)
            dve.wait_ge(s_const, 32)
            dve.tensor_copy(first_i[:, :], dst_i[:, 0:1])
            link(dve.tensor_copy(dst_f, dst_i[:, :]))

            def histogram(turn, ids):
                link(ts(hi_f, ids, 1.0 / J, 0.5 / J - 0.5, ALU.mult, ALU.add))
                link(ts(hi_f, hi_f, MAGIC, MAGIC, ALU.add, ALU.subtract))
                if turn == 0:
                    dve.tensor_copy(iota_b[:, :], iota_f)
                dve.tensor_copy(hi_lo[:, 0:T], hi_f)
                link(stt(hi_lo[:, T:2 * T], hi_f, -float(J), ids, ALU.mult, ALU.add))

                def build(b, slot):
                    wait(dve, s_hist, turn * NHB + b - 1)
                    hi, lo = hi_lo[:, bass.ds(b * HB, HB)], hi_lo[:, bass.ds(b * HB + T, HB)]
                    io = iota_b
                    tt(hot(slot)[0], bc(hi, P), io[:, 0:P].unsqueeze(1).broadcast_to([P, HB, P]), ALU.is_equal)
                    tt(hot(slot)[1], bc(lo, J), io[:, 0:J].unsqueeze(1).broadcast_to([P, HB, J]), ALU.is_equal)\
                        .then_inc(s_hot, 1)

                build(0, 0)
                build(1, 1)
                with dve.Fori(1, NHB // 2) as kk:
                    for slot in range(2):
                        build(2 * kk + slot, slot)
                dve.wait_ge(s_hist, (turn + 1) * NHB)

            histogram(0, dst_f)
            link(dve.tensor_copy(deg, ps_misc[0:P, 0:J]))
            START, ENDP, HAS, PEND, CROSS, INCL, OWN, CNEG, RDEG, DEG1 = range(10)
            GATE, RS_DST, HN, RS_SRC = START, ENDP, PEND, INCL

            def ndc(r):
                return nd[:, r, :]

            link(dve.tensor_tensor_scan(ndc(INCL), cst("ones", P, J), deg, 0.0, ALU.mult, ALU.add))
            dve.tensor_copy(tot[:, 0:1], nd[:, INCL, J - 1:J]).then_inc(s_tot, 1)
            link(ts(ndc(HAS), deg, 1.0, None, ALU.min))
            link(ts(ndc(DEG1), deg, 1.0, None, ALU.max))
            link(dve.reciprocal(ndc(RDEG), ndc(DEG1)))
            link(tt(ndc(START), ndc(INCL), deg, ALU.subtract))
            dve.wait_ge(s_off, 1)
            link(ts(ndc(START), ndc(START), ps_misc[0:P, 64:65], None, ALU.add))
            link(stt(ndc(ENDP), ndc(START), -1.0, deg, ALU.add, ALU.add))
            link(ts(ndc(PEND), ndc(ENDP), 1.0 / T, 0.5 / T - 0.5, ALU.mult, ALU.add))
            link(ts(ndc(PEND), ndc(PEND), MAGIC, MAGIC, ALU.add, ALU.subtract))
            link(ts(ndc(CROSS), ndc(PEND), float(T), None, ALU.mult))
            link(tt(ndc(CROSS), ndc(START), ndc(CROSS), ALU.is_lt))
            link(tt(ndc(CROSS), ndc(CROSS), ndc(HAS), ALU.mult))
            link(stt(ndc(OWN), ndc(PEND), 1.0, ndc(CROSS), ALU.add, ALU.mult))
            link(ts(ndc(OWN), ndc(OWN), -1.0, None, ALU.add))
            link(ts(ndc(CNEG), ndc(CROSS), -1.0, BIG, ALU.add, ALU.mult))
            link(ts(ndc(ENDP), ndc(ENDP), 0.0, None, ALU.max))
            link(dve.tensor_copy(end_i[:, :], ndc(ENDP)))
            link(ts(ndc(INCL), ndc(HAS), -1.0, -1.0e6, ALU.add, ALU.mult))
            link(tt(ndc(INCL), ndc(INCL), ndc(START), ALU.add))
            link(dve.tensor_copy(start_i[:, :], ndc(INCL)))
            link(ts(be2s[:, :], w("be2", P), 10.0, None, ALU.mult))
            dve.wait_ge(s_x_in, 16)
            dve.memset(nf[:, :, C:CW], 0.0)
            dve.tensor_copy(nf[:, :, 0:C], X[:, :, :]).then_inc(s_rows, 1)
            dve.tensor_copy(same_neg[:, 0:1], prev_i[:, :]).then_inc(s_place, 1)
            dve.wait_ge(s_place, 1)
            tt(same[:, 0:1], dst_f[:, 0:1], same_neg[:, 0:1], ALU.is_equal)
            link(tt(same[:, 1:T], dst_f[:, 1:T], dst_f[:, 0:T - 1], ALU.is_equal))
            link(ts(same_neg[:, :], same[:, :], -1.0, BIG, ALU.add, ALU.mult))
            ts(diag[:, 0:P], IDENT, dst_f[:, T - 1:T], None, ALU.mult)
            ts(diag[:, P:2 * P], IDENT, dst_f[:, 0:1], None, ALU.mult).then_inc(s_rowsd, 1)
            for l in range(3):
                dve.tensor_copy(att[:, l, 0:H], w("att")[:, l * H:(l + 1) * H])
                last = dve.tensor_copy(att[:, l, H:36], cst("mean", 128))
            link(last)
            ts(att_neg[:, :, :], att[:, :, :], -NEG_SLOPE, None, ALU.mult).then_inc(s_att, 1)
            dve.wait_ge(s_bcast, 1)
            link(ts(cont01[:, :], bank[2][0:P, P:2 * P], dst_f[:, T - 1:T], None, ALU.is_equal))
            link(tt(cont01[:, :], cont01[:, :], cst("tri", P, P), ALU.mult))
            ts(cont_neg[:, :], cont01[:, :], -1.0, 1.0e36, ALU.add, ALU.mult)
            link(ts(contT_neg[:, :], bank[2][0:P, 0:P], dst_f[:, 0:1], None, ALU.is_equal))
            link(tt(contT_neg[:, :], contT_neg[:, :], cst("triT", P, P), ALU.mult))
            link(ts(contT_neg[:, :], contT_neg[:, :], -1.0, BIG, ALU.add, ALU.mult))
            dve.sem_inc(s_setup, 1)
            dve.wait_ge(s_owner_r, 16)
            link(ts(owner[:, :], owner[:, :], cst("col", P), None, ALU.is_equal))

            def degree_terms():
                link(dve.tensor_reduce(tot[:, 0:1], ndc(DEG1), AX, ALU.add))
                dve.sem_inc(s_wlr, 1)
                dve.wait_ge(s_off, 2)
                link(ts(tot[:, 0:1], ps_misc[0:P, 64:65], 1.0 / N, None, ALU.mult))
                link(ts(ndc(HN), ndc(DEG1), tot[:, 0:1], None, ALU.subtract))
                link(tt(sm[:, 5, :], ndc(HN), ndc(HN), ALU.mult))
                dve.tensor_reduce(tot[:, 1:2], sm[:, 5, :], AX, ALU.add).then_inc(s_wlr, 1)
                dve.wait_ge(s_off, 3)
                ts(tot[:, 1:2], ps_misc[0:P, 65:66], 1.0 / (N - 1), None, ALU.mult)
                dve.tensor_copy(sm[:, 6, :], ndc(DEG1))
                ts(sm[:, 7, :], sdeg[:, :], 1.0, None, ALU.max).then_inc(s_sq, 1)
                dve.wait_ge(s_sqd, 1)
                link(ts(tot[:, 1:2], tot[:, 1:2], 1e-8, None, ALU.add))
                link(dve.reciprocal(tot[:, 1:2], tot[:, 1:2]))
                link(ts(ndc(HN), ndc(HN), tot[:, 1:2], None, ALU.mult))
                dve.reciprocal(ndc(RS_DST), sm[:, 6, :])
                link(dve.reciprocal(ndc(RS_SRC), sm[:, 7, :]))
                gw = dst_in_flat[:, 0:J * 16].rearrange("p (j c) -> p j c", c=16)

                def w16(name):
                    return w(name, P).unsqueeze(1).broadcast_to([P, J, 16])

                link(tt(gw, bc(ndc(HN), 16), w16("wn1"), ALU.mult))
                link(tt(gw, gw, w16("bn1"), ALU.add))
                link(ts(gw, gw, 0.0, None, ALU.max))
                link(tt(gw, gw, w16("wn2"), ALU.mult))
                link(dve.tensor_reduce(ndc(GATE), gw, AX, ALU.add))
                ts(ndc(GATE), ndc(GATE), w("bn2", P), None, ALU.add).then_inc(s_gate, 1)
                dve.wait_ge(s_gated, 1)
                link(ts(ndc(GATE), ndc(GATE), 1.0, None, ALU.add))
                link(dve.reciprocal(ndc(GATE), ndc(GATE)))

            for i in range(NP):
                kind = PASSES[i]
                k = KIND[kind]
                nh, wd, dw = k["heads"], width(i), k["dst_w"]
                plain = k["plain"]

                def msg3(slot):
                    return msg[:, slot, 0:TC * wd].rearrange("p (t c) -> p t c", c=wd)

                def fill(c, slot, turn):
                    dve.wait_ge(s_dstrow[slot], 16 * (before(i, lambda k: k["dst_w"]) * (NCH // 2) + turn + 1))
                    wait(dve, s_free, chunk_no(i, c) - 1)
                    first = isinstance(c, int) and c == 0
                    if first:
                        dve.wait_ge(s_first, 16 * (before(i, lambda k: k["dst_w"]) + 1))
                    if kind == "filter":
                        wait(dve, s_fsub, 2 * c - 1)
                    else:
                        wait(dve, s_filled, dst_chunk_no(i, c))
                    into = (filter_stage(slot)[0] if kind == "filter" else stage[:, slot, :, :])[:, :, k["dst_at"]:k["dst_at"] + dw]
                    for ch in range(dw):
                        init = dst_first[:, ch:ch + 1] if first else dst_last[:, ch:ch + 1]
                        last = dve.tensor_tensor_scan(into[:, :, ch], same[:, cols(c)], dst_in[:, slot, :, ch],
                                                      init, ALU.mult, ALU.add)
                    last.then_inc(s_fscan, 1)
                    dve.wait_ge(s_fscan, dst_chunk_no(i, c) + 1)
                    last = dve.tensor_copy(dst_last[:, 0:dw], into[:, TC - 1, :])
                    last.then_inc(s_fsub if kind == "filter" else s_filled, 1)

                def difference(c, slot):
                    dve.wait_ge(s_staged, chunk_no(i, c) + 1)
                    dve.wait_ge(s_fsub, 2 * c + 1)
                    d, rest = filter_stage(slot)[0][:, :, 0:C], filter_stage(slot)[1]
                    tt(d, d, rest[:, :, 0:C], ALU.subtract).then_inc(s_fsub, 1)
                    dve.wait_ge(s_fsub, 2 * c + 2)
                    stt(d, d, -1.0, d, ALU.mult, ALU.max).then_inc(s_filled, 1)

                def head_view(buf):
                    return buf.rearrange("p (t h) -> p t h", h=nh)

                def maxima(c, slot, turn):
                    first = isinstance(c, int) and c == 0
                    sc = soft_chunk_no(i, c)
                    lg = head_view(logits[:, slot, 0:TC * nh])
                    if first:
                        dve.memset(run_max[:, 0, 0:nh], -BIG).then_inc(s_mcar, 1)
                    else:
                        dve.tensor_copy(run_max[:, 0, 0:nh], run_max[:, TC, 0:nh]).then_inc(s_mcar, 1)
                    if kind == "gat":
                        dve.wait_ge(s_staged, chunk_no(i, c) + 1)
                        dve.wait_ge(s_filled, dst_chunk_no(i, c) + 1)
                        tt(head_view(w_arg[:, 0:TC * nh]), stage[:, slot, :, 33:37], stage[:, slot, :, 40:44], ALU.add)\
                            .then_inc(s_lg, 1)
                        dve.wait_ge(s_lg, 2 * c + 1)
                        stt(lg, head_view(w_arg[:, 0:TC * nh]), NEG_SLOPE, head_view(w_arg[:, 0:TC * nh]), ALU.mult, ALU.max)\
                            .then_inc(s_lg, 1)
                        dve.wait_ge(s_lg, 2 * c + 2)
                    else:
                        dve.wait_ge(s_lec, group_no(i, c, NG))
                    dve.wait_ge(s_mcar, sc + 1)
                    for h in range(nh):
                        last = dve.tensor_tensor_scan(run_max[:, 1:TC + 1, h], same_neg[:, cols(c)], lg[:, :, h],
                                                      run_max[:, 0, h:h + 1], ALU.add, ALU.max)
                    last.then_inc(s_max, 1)
                    dve.wait_ge(s_max, sc + 1)
                    wait(dve, s_exp, sc)
                    tt(head_view(w_arg[:, 0:TC * nh]), lg, run_max[:, 1:TC + 1, 0:nh], ALU.subtract)
                    tt(head_view(d_arg[:, 0:TC * nh]), run_max[:, 0:TC, 0:nh], run_max[:, 1:TC + 1, 0:nh], ALU.subtract)\
                        .then_inc(s_max2, 1)
                    dve.wait_ge(s_max2, sc + 1)
                    tt(head_view(d_arg[:, 0:TC * nh]), head_view(d_arg[:, 0:TC * nh]), bc(same_neg[:, cols(c)], nh), ALU.add)\
                        .then_inc(s_arg, 1)

                def weigh(c, slot, turn):
                    if not (isinstance(c, int) and i == 0 and c < 2):
                        dve.wait_ge(s_store[slot], 32 * (i * (NCH // 2) + turn))
                    m3 = msg3(slot)
                    if plain:
                        rest = filter_stage(slot)[1]
                        tt(m3[:, :, CW:CW + C], rest[:, :, 0:C], bc(rest[:, :, 33], C), ALU.mult)
                    dve.wait_ge(s_exp, soft_chunk_no(i, c) + 1)
                    dve.tensor_copy(m3[:, :, wd - nh:wd], run_max[:, 1:TC + 1, 0:nh])
                    if nh > 1:
                        o = m3[:, :, 0:nh * CW].rearrange("p t (h c) -> p t h c", c=CW)
                        wgt = bc(head_view(ps_w[0:P, 0:TC * nh]), CW)
                        row = stage[:, slot, :, 0:CW].unsqueeze(2).broadcast_to([P, TC, nh, CW])
                    else:
                        o = m3[:, :, 0:CW]
                        wgt = bc(ps_w[0:P, 0:TC], CW)
                        row = filter_stage(slot)[1][:, :, 0:CW]
                    tt(o, wgt, row, ALU.mult).then_inc(s_mult, 1)
                    if not plain:
                        dve.wait_ge(s_mult, soft_chunk_no(i, c) + 1)
                        dve.sem_inc(s_free, 1)

                def sums(c, slot, turn):
                    first = isinstance(c, int) and c == 0
                    m3, p3 = msg3(slot), msg3(1 - slot)
                    wait(dve, s_scan, chunk_no(i, c))
                    if nh:
                        dve.wait_ge(s_mult, soft_chunk_no(i, c) + 1)
                    else:
                        dve.wait_ge(s_staged, chunk_no(i, c) + 1)
                        if not (isinstance(c, int) and i == 0 and c < 2):
                            dve.wait_ge(s_store[slot], 32 * (i * (NCH // 2) + turn))
                    dv = head_view(decay[:, 0:TC * nh]) if nh else None
                    for h in range(nh):
                        for ch in range(CW):
                            q = h * CW + ch
                            last = dve.tensor_tensor_scan(m3[:, :, q], dv[:, :, h], m3[:, :, q],
                                                          0.0 if first else p3[:, TC - 1, q:q + 1], ALU.mult, ALU.add)
                    for ch in range(plain):
                        q = nh * CW + ch
                        last = dve.tensor_tensor_scan(m3[:, :, q], same[:, cols(c)],
                                                      m3[:, :, q] if nh else stage[:, slot, :, ch],
                                                      0.0 if first else p3[:, TC - 1, q:q + 1], ALU.mult, ALU.add)
                    last.then_inc(s_scan, 1)
                    if plain:
                        dve.wait_ge(s_scan, chunk_no(i, c) + 1)
                        dve.sem_inc(s_free, 1)

                if kind == "egat" and i:
                    link(dve.memset(stage[:, :, :, 32:33], 1.0))
                if nh:
                    def step(c, slot, turn, last=False):
                        if kind == "filter":
                            difference(c, slot)
                        if not (isinstance(c, int) and c == 0):
                            sums(c - 1, 1 - slot, turn - 1 + slot)
                        if not last:
                            fill(c + 1, 1 - slot, turn + slot)
                        maxima(c, slot, turn)
                        weigh(c, slot, turn)

                    fill(0, 0, 0)
                    step(0, 0, 0)
                    step(1, 1, 0)
                    with dve.Fori(1, NCH // 2 - 1) as kk:
                        for slot in range(2):
                            step(2 * kk + slot, slot, kk)
                    step(NCH - 2, 0, NCH // 2 - 1)
                    step(NCH - 1, 1, NCH // 2 - 1, last=True)
                    sums(NCH - 1, 1, NCH // 2 - 1)
                else:
                    if i == 3:
                        link(dve.tensor_copy(id_f, src_i[:, 0:T]))
                        histogram(1, id_f)
                        link(dve.tensor_copy(sdeg[:, :], ps_misc[0:P, 0:J]))
                    if i == 4:
                        degree_terms()
                    chunks(dve, sums)

                a = before(i, lambda k: k["heads"])
                if nh:
                    m0 = wd - nh
                    dve.wait_ge(s_scan, chunk_no(i, NCH))
                    link(dve.tensor_copy(tail[:, 0:wd], msg[:, 1, (TC - 1) * wd:TC * wd]))
                    for h in range(nh):
                        last = ts(diag[:, h * P:(h + 1) * P], IDENT, tail[:, m0 + h:m0 + h + 1], None, ALU.mult)
                    last.then_inc(s_diag, 1)
                    dve.wait_ge(s_bcast, 1 + 2 * a + 1)
                    v3 = seen[:, 0:nh * P].rearrange("p (h q) -> p h q", q=P)
                    b3 = bank[2][0:P, 0:nh * P].rearrange("p (h q) -> p h q", q=P)
                    link(tt(v3, b3, contT_neg[:, :].unsqueeze(1).broadcast_to([P, nh, P]), ALU.add))
                    link(dve.tensor_reduce(carry_max[:, 0:nh], v3, AX, ALU.max))
                    for h in range(nh):
                        last = ts(diag[:, h * P:(h + 1) * P], IDENT, carry_max[:, h:h + 1], None, ALU.mult)
                    last.then_inc(s_diag, 1)
                    dve.wait_ge(s_bcast, 1 + 2 * a + 2)
                    tt(v3, cont_neg[:, :].unsqueeze(1).broadcast_to([P, nh, P]), b3, ALU.subtract).then_inc(s_carg, 1)
                dve.wait_ge(s_carry_mm, i + 1)
                if nh:
                    dve.tensor_copy(carry[:, m0:wd], carry_max[:, 0:nh])
                dve.tensor_copy(carry[:, 0:nh * CW + plain], bank[3][0:P, 0:nh * CW + plain]).then_inc(s_carry, 1)
                dve.wait_ge(s_selc, (i + 1) * len(SEL))
                en, cv = ends_view(wd), carried_view(wd)
                if nh:
                    link(tt(cv[:, :, m0:wd], cv[:, :, m0:wd], bc(ndc(CNEG), nh), ALU.add))

                def aggregate_block(b):
                    j0, m = BLOCKS[b]
                    js = slice(j0, j0 + m)
                    dve.wait_ge(s_ends[b], 16 * m * (i + 1))
                    e, v = en[:, js, :], cv[:, js, :]
                    has, x = ndc(HAS)[:, js], X[:, js, :]
                    if not nh:
                        link(tt(e, e, bc(has, C), ALU.mult))
                        link(tt(e, e, v, ALU.add))
                        if i == 3:
                            tt(aggregate[:, js, 0:C], e, bc(ndc(RDEG)[:, js], C), ALU.mult)
                            dve.memset(aggregate[:, js, 64:65], 1.0)
                            dve.tensor_copy(aggregate[:, js, C:2 * C], x).then_inc(s_agg, 1)
                        else:
                            link(tt(e, e, bc(ndc(RDEG)[:, js], C), ALU.mult))
                        return

                    def hv(r):
                        return hw[:, r, j0 * nh:(j0 + m) * nh].rearrange("p (j h) -> p j h", h=nh)

                    link(tt(hv(4), e[:, :, m0:wd], v[:, :, m0:wd], ALU.max))
                    tt(hv(0), e[:, :, m0:wd], hv(4), ALU.subtract)
                    tt(hv(1), v[:, :, m0:wd], hv(4), ALU.subtract).then_inc(s_narg, 1)
                    dve.wait_ge(s_nexp, a * NBL + b + 1)
                    tt(hv(0), hv(2), e[:, :, C:nh * CW:CW], ALU.mult)
                    link(tt(hv(1), hv(3), v[:, :, C:nh * CW:CW], ALU.mult))
                    link(tt(hv(4), hv(0), hv(1), ALU.add))
                    if kind == "filter":
                        link(ts(hv(0), hv(4), 1e-16, None, ALU.add))
                        link(dve.reciprocal(hv(0), hv(0)))
                    elif kind == "gat":
                        link(ts(hv(4), hv(4), 1e-9, None, ALU.max))
                        link(dve.reciprocal(hv(0), hv(4)))
                    else:
                        link(dve.reciprocal(hv(0), hv(4)))
                    link(tt(hv(0), hv(0), bc(has, nh), ALU.mult))
                    tt(hv(2), hv(2), hv(0), ALU.mult)
                    link(tt(hv(3), hv(3), hv(0), ALU.mult))

                    def chans(t):
                        return t[:, :, 0:nh * CW].rearrange("p j (h c) -> p j h c", c=CW)[:, :, :, 0:C] if nh > 1 else t[:, :, 0:C]

                    def share(r):
                        return bc(hv(r), C) if nh > 1 else bc(hw[:, r, js], C)

                    ag = aggregate[:, js, 0:nh * C]
                    if nh > 1:
                        ag = ag.rearrange("p j (h c) -> p j h c", c=C)
                    tt(chans(v), chans(v), share(3), ALU.mult)
                    link(tt(ag, chans(e), share(2), ALU.mult))
                    last = tt(ag, ag, chans(v), ALU.add)
                    if kind == "filter":
                        link(last)
                    else:
                        last.then_inc(s_agg, 1)

                def layer_norm(b, r):
                    j0, m = BLOCKS[b]
                    js = slice(j0, j0 + m)
                    y, sq = yt[:, js, :], rr[:, js, :]
                    link(dve.tensor_reduce(sm[:, 0, js], y, AX, ALU.add))
                    link(ts(sm[:, 0, js], sm[:, 0, js], 1.0 / C, None, ALU.mult))
                    link(tt(y, y, bc(sm[:, 0, js], C), ALU.subtract))
                    link(tt(sq, y, y, ALU.mult))
                    link(dve.tensor_reduce(sm[:, 1, js], sq, AX, ALU.add))
                    ts(sm[:, 2, js], sm[:, 1, js], 1.0 / C, LN_EPS, ALU.mult, ALU.add).then_inc(s_var, 1)
                    dve.wait_ge(s_std, r * NBL + b + 1)
                    link(dve.reciprocal(sm[:, 3, js], sm[:, 2, js]))
                    return tt(X[:, js, :], y, bc(sm[:, 3, js], C), ALU.mult)

                def update_block(b):
                    j0, m = BLOCKS[b]
                    js = slice(j0, j0 + m)
                    x, y = X[:, js, :], yt[:, js, :]
                    if i in TPASS:
                        dve.wait_ge(s_no, prod_no(i) * NBL + b + 1)
                        out_w = PROD[kind]["m"]
                        prods = [(slice(j, j + n), n, bank[bk][0:P, at:at + n * out_w].rearrange("p (j c) -> p j c", c=out_w))
                                 for j, n, bk, at in product_at(j0, m, out_w)]
                    if kind == "egat":
                        for q, n, v in prods:
                            if i < 2:
                                ts(nf[:, q, 0:C], v, 1.0 / H, None, ALU.mult)
                                ts(yt[:, q, :], v, 1.0 / H, None, ALU.mult).then_inc(s_table, 1)
                            else:
                                link(stt(yt[:, q, :], v, 1.0 / H, X[:, q, :], ALU.mult, ALU.add))
                        if i == 2:
                            layer_norm(b, 0).then_inc(s_table, 1)
                    if i == 3:
                        for q, n, v in prods:
                            dve.tensor_copy(rr[:, q, :], v[:, :, C:2 * C])
                            last = dve.tensor_copy(yt[:, q, :], v[:, :, 0:C])
                        last.then_inc(s_table, 1)
                    if i == 4:
                        e = en[:, js, :]
                        link(tt(e, e, rr[:, js, :], ALU.add))
                        link(tt(e, e, w("b2", P).unsqueeze(1).broadcast_to([P, m, C]), ALU.add))
                        link(tt(y, e, x, ALU.add))
                        link(layer_norm(b, 1))
                        tb = pair[:, 0:J * 35].rearrange("p (j c) -> p j c", c=35)[:, js, :]
                        dve.tensor_copy(tb[:, :, 0:1], ndc(HN)[:, js].unsqueeze(2))
                        dve.tensor_copy(tb[:, :, 1:33], x)
                        dve.memset(tb[:, :, 33:34], 1.0)
                        dve.tensor_copy(tb[:, :, 34:35], ndc(RS_SRC)[:, js].unsqueeze(2))
                        dve.tensor_copy(nf[:, js, 0:C], x)
                        dve.tensor_copy(nf[:, js, C:CW], ndc(HN)[:, js].unsqueeze(2)).then_inc(s_table, 1)
                    if kind == "filter":
                        low, low_c = en[:, js, CW:CW + C], cv[:, js, CW:CW + C]
                        link(tt(low, low, bc(ndc(HAS)[:, js], C), ALU.mult))
                        link(tt(low, low, low_c, ALU.add))
                        link(tt(low, low, bc(ndc(RS_DST)[:, js], C), ALU.mult))
                        link(tt(hw[:, 4, js], hw[:, 4, js], hw[:, 0, js], ALU.mult))
                        link(tt(y, x, bc(hw[:, 4, js], C), ALU.mult))
                        link(tt(y, y, aggregate[:, js, 0:C], ALU.subtract))
                        link(tt(y, y, low, ALU.subtract))
                        link(tt(y, y, bc(ndc(GATE)[:, js], C), ALU.mult))
                        link(tt(y, y, low, ALU.add))
                        link(tt(y, y, x, ALU.add))
                        layer_norm(b, 2).then_inc(s_agg, 1)
                    if kind == "gat":
                        for q, n, v in prods:
                            link(tt(yt[:, q, :], v, w("bout", P).unsqueeze(1).broadcast_to([P, n, C]), ALU.add))
                        r = rr[:, js, :]
                        ts(r, y, 0.0, None, ALU.min).then_inc(s_elu, 1)
                        link(ts(y, y, 0.0, None, ALU.max))
                        dve.wait_ge(s_elud, b + 1)
                        link(stt(r, r, -1.0, y, ALU.add, ALU.add))
                        link(stt(y, x, 2.0, r, ALU.mult, ALU.add))
                        layer_norm(b, 3).then_inc(s_table, 1)

                def gat_rows(b):
                    if kind != "filter":
                        return
                    j0, m = BLOCKS[b]
                    js = slice(j0, j0 + m)
                    dve.wait_ge(s_lr, b + 1)
                    (_, _, bk, at), = product_at(j0, m, 2 * H)
                    lr = bank[bk][0:P, at:at + m * 2 * H].rearrange("p (j c) -> p j c", c=2 * H)
                    tb = pair[:, 0:J * 37].rearrange("p (j c) -> p j c", c=37)[:, js, :]
                    dve.tensor_copy(tb[:, :, 0:C], X[:, js, :])
                    dve.memset(tb[:, :, C:CW], 1.0)
                    dve.tensor_copy(tb[:, :, 33:37], lr[:, :, 0:H])
                    dve.tensor_copy(nf[:, js, 0:H], lr[:, :, H:2 * H]).then_inc(s_table, 1)

                if kind == "filter":
                    for s in range(2):
                        link(tt(lr_tmp, w("wfc_row", C), w("attn_lr", C)[:, s * 128:(s + 1) * 128], ALU.mult))
                        link(dve.tensor_reduce(wlr[:, s * H:(s + 1) * H], lr_tmp.rearrange("c (h d) -> c h d", d=C), AX, ALU.add))
                aggregate_block(0)
                aggregate_block(1)
                update_block(0)
                aggregate_block(2)
                update_block(1)
                gat_rows(0)
                update_block(2)
                gat_rows(1)
                gat_rows(2)


def pack_weights(np, a):
    wp = np.zeros((128, WCOLS), np.float32)

    def put(name, rows, block, col=0, row=0):
        wp[row:row + rows, W_OFF[name][0] + col:W_OFF[name][0] + col + block.shape[1]] = block

    for l in range(3):
        put("edge", C, a["L0_gnn_W_ni"][l], l * 128, 0)
        put("edge", 1, a["L0_gnn_bias"][l][None], l * 128, 32)
        put("edge", C, a["L0_gnn_W_fij"][l], l * 128, 33)
        put("edge", C, a["L0_gnn_W_nj"][l], l * 128, 65)
        for h in range(H):
            put("att", C, a["L0_gnn_attn"][l, h][:, None], l * H + h, h * C)
            put("node", C, a["L0_gnn_W_node"][l][:, h * C:(h + 1) * C], l * C, h * C)
    put("sage1", C, a["L1_gnn_W1_l"].T)
    put("sage1", C, a["L1_gnn_W1_r"].T, 0, C)
    put("sage1", 1, a["L1_gnn_b1"][None], 0, 2 * C)
    put("sage2", 128, a["L1_gnn_W2_l"].T)
    put("sage2", 128, a["L1_gnn_W2_r"].T, C)
    for u in range(2):
        put("filt1", C, a["L2_gnn_We1"][2:], u * 32, u * 34)
        put("filt1", 1, a["L2_gnn_We1"][1:2], u * 32, u * 34 + C)
        put("filt1", 1, a["L2_gnn_We1"][0:1], u * 32, u * 34 + C + 1)
        put("filt2", 32, a["L2_gnn_We2"], u, u * 32)
        put("be1", 32, a["L2_gnn_be1"][:, None], 0, u * 32)
    for h in range(H):
        put("wfc", C, a["L3_gnn_W_fc"][:, h * C:(h + 1) * C], h * C, h * C)
    put("wfc_row", C, a["L3_gnn_W_fc"])
    put("attn_lr", C, np.tile(a["L3_gnn_attn_l"].reshape(1, -1), (C, 1)))
    put("attn_lr", C, np.tile(a["L3_gnn_attn_r"].reshape(1, -1), (C, 1)), 128)
    put("wout", 128, a["L3_gnn_W_out"])
    put("bias_gat", 128, a["L3_gnn_bias_gat"][:, None])
    for name, v in (("be2", a["L2_gnn_be2"]), ("b2", a["L1_gnn_b2"]), ("bout", a["L3_gnn_b_out"]),
                    ("wn1", a["L2_gnn_Wn1"]), ("bn1", a["L2_gnn_bn1"]), ("wn2", a["L2_gnn_Wn2"]),
                    ("bn2", a["L2_gnn_bn2"])):
        put(name, 128, np.tile(v.reshape(1, -1), (128, 1)))
    return wp


def pack_constants(np):
    c = np.zeros((128, CCOLS + 128), np.float32)
    c[:, 0:128] = np.eye(128)
    c[:, 128:256] = 1.0
    c[:, 256:384] = np.triu(np.ones((128, 128)), 1)
    c[:, 384:512] = np.tril(np.ones((128, 128)), -1)
    c[:, 512:544] = np.tile(np.eye(C), (H, 1)) / H
    c[:, 544] = np.arange(128)
    c[:, 545:673] = np.arange(128)[None]
    return c


def build(nc):
    f32, i32 = mybir.dt.float32, mybir.dt.int32
    shapes = {"x": ((N, C), f32), "src": ((E,), i32), "dst": ((E,), i32), "edge_attr": ((E, C), f32),
              "wpack": ((128, WCOLS), f32), "cpack": ((128, CCOLS + 128), f32)}
    ins = [nc.dram_tensor(n, s, d, kind="ExternalInput").ap() for n, (s, d) in shapes.items()]
    out = nc.dram_tensor("out", (N, C), f32, kind="ExternalOutput").ap()
    graph_kernel(nc, *ins, out)


def kernel(**inputs):
    import numpy as np
    import concourse.bacc as bacc
    from concourse.bass_utils import run_bass_kernel_spmd

    a = {n: np.ascontiguousarray(v) for n, v in inputs.items()}
    nc = bacc.Bacc("TRN2", target_bir_lowering=False, num_devices=1)
    build(nc)
    arrays = {"x": a["x"], "src": a["src"], "dst": a["dst"], "edge_attr": a["edge_attr_32"],
              "wpack": pack_weights(np, a), "cpack": pack_constants(np)}
    r = run_bass_kernel_spmd(nc, [arrays], core_ids=[0])
    return r.results[0]["out"]
```

```python
import concourse.bass as bass
from concourse import mybir
from contextlib import ExitStack

N, E, C, H = 3125, 50000, 32, 4
P = 125
T = E // P
J = N // P
TC = 40
NCH = T // TC
GT = 4
NG = TC // GT
PARTS = ((0, TC // 2), (TC // 2, TC // 2))
NPT = len(PARTS)
HB = 10
NHB = T // HB
HSLOTS = 4
CW = C + 1
ROW = H * CW + H
SW = 100
GW = 37
BIG = 1.0e30
MAGIC = 12582912.0
LN_EPS = 1e-5
NEG_SLOPE = 0.2
EDGE_SPLIT = 112

W_OFF = {}


def _w_layout():
    at = 0
    for name, n in (("edge", 3 * 128), ("att", 3 * H), ("node", 3 * C), ("sage1", 128), ("sage2", 2 * C),
                    ("filt1", 64), ("filt2", 2), ("wfc", 128), ("wfc_row", 128), ("attn_lr", 2 * 128),
                    ("wout", C), ("bias_gat", 1), ("be1", 1), ("be2", 1), ("b2", C), ("bout", C),
                    ("wn1", 16), ("bn1", 16), ("wn2", 16), ("bn2", 1)):
        W_OFF[name] = (at, n)
        at += n
    return at


WCOLS = _w_layout()
C_OFF = {"ident": (0, 128), "ones": (128, 128), "tri": (256, 128), "triT": (384, 128), "mean": (512, 32),
         "col": (544, 1)}
CCOLS = 545

PASSES = ("egat", "egat", "egat", "sage", "sage", "filter", "gat")
KIND = {
    "egat": dict(src_w=C, dst_w=C, dst_at=65, heads=H, plain=0, feat=97, hid=128, le=36, pair=1),
    "sage": dict(src_w=C, dst_w=0, dst_at=0, heads=0, plain=C, feat=0),
    "filter": dict(src_w=35, dst_w=33, dst_at=0, heads=1, plain=C,
                   feat=68, hid=64, le=1, pair=2),
    "gat": dict(src_w=37, dst_w=H, dst_at=40, heads=H, plain=0, feat=0),
}
NP = len(PASSES)


def before(i, test):
    return sum(1 for k in PASSES[:i] if test(KIND[k]))


def graph_kernel(nc, x, src, dst, edge_attr, wpack, cpack, out):
    f32, i32, bf16 = mybir.dt.float32, mybir.dt.int32, mybir.dt.bfloat16
    ALU, ACT, AX = mybir.AluOpType, mybir.ActivationFunctionType, mybir.AxisListType.X

    def dram(name, shape):
        return nc.dram_tensor(name, shape, f32).ap()

    run_start_rows = dram("run_start_rows", (E, CW))
    dst_table = dram("dst_table", (N, CW))
    message_rows = {k: dram(f"message_rows_{k}", (E, ROW if k in ("egat", "gat") else C if k == "sage" else 66))
                    for k in KIND}
    src_tables = [x] + [dram(f"src_table_{i}", (N, KIND[PASSES[i]]["src_w"])) for i in range(1, NP)]
    carry_owner_d = dram("carry_owner_d", (N,))
    sorted_src = nc.dram_tensor("sorted_src", (E,), i32).ap()
    sorted_dst = nc.dram_tensor("sorted_dst", (E,), i32).ap()
    sorted_attr = dram("sorted_attr", (E, C))

    ctx = ExitStack()
    with ctx:
        def sb(name, shape, dt=f32):
            return ctx.enter_context(nc.sbuf_tensor(name, shape, dt))

        def pb(name):
            return ctx.enter_context(nc.psum_tensor(name, [128, 512], f32))

        def sem(name):
            return ctx.enter_context(nc.semaphore(name))

        W = sb("W", [128, WCOLS])
        CS = sb("CS", [128, CCOLS])

        def w(name, rows=128):
            a, n = W_OFF[name]
            return W[0:rows, a:a + n]

        def cst(name, rows=P, cols=None):
            a, n = C_OFF[name]
            return CS[0:rows, a:a + (cols or n)]

        src_i = sb("src_i", [P, T + 2 * TC], i32)
        src_ring = sb("src_ring", [P, 2, TC], i32)
        first_i = sb("first_i", [P, 1], i32)
        prev_i = sb("prev_i", [P, 1], i32)
        same = sb("same", [P, T])
        same_neg = sb("same_neg", [P, T])
        edge_feat = sb("edge_feat", [P, T, C])
        gathered = sb("gathered", [P, 2, TC * GW])
        stage = sb("stage", [P, 2, TC, SW])
        dst_in = sb("dst_in", [P, 2, TC, CW])
        dst_first = sb("dst_first", [P, CW])
        featT = sb("featT", [128, 2, GT * P])
        hidT = sb("hidT", [128, 2, GT * P])
        hid_negT = sb("hid_negT", [128, 2, GT * P])
        logits = sb("logits", [P, 2, TC * H])
        run_max = sb("run_max", [P, TC + 1, H])
        w_arg = sb("w_arg", [P, TC * H])
        d_arg = sb("d_arg", [P, TC * H])
        decay = sb("decay", [P, TC * H])
        msg = sb("msg", [P, 2, TC * ROW])
        att = sb("att", [128, 3, 36])
        att_neg = sb("att_neg", [128, 3, 36])
        wlr = sb("wlr", [C, 2 * H])
        X = sb("X", [P, J, C])
        nf = sb("nf", [P, J, CW])
        sdeg = sb("sdeg", [P, J])
        nd = sb("nd", [P, 10, J])
        end_i = sb("end_i", [P, J], i32)
        start_i = sb("start_i", [P, J], i32)
        owner = sb("owner", [P, N])
        tail = sb("tail", [P, ROW])
        carry = sb("carry", [P, ROW])
        carry_max = sb("carry_max", [P, H])
        cont01 = sb("cont01", [P, P])
        cont_neg = sb("cont_neg", [P, P])
        contT_neg = sb("contT_neg", [P, P])
        sm = sb("sm", [P, 8, J])
        deg = sm[:, 4, :]
        hw = sb("hw", [P, 5, J * H])
        yt = sb("yt", [P, J, C])
        rr = sb("rr", [P, J, C])
        lr_tmp = rr[0:C, :, :].rearrange("p j c -> p (j c)")[:, 0:128]
        iota_b = sb("iota_b", [P, 128], bf16)
        dst_last = sb("dst_last", [P, CW])
        be2s = sb("be2s", [P, 1])
        tot = sb("tot", [P, 2])
        descents_i = sb("descents_i", [P, 1], i32)

        def filter_stage(slot):
            flat = stage[:, slot, :, :].rearrange("p t c -> p (t c)")
            return (flat[:, 0:TC * 34].rearrange("p (t c) -> p t c", c=34),
                    flat[:, TC * 34:TC * 68].rearrange("p (t c) -> p t c", c=34))

        dst_in_flat = dst_in[:, :, :, :].rearrange("p a t c -> p (a t c)")
        id_f, hi_f = (dst_in_flat[:, n * T:(n + 1) * T] for n in range(2))
        dst_i = dst_in_flat[:, 3 * T:4 * T].bitcast(i32)
        dst_f = dst_in_flat[:, 4 * T:5 * T]
        iota_f = dst_in_flat[:, 6 * T:6 * T + 128]
        hi_lo = dst_in_flat[:, 5 * T:6 * T].bitcast(bf16)

        def hot(slot):
            n = HB * (P + J) // 2
            b = (featT[0:P, :, :].rearrange("p a b -> p (a b)"), hidT[0:P, :, :].rearrange("p a b -> p (a b)"),
                 msg[:, 1, 0:n], msg[:, 1, n:2 * n])[slot].bitcast(bf16)
            return (b[:, 0:HB * P].rearrange("p (n t) -> p n t", t=HB),
                    b[:, HB * P:HB * (P + J)].rearrange("p (n t) -> p n t", t=HB))

        iota_rep = hid_negT[0:P, :, :].rearrange("p a b -> p (a b)").bitcast(bf16)[:, 0:HB * P]\
            .rearrange("p (n t) -> p n t", t=HB)

        sort_at = [0]

        def sort_tile(n):
            sort_at[0] += n
            return msg[:, 1, sort_at[0] - n:sort_at[0]]

        node_next, id_c, hi_c, lo_c = sort_tile(J), sort_tile(1), sort_tile(1), sort_tile(1)
        hi_hot, lo_hot, id_diag, hi_hotT, earlier = (sort_tile(n) for n in (P, J, P, P, P))
        base_lo, base, place_f, attr_c = sort_tile(J), sort_tile(1), sort_tile(1), sort_tile(C)
        src_c, dst_c, place_c = (sort_tile(1).bitcast(i32) for _ in range(3))

        def ends_view(width):
            return msg[:, 0, 0:J * width].rearrange("p (j c) -> p j c", c=width)

        aggregate = msg[:, 1, 0:J * 128].rearrange("p (j c) -> p j c", c=128)
        stage_flat = stage[:, 0, :, :].rearrange("p t c -> p (t c)")

        def carried_view(width):
            return stage_flat[:, 0:J * width].rearrange("p (j c) -> p j c", c=width)

        pair = stage[:, 1, :, :].rearrange("p t c -> p (t c)")
        diag = featT[0:P, :, :].rearrange("p a b -> p (a b)")[:, 0:H * P]
        seen = hidT[0:P, :, :].rearrange("p a b -> p (a b)")[:, 0:H * P]
        weights_pq = featT[0:P, :, :].rearrange("p a b -> p (a b)")[:, H * P:2 * H * P]

        bank = [pb(f"bank{i}") for i in range(8)]
        ps_featT, ps_hid, ps_le, ps_w, ps_misc = bank[0:2], bank[2:4], bank[4:6], bank[6], bank[7]

        s_const = sem("s_const")
        s_apart = sem("s_apart")
        s_idx_in = sem("s_idx_in")
        s_dst_in = sem("s_dst_in")
        s_ef_in = sem("s_ef_in")
        s_x_in = sem("s_x_in")
        s_descents = sem("s_descents")
        s_descents_mm = sem("s_descents_mm")
        s_order = sem("s_order")
        s_sort_v = sem("s_sort_v")
        s_sort_hot = sem("s_sort_hot")
        s_sort_row = sem("s_sort_row")
        s_sort_rank = sem("s_sort_rank")
        s_sort_sum = sem("s_sort_sum")
        s_sort_place = sem("s_sort_place")
        s_sort_moved = sem("s_sort_moved")
        s_sort_in = sem("s_sort_in")
        s_zero = sem("s_zero")
        s_zeroed = sem("s_zeroed")
        s_ones_col = sem("s_ones_col")
        s_v = sem("s_v")
        s_a = sem("s_a")
        s_att = sem("s_att")
        s_hot = sem("s_hot")
        s_hist = sem("s_hist")
        s_tot = sem("s_tot")
        s_off = sem("s_off")
        s_rows = sem("s_rows")
        s_rowsd = sem("s_rowsd")
        s_wlr = sem("s_wlr")
        s_setup = sem("s_setup")
        s_place = sem("s_place")
        s_owner_w = sem("s_owner_w")
        s_owner_r = sem("s_owner_r")
        s_ring = sem("s_ring")
        s_gather = [[sem(f"s_gather{slot}_{part}") for part in range(NPT)] for slot in range(2)]
        s_staged = sem("s_staged")
        s_ef = sem("s_ef")
        s_free = sem("s_free")
        s_dstrow = [sem("s_dstrow0"), sem("s_dstrow1")]
        s_filled = sem("s_filled")
        s_fscan = sem("s_fscan")
        s_fsub = sem("s_fsub")
        s_T = sem("s_T")
        s_featT = sem("s_featT")
        s_main = sem("s_main")
        s_hid = sem("s_hid")
        s_le = sem("s_le")
        s_lec = sem("s_lec")
        s_mcar = sem("s_mcar")
        s_lg = sem("s_lg")
        s_max = sem("s_max")
        s_max2 = sem("s_max2")
        s_arg = sem("s_arg")
        s_exp = sem("s_exp")
        s_mult = sem("s_mult")
        s_scan = sem("s_scan")
        s_store = [sem("s_store0"), sem("s_store1")]
        s_scatter = sem("s_scatter")
        s_first = sem("s_first")
        s_diag = sem("s_diag")
        s_bcast = sem("s_bcast")
        s_carg = sem("s_carg")
        s_cexp = sem("s_cexp")
        s_carry_mm = sem("s_carry_mm")
        s_carry = sem("s_carry")
        s_sel = sem("s_sel")
        s_selc = sem("s_selc")
        s_ends = [sem(f"s_ends{b}") for b in range(3)]
        s_narg = sem("s_narg")
        s_nexp = sem("s_nexp")
        s_agg = sem("s_agg")
        s_nT = sem("s_nT")
        s_nTc = sem("s_nTc")
        s_nh = sem("s_nh")
        s_nhc = sem("s_nhc")
        s_lr = sem("s_lr")
        s_xT = sem("s_xT")
        s_xTc = sem("s_xTc")
        s_no = sem("s_no")
        s_noc = sem("s_noc")
        s_var = sem("s_var")
        s_std = sem("s_std")
        s_sq = sem("s_sq")
        s_sqd = sem("s_sqd")
        s_gate = sem("s_gate")
        s_gated = sem("s_gated")
        s_elu = sem("s_elu")
        s_elud = sem("s_elud")
        s_table = sem("s_table")
        s_table_w = sem("s_table_w")
        s_out = sem("s_out")

        block = ctx.enter_context(nc.Block())

        def wait(eng, s, value):
            if isinstance(value, int) and value <= 0:
                return
            eng.wait_ge(s, value)

        def apart(eng):
            eng.sem_inc(s_apart, 1)

        def chunk_no(i, c):
            return i * NCH + c

        def dst_chunk_no(i, c):
            return before(i, lambda k: k["dst_w"]) * NCH + c

        def soft_chunk_no(i, c):
            return before(i, lambda k: k["heads"]) * NCH + c

        def group_no(i, c, g):
            return (before(i, lambda k: k["feat"]) * NCH + c) * NG + g

        def cols(c):
            return bass.ds(c * TC, TC)

        def slot_turn(i, c, slot):
            return i * (NCH // 2) + ((c - slot) // 2 if isinstance(c, int) else c)

        def chunks(eng, body):
            for slot in range(2):
                body(slot, slot, 0)
            with eng.Fori(1, NCH // 2) as k:
                for slot in range(2):
                    body(2 * k + slot, slot, k)

        SPLIT_FROM = 3

        def mlp_chunks(eng, i, body):
            split = PASSES[i] == "egat"
            for slot in range(2):
                body(slot, slot, 0, split and i > 0)
            for lo, hi in ((1, SPLIT_FROM), (SPLIT_FROM, NCH // 2)) if i == 0 else ((1, NCH // 2),):
                with eng.Fori(lo, hi) as k:
                    for slot in range(2):
                        body(2 * k + slot, slot, k, split and (i > 0 or lo > 1))

        def runs(split):
            if split:
                return [([part], t // GT, n // GT) for part, (t, n) in enumerate(PARTS)]
            return [(range(NPT), 0, NG)]

        NSEL = 3
        SEL = [(j, min(NSEL, J - j)) for j in range(0, J, NSEL)]
        BLOCKS = [(0, 8), (8, 8), (16, J - 16)]
        NBL = len(BLOCKS)
        GROUPS = [[(j, min(4, j0 + m0 - j)) for j in range(j0, j0 + m0, 4)] for j0, m0 in BLOCKS]
        NGR = sum(len(g) for g in GROUPS)

        def groups(b):
            at = sum(len(g) for g in GROUPS[:b])
            return [(at + n, j, m) for n, (j, m) in enumerate(GROUPS[b])]

        TPASS = [i for i in range(NP) if PASSES[i] == "egat"] + [3, 6]
        PROD = {"egat": dict(k=128, hid=None, m=C), "sage": dict(k=65, hid="sage1", m=2 * C),
                "gat": dict(k=128, hid="wfc", m=C)}

        def product_at(j, m, width):
            b = 0 if j < 8 else 1 if j < 16 else 2
            at = j - BLOCKS[b][0]
            per = 512 // width
            if at + m <= per:
                return [(j, m, (2, 3, 7)[b], at * width)]
            return ([(j, per - at, (2, 3, 7)[b], at * width)] if at < per else []) + \
                   [(max(j, BLOCKS[b][0] + per), at + m - max(per, at), 0, 0)]

        def prod_no(i):
            return sum(1 for t in TPASS if t < i)

        def hid_no(i):
            return sum(1 for t in TPASS if t < i and PROD[PASSES[t]]["hid"])

        def width(i):
            return {"egat": ROW, "gat": ROW, "filter": 66, "sage": C}[PASSES[i]]

        def descents(eng):
            eng.wait_ge(s_descents, 2)
            return eng.value_load(descents_i[0:1, 0:1])

        @block.sync
        def _(sp):
            def load_src(ids, done):
                rows = ids.rearrange("(p t) -> p t", t=T)
                sp.dma_start(src_i[:, 0:T], rows).then_inc(done, 16)
                sp.dma_start(src_i[:, T:T + 2 * TC], rows[:, 0:2 * TC]).then_inc(done, 16)

            def load_dst_ids(ids, done):
                rows = ids.rearrange("(p t) -> p t", t=T)
                sp.dma_start(dst_i, rows).then_inc(done, 16)
                sp.dma_start(prev_i[1:P, :], rows[0:P - 1, T - 1:T], allow_slow_non_contiguous=True).then_inc(done, 16)

            def load_attr(attr, done):
                rows = attr.rearrange("(p t) c -> p t c", t=T)
                sp.dma_start(edge_feat[0:EDGE_SPLIT, :, :], rows[0:EDGE_SPLIT]).then_inc(done, 16)
                sp.dma_start(edge_feat[EDGE_SPLIT:P, :, :], rows[EDGE_SPLIT:P]).then_inc(done, 16)

            load_dst_ids(dst, s_dst_in)
            sp.dma_start(CS[:, :], cpack[:, 0:CCOLS]).then_inc(s_const, 16)
            load_src(src, s_idx_in)
            sp.dma_start(W[:, :], wpack).then_inc(s_const, 16)
            sp.dma_start(iota_f, cpack[0:P, CCOLS:CCOLS + 128]).then_inc(s_dst_in, 16)
            sp.dma_start(X[:, :, :], x.rearrange("(p j) c -> p j c", j=J)).then_inc(s_x_in, 16)
            load_attr(edge_attr, s_ef_in)
            with sp.If(descents(sp) != 0):
                sp.wait_ge(s_sort_moved, 3 * 16 * T)
                load_src(sorted_src, s_sort_in)
                load_dst_ids(sorted_dst, s_sort_in)
                load_attr(sorted_attr, s_sort_in)
                sp.wait_ge(s_sort_in, 6 * 16)
            sp.sem_inc(s_order, 1)
            sp.wait_ge(s_zero, 1)
            rs = run_start_rows.rearrange("(p t) c -> p t c", t=T)
            for c in range(NCH):
                sp.dma_start(rs[:, c * TC:(c + 1) * TC, :],
                             msg[:, 0, 0:TC * CW].rearrange("p (t c) -> p t c", c=CW)).then_inc(s_zeroed, 16)
            sp.wait_ge(s_place, 1)
            sp.dma_start(carry_owner_d.rearrange("(p j) -> p j", j=J), nd[:, 6, :]).then_inc(s_owner_w, 16)
            sp.wait_ge(s_owner_w, 16)
            sp.dma_start(owner[:, :], carry_owner_d.rearrange("(a n) -> a n", a=1).broadcast_to([P, N])).then_inc(s_owner_r, 16)

            for i in range(NP):
                k = KIND[PASSES[i]]
                wd = width(i)
                rows = message_rows[PASSES[i]].rearrange("(p t) c -> p t c", t=T)
                if i == 0:
                    sp.wait_ge(s_rows, 1)
                    sp.dma_start(dst_table.rearrange("(p j) c -> p j c", j=J), nf[:, :, :]).then_inc(s_table_w, 16)
                else:
                    tw = k["src_w"]
                    from_ = (yt[:, :, :] if PASSES[i] == "egat" or i == 4 else X[:, :, :] if i == 3 else
                             pair[:, 0:J * tw].rearrange("p (j c) -> p j c", c=tw))
                    for b, (j, m) in enumerate(BLOCKS):
                        sp.wait_ge(s_table, (i - 1) * NBL + b + 1)
                        sp.dma_start(src_tables[i].rearrange("(p j) c -> p j c", j=J)[:, j:j + m, :],
                                     from_[:, j:j + m, :]).then_inc(s_table_w, 16)
                        if k["dst_w"]:
                            sp.dma_start(dst_table.rearrange("(p j) c -> p j c", j=J)[:, j:j + m, :],
                                         nf[:, j:j + m, :]).then_inc(s_table_w, 16)
                if k["dst_w"]:
                    sp.wait_ge(s_scatter, 16 * J * (before(i, lambda k: k["dst_w"]) + 1))

                def load_dst(c, slot, turn):
                    wait(sp, s_filled, dst_chunk_no(i, c) - 1)
                    sp.dma_start(dst_in[:, slot, :, :], rs[:, cols(c), :]).then_inc(s_dstrow[slot], 16)

                def store(c, slot, turn):
                    sp.wait_ge(s_scan, chunk_no(i, c) + 1)
                    m = msg[:, slot, 0:TC * wd].rearrange("p (t c) -> p t c", c=wd)
                    sp.dma_start(rows[0:EDGE_SPLIT, cols(c), :], m[0:EDGE_SPLIT]).then_inc(s_store[slot], 16)
                    sp.dma_start(rows[EDGE_SPLIT:P, cols(c), :], m[EDGE_SPLIT:P]).then_inc(s_store[slot], 16)

                if k["dst_w"]:
                    if i == 0:
                        sp.wait_ge(s_setup, 1)
                    for c in range(4):
                        load_dst(c, c % 2, c // 2)
                    for c in range(2):
                        store(c, c, 0)
                        load_dst(c + 4, c, 2)
                    with sp.Fori(1, NCH // 2 - 2) as kk:
                        for slot in range(2):
                            store(2 * kk + slot, slot, kk)
                            load_dst(2 * kk + 4 + slot, slot, kk + 2)
                    for c in range(NCH - 4, NCH):
                        store(c, c % 2, c // 2)
                else:
                    chunks(sp, store)
            for b, (j, m) in enumerate(BLOCKS):
                sp.wait_ge(s_table, (NP - 1) * NBL + b + 1)
                sp.dma_start(out.rearrange("(p j) c -> p j c", j=J)[:, j:j + m, :], X[:, j:j + m, :]).then_inc(s_out, 16)
            sp.wait_ge(s_out, 16 * NBL)

        @block.gpsimd
        def _(pool):
            at = bass.IndirectOffsetOnAxis

            def move_column(t):
                pool.wait_ge(s_sort_place, t + 1)
                apart(pool)
                for rows, col in ((sorted_attr, attr_c), (sorted_src.rearrange("(e a) -> e a", a=1), src_c),
                                  (sorted_dst.rearrange("(e a) -> e a", a=1), dst_c)):
                    pool.indirect_dma_start(rows, at(place_c, 0), col, None).then_inc(s_sort_moved, 16)

            with pool.If(descents(pool) != 0):
                with pool.Fori(0, T) as t:
                    move_column(t)

            tables = 0
            for i in range(NP):
                k = KIND[PASSES[i]]
                wd, tw = width(i), k["src_w"]
                def gather(c, slot, turn, lo=0, hi=TC):
                    pool.wait_ge(s_ring, chunk_no(i, c) + 1)
                    wait(pool, s_staged, (chunk_no(i, c) - 1) * NPT)
                    apart(pool)
                    for part, (t0, n) in enumerate(PARTS):
                        for t in range(max(t0, lo), min(t0 + n, hi)):
                            pool.indirect_dma_start(gathered[:, slot, t * tw:(t + 1) * tw], None, src_tables[i],
                                                    at(src_ring[:, slot, t:t + 1], 0)).then_inc(s_gather[slot][part], 16)

                def place(j):
                    pool.indirect_dma_start(run_start_rows, at(start_i[:, j:j + 1], 0), nf[:, j, :], None,
                                            bounds_check=E - 1, oob_is_err=False).then_inc(s_scatter, 16)

                def place_first():
                    pool.indirect_dma_start(dst_first[:, :], None, dst_table, at(first_i[:, 0:1], 0)).then_inc(s_first, 16)

                if i:
                    if k["dst_w"]:
                        pool.wait_ge(s_filled, dst_chunk_no(i, 0))
                        for b, (j0, m) in enumerate(BLOCKS):
                            pool.wait_ge(s_table, (i - 1) * NBL + b + 1)
                            for j in range(j0, j0 + m):
                                place(j)
                    tables += NBL * (2 if k["dst_w"] else 1)
                    pool.wait_ge(s_table_w, 16 * tables)
                    if k["dst_w"]:
                        place_first()
                    gather(0, 0, 0)
                    gather(1, 1, 0)
                else:
                    gather(0, 0, 0)
                    gather(1, 1, 0, 0, 8)
                    tables = 1
                    pool.wait_ge(s_place, 1)
                    pool.wait_ge(s_zeroed, 16 * NCH)
                    for j in range(J):
                        place(j)
                    pool.wait_ge(s_table_w, 16)
                    place_first()
                    gather(1, 1, 0, 8)
                with pool.Fori(1, NCH // 2) as kk:
                    for slot in range(2):
                        gather(2 * kk + slot, slot, kk)
                for slot in range(2):
                    pool.wait_ge(s_store[slot], 32 * (i + 1) * (NCH // 2))
                ends = ends_view(wd)
                for b, (j0, m) in enumerate(BLOCKS):
                    for j in range(j0, j0 + m):
                        pool.indirect_dma_start(ends[:, j, :], None, message_rows[PASSES[i]],
                                                at(end_i[:, j:j + 1], 0)).then_inc(s_ends[b], 16)

        @block.scalar
        def _(act):
            act.wait_ge(s_idx_in, 32)
            act.wait_ge(s_order, 1)
            for slot in range(2):
                act.copy(src_ring[:, slot, :], src_i[:, slot * TC:(slot + 1) * TC]).then_inc(s_ring, 1)
            act.wait_ge(s_const, 32)
            act.wait_ge(s_ef_in, 32)
            act.wait_ge(s_ones_col, 1)
            for i in range(NP):
                kind = PASSES[i]
                k = KIND[kind]
                nh = k["heads"]
                if i == 4:
                    act.wait_ge(s_sq, 1)
                    act.activation(tot[:, 1:2], tot[:, 1:2], ACT.Sqrt)
                    act.activation(sm[:, 6:8, :], sm[:, 6:8, :], ACT.Sqrt).then_inc(s_sqd, 1)
                    act.wait_ge(s_gate, 1)
                    act.activation(nd[:, 0, :], nd[:, 0, :], ACT.Exp, scale=-1.0).then_inc(s_gated, 1)

                def arrive(c, slot, turn, parts):
                    for part in parts:
                        act.wait_ge(s_gather[slot][part], 16 * PARTS[part][1] * (i * (NCH // 2) + turn + 1))
                    apart(act)
                    if parts[-1] == NPT - 1:
                        act.copy(src_ring[:, slot, :], src_i[:, bass.ds((c + 2) * TC, TC)]).then_inc(s_ring, 1)
                    if parts[0] == 0:
                        wait(act, s_free, chunk_no(i, c) - 1)
                    tw = k["src_w"]
                    t0, n = PARTS[parts[0]][0], sum(PARTS[part][1] for part in parts)
                    rows = gathered[:, slot, t0 * tw:(t0 + n) * tw].rearrange("p (t c) -> p t c", c=tw)
                    if kind == "filter":
                        features, rest = (v[:, t0:t0 + n, :] for v in filter_stage(slot))
                        act.copy(features[:, :, 33:34], rows[:, :, 0:1])
                        act.copy(rest, rows[:, :, 1:tw]).then_inc(s_staged, len(parts))
                    else:
                        act.copy(stage[:, slot, t0:t0 + n, 0:tw], rows).then_inc(s_staged, len(parts))
                    if kind == "egat":
                        act.copy(stage[:, slot, t0:t0 + n, 33:65], edge_feat[:, bass.ds(c * TC + t0, n), :])\
                           .then_inc(s_ef, len(parts))

                def feat_copy(c, g):
                    act.wait_ge(s_T, group_no(i, c, g) + 1)
                    wait(act, s_main, group_no(i, c, g) - 1)
                    n = GT // k["pair"] * P
                    act.copy(featT[0:k["feat"], g % 2, 0:n], ps_featT[g % 2][0:k["feat"], 0:n]).then_inc(s_featT, 1)

                def hidden(c, g):
                    act.wait_ge(s_main, group_no(i, c, g) + 1)
                    wait(act, s_le, group_no(i, c, g) - 1)
                    m = GT // k["pair"] * P
                    o, n = hidT[0:k["hid"], g % 2, 0:m], ps_hid[g % 2][0:k["hid"], 0:m]
                    if kind == "egat":
                        act.activation(o, n, ACT.Relu)
                        act.activation(hid_negT[0:k["hid"], g % 2, 0:GT * P], n, ACT.Relu, scale=-1.0).then_inc(s_hid, 1)
                    else:
                        act.activation(o, n, ACT.Relu, bias=w("be1", k["hid"])).then_inc(s_hid, 1)

                def logit_copy(c, slot, g):
                    act.wait_ge(s_le, group_no(i, c, g) + 1)
                    le = ps_le[g % 2][0:P, 0:GT * k["le"]].rearrange("p (t c) -> p t c", c=k["le"])
                    lg = logits[:, slot, 0:TC * nh].rearrange("p (t h) -> p t h", h=nh)[:, g * GT:(g + 1) * GT, :]
                    if kind == "egat":
                        last = act.copy(lg, le[:, :, 0:H])
                        if i < 2:
                            last = act.copy(edge_feat[:, bass.ds(c * TC + g * GT, GT), :], le[:, :, H:36])
                        last.then_inc(s_lec, 1)
                    else:
                        act.activation(lg, le, ACT.Identity, scale=10.0, bias=be2s[:, 0:1]).then_inc(s_lec, 1)

                def chunk(c, slot, turn, split):
                    for parts, g0, n in runs(split):
                        arrive(c, slot, turn, parts)
                        if kind == "filter" and isinstance(c, int) and c == 0:
                            act.wait_ge(s_place, 1)
                        for g in range(g0, g0 + n + 2) if k["feat"] else ():
                            if g < g0 + n:
                                feat_copy(c, g)
                            if g0 + 1 <= g <= g0 + n:
                                hidden(c, g - 1)
                            if g >= g0 + 2:
                                logit_copy(c, slot, g - 2)
                    if nh:
                        act.wait_ge(s_arg, soft_chunk_no(i, c) + 1)
                        act.activation(decay[:, 0:TC * nh], d_arg[:, 0:TC * nh], ACT.Exp)
                        act.activation(ps_w[0:P, 0:TC * nh], w_arg[:, 0:TC * nh], ACT.Exp).then_inc(s_exp, 1)

                mlp_chunks(act, i, chunk)

                if nh:
                    a = before(i, lambda k: k["heads"])
                    act.wait_ge(s_carg, a + 1)
                    for h in range(nh):
                        last = act.activation(weights_pq[:, h * P:(h + 1) * P], seen[:, h * P:(h + 1) * P], ACT.Exp,
                                              bias=tail[:, width(i) - nh + h:width(i) - nh + h + 1])
                    last.then_inc(s_cexp, 1)
                cv = carried_view(width(i))
                for n, (j, m) in enumerate(SEL):
                    act.wait_ge(s_sel, i * len(SEL) + n + 1)
                    act.copy(cv[:, j:j + m, :], bank[n % 2][0:P, 0:m * width(i)].rearrange("p (j c) -> p j c", c=width(i)))\
                       .then_inc(s_selc, 1)
                def end_weights(b):
                    if nh:
                        j, m = BLOCKS[b]
                        act.wait_ge(s_narg, a * NBL + b + 1)
                        act.activation(hw[:, 2:4, j * nh:(j + m) * nh], hw[:, 0:2, j * nh:(j + m) * nh], ACT.Exp)\
                           .then_inc(s_nexp, 1)

                def products(b):
                    if i not in TPASS:
                        return
                    pr = PROD[kind]
                    for n, j, m in groups(b):
                        g, hg = prod_no(i) * NGR + n, hid_no(i) * NGR + n
                        act.wait_ge(s_nT, g + 1)
                        act.copy(featT[0:pr["k"], n % 2, 0:m * P], bank[4 + n % 2][0:pr["k"], 0:m * P]).then_inc(s_nTc, 1)
                        if pr["hid"]:
                            act.wait_ge(s_nh, hg + 1)
                            o, v = hidT[:, n % 2, 0:m * P], bank[6][:, 0:m * P]
                            if kind == "sage":
                                act.activation(o, v, ACT.Relu).then_inc(s_nhc, 1)
                            else:
                                act.activation(o, v, ACT.Identity, bias=w("bias_gat")).then_inc(s_nhc, 1)

                def finish(b):
                    j, m = BLOCKS[b]
                    if kind == "gat":
                        act.wait_ge(s_elu, b + 1)
                        act.activation(rr[:, j:j + m, :], rr[:, j:j + m, :], ACT.Exp).then_inc(s_elud, 1)
                    if i in (2, 4, 5, 6):
                        act.wait_ge(s_var, (2, 4, 5, 6).index(i) * NBL + b + 1)
                        act.activation(sm[:, 2, j:j + m], sm[:, 2, j:j + m], ACT.Sqrt).then_inc(s_std, 1)
                    if kind == "filter":
                        for n, j, m in groups(b):
                            act.wait_ge(s_xT, n + 1)
                            act.copy(featT[0:C, n % 2, 0:m * P], bank[4 + n % 2][0:C, 0:m * P]).then_inc(s_xTc, 1)

                end_weights(0)
                end_weights(1)
                products(0)
                finish(0)
                end_weights(2)
                products(1)
                finish(1)
                products(2)
                finish(2)

        @block.tensor
        def _(pe):
            ident = cst("ident", P, P)
            ones = cst("ones", P, P)
            pe.wait_ge(s_const, 32)
            pe.wait_ge(s_descents, 1)
            pe.matmul(ps_misc[0:P, 65:66], ones, tot[:, 1:2], start=True, stop=True).then_inc(s_descents_mm, 1)

            def histogram(turn):
                def count(b, slot, start=False, stop=False):
                    pe.wait_ge(s_hot, turn * NHB + b + 1)
                    for t in range(HB):
                        last = pe.matmul(ps_misc[0:P, 0:J], hot(slot)[0][:, :, t], hot(slot)[1][:, :, t],
                                         start=start and t == 0, stop=stop and t == HB - 1)
                    last.then_inc(s_hist, 1)

                for slot in range(HSLOTS):
                    count(slot, slot, start=slot == 0)
                with pe.Fori(1, NHB // HSLOTS - 1) as kk:
                    for slot in range(HSLOTS):
                        count(HSLOTS * kk + slot, slot)
                for slot in range(HSLOTS):
                    count(NHB - HSLOTS + slot, slot, stop=slot == HSLOTS - 1)

            histogram(0)
            pe.wait_ge(s_tot, 1)
            pe.matmul(ps_misc[0:P, 64:65], cst("tri", P, P), tot[:, 0:1], start=True, stop=True).then_inc(s_off, 1)

            def rank_column(t):
                pe.wait_ge(s_sort_hot, t + 1)
                pe.matmul(bank[2][0:P, 0:P], ones, id_diag, start=True, stop=True)
                pe.transpose(bank[3][0:P, 0:P], hi_hot, ident).then_inc(s_sort_row, 1)
                pe.wait_ge(s_sort_rank, t + 1)
                pe.matmul(bank[4][0:P, 0:1], earlier, ones[:, 0:1], start=True, stop=True)
                pe.matmul(bank[5][0:P, 0:J], hi_hotT, node_next, start=True, stop=True)
                pe.matmul(bank[6][0:P, 0:J], hi_hot, lo_hot, start=True, stop=True).then_inc(s_sort_sum, 1)

            with pe.If(descents(pe) != 0):
                with pe.Fori(0, T) as t:
                    rank_column(t)
            pe.wait_ge(s_rowsd, 1)
            pe.matmul(bank[2][0:P, 0:2 * P], ones, diag[:, 0:2 * P], start=True, stop=True).then_inc(s_bcast, 1)

            for i in range(NP):
                kind = PASSES[i]
                k = KIND[kind]
                nh, wd = k["heads"], width(i)

                two = k.get("pair", 1)

                def transposes(c, slot, g):
                    wait(pe, s_featT, group_no(i, c, g) - 1)
                    for u in range(GT // two):
                        t = g * GT + two * u
                        last = pe.transpose(ps_featT[g % 2][0:k["feat"], u * P:(u + 1) * P],
                                            filter_stage(slot)[0][:, t:t + two, :].rearrange("p t c -> p (t c)")
                                            if kind == "filter" else stage[:, slot, t, 0:k["feat"]], ident)
                    last.then_inc(s_T, 1)

                def main(c, g):
                    pe.wait_ge(s_featT, group_no(i, c, g) + 1)
                    wait(pe, s_hid, group_no(i, c, g) - 1)
                    lhs = w("edge", 97)[:, i * 128:(i + 1) * 128] if kind == "egat" else w("filt1", k["feat"])
                    n = GT // two * P
                    pe.matmul(ps_hid[g % 2][0:k["hid"], 0:n], lhs, featT[0:k["feat"], g % 2, 0:n],
                              start=True, stop=True).then_inc(s_main, 1)

                def logit(c, g):
                    pe.wait_ge(s_hid, group_no(i, c, g) + 1)
                    wait(pe, s_lec, group_no(i, c, g) - 1)
                    n = k["le"]
                    if kind == "egat":
                        for t in range(GT):
                            o = ps_le[g % 2][0:P, t * n:(t + 1) * n]
                            pe.matmul(o, hidT[:, g % 2, t * P:(t + 1) * P], att[:, i, :], start=True, stop=False)
                            last = pe.matmul(o, hid_negT[:, g % 2, t * P:(t + 1) * P], att_neg[:, i, :],
                                             start=False, stop=True)
                    else:
                        for u in range(GT // two):
                            last = pe.matmul(ps_le[g % 2][0:P, u * two:(u + 1) * two],
                                             hidT[0:k["hid"], g % 2, u * P:(u + 1) * P], w("filt2", k["hid"]),
                                             start=True, stop=True)
                    last.then_inc(s_le, 1)

                def chunk(c, slot, turn, split):
                    pe.wait_ge(s_filled, dst_chunk_no(i, c) + 1)
                    for parts, g0, n in runs(split):
                        if kind == "egat":
                            pe.wait_ge(s_ef, (before(i, lambda k: k["feat"] == 97) * NCH + c) * NPT + parts[-1] + 1)
                        for g in range(g0, g0 + n + 2):
                            if g < g0 + n:
                                transposes(c, slot, g)
                            if g0 + 1 <= g <= g0 + n:
                                main(c, g - 1)
                            if g >= g0 + 2:
                                logit(c, g - 2)

                if k["feat"]:
                    if i == 0:
                        pe.wait_ge(s_att, 1)
                    mlp_chunks(pe, i, chunk)
                if i == 3:
                    histogram(1)
                if i == 4:
                    pe.wait_ge(s_wlr, 1)
                    pe.matmul(ps_misc[0:P, 64:65], ones, tot[:, 0:1], start=True, stop=True).then_inc(s_off, 1)
                    pe.wait_ge(s_wlr, 2)
                    pe.matmul(ps_misc[0:P, 65:66], ones, tot[:, 1:2], start=True, stop=True).then_inc(s_off, 1)

                if nh:
                    a = before(i, lambda k: k["heads"])
                    for r in range(2):
                        pe.wait_ge(s_diag, 2 * a + r + 1)
                        pe.matmul(bank[2][0:P, 0:nh * P], ones, diag[:, 0:nh * P], start=True, stop=True).then_inc(s_bcast, 1)
                    pe.wait_ge(s_cexp, a + 1)
                    for h in range(nh):
                        last = pe.matmul(bank[3][0:P, h * CW:(h + 1) * CW], weights_pq[:, h * P:(h + 1) * P],
                                         tail[:, h * CW:(h + 1) * CW], start=True, stop=True)
                else:
                    pe.wait_ge(s_scan, chunk_no(i, NCH))
                if k["plain"]:
                    p0 = nh * CW
                    src_rows = tail[:, p0:p0 + C] if nh else msg[:, 1, (TC - 1) * wd:(TC - 1) * wd + C]
                    last = pe.matmul(bank[3][0:P, p0:p0 + C], cont01[:, :], src_rows, start=True, stop=True)
                last.then_inc(s_carry_mm, 1)
                pe.wait_ge(s_carry, i + 1)
                own = owner[:, :].rearrange("q (p j) -> q j p", j=J)
                for n, (j, m) in enumerate(SEL):
                    wait(pe, s_selc, i * len(SEL) + n - 1)
                    for e in range(m):
                        last = pe.matmul(bank[n % 2][0:P, e * wd:(e + 1) * wd], own[:, j + e, :], carry[:, 0:wd],
                                         start=True, stop=True)
                    last.then_inc(s_sel, 1)
                def transposed(src_, rows, b, number, done, copied):
                    def transpose(n, j, m):
                        wait(pe, copied, number(n) - 1)
                        for e in range(m):
                            last = pe.transpose(bank[4 + n % 2][0:rows, e * P:(e + 1) * P], src_[:, j + e, 0:rows], ident)
                        last.then_inc(done, 1)

                    todo = groups(b)
                    transpose(*todo[0])
                    for at, (n, j, m) in enumerate(todo):
                        if at + 1 < len(todo):
                            transpose(*todo[at + 1])
                        pe.wait_ge(copied, number(n) + 1)
                        yield n, j, m

                for b in range(NBL):
                    if i in TPASS:
                        pr = PROD[kind]
                        out_w = pr["m"]
                        pe.wait_ge(s_agg, (i if i < 4 else i - 1) * NBL + b + 1)
                        for n, j, m in transposed(aggregate, pr["k"], b, lambda n: prod_no(i) * NGR + n, s_nT, s_nTc):
                            hg = hid_no(i) * NGR + n
                            lhs = featT
                            if pr["hid"]:
                                wait(pe, s_nhc, hg)
                                pe.matmul(bank[6][:, 0:m * P], w(pr["hid"], pr["k"]), featT[0:pr["k"], n % 2, 0:m * P],
                                          start=True, stop=True).then_inc(s_nh, 1)
                                pe.wait_ge(s_nhc, hg + 1)
                                lhs = hidT
                            rhs = w("node")[:, i * C:(i + 1) * C] if kind == "egat" else w({"sage": "sage2", "gat": "wout"}[kind])
                            for e in range(m):
                                (_, _, bk, at), = product_at(j + e, 1, out_w)
                                last = pe.matmul(bank[bk][0:P, at:at + out_w], lhs[:, n % 2, e * P:(e + 1) * P], rhs,
                                                 start=True, stop=True)
                        last.then_inc(s_no, 1)
                    if kind == "filter":
                        pe.wait_ge(s_agg, (i - 1) * NBL + b + 1)
                        for n, j, m in transposed(X, C, b, lambda n: n, s_xT, s_xTc):
                            for e in range(m):
                                (_, _, bk, at), = product_at(j + e, 1, 2 * H)
                                last = pe.matmul(bank[bk][0:P, at:at + 2 * H], featT[0:C, n % 2, e * P:(e + 1) * P],
                                                 wlr[:, :], start=True, stop=True)
                        last.then_inc(s_lr, 1)

        @block.vector
        def _(dve):
            chain = [0]

            def link(ins):
                chain[0] += 1
                ins.then_inc(s_v, 1)
                dve.wait_ge(s_v, chain[0])

            tt, ts, stt = dve.tensor_tensor, dve.tensor_scalar, dve.scalar_tensor_tensor
            IDENT = cst("ident", P, P)

            def bc(ap, n):
                s = [int(d) for d in ap.shape]
                return ap.unsqueeze(len(s)).broadcast_to(s + [n])

            dve.memset(msg[:, 0, 0:TC * CW], 0.0).then_inc(s_zero, 1)
            link(dve.memset(prev_i[0:1, :], -1))
            dve.memset(stage[:, :, :, 32:33], 1.0).then_inc(s_ones_col, 1)
            dve.wait_ge(s_dst_in, 48)
            dve.wait_ge(s_const, 32)
            dve.tensor_copy(same_neg[:, 0:1], prev_i[:, :])
            link(dve.tensor_copy(dst_f, dst_i[:, :]))
            tt(same[:, 0:1], dst_f[:, 0:1], same_neg[:, 0:1], ALU.is_lt)
            link(tt(same[:, 1:T], dst_f[:, 1:T], dst_f[:, 0:T - 1], ALU.is_lt))
            dve.tensor_reduce(tot[:, 1:2], same[:, :], AX, ALU.add).then_inc(s_descents, 1)
            dve.wait_ge(s_descents_mm, 1)
            dve.tensor_copy(descents_i[:, :], ps_misc[0:P, 65:66]).then_inc(s_descents, 1)

            def histogram(turn, ids):
                link(ts(hi_f, ids, 1.0 / J, 0.5 / J - 0.5, ALU.mult, ALU.add))
                link(ts(hi_f, hi_f, MAGIC, MAGIC, ALU.add, ALU.subtract))
                if turn == 0:
                    dve.tensor_copy(iota_b[:, :], iota_f)
                dve.tensor_copy(hi_lo[:, 0:T], hi_f)
                dve.tensor_copy(iota_rep, (iota_f if turn == 0 else iota_b)[:, 0:P].unsqueeze(2).broadcast_to([P, P, HB]))
                link(stt(hi_lo[:, T:2 * T], hi_f, -float(J), ids, ALU.mult, ALU.add))

                def build(b, slot):
                    wait(dve, s_hist, turn * NHB + b - HSLOTS + 1 if turn or not isinstance(b, int) or b >= HSLOTS else 0)
                    hi, lo = hi_lo[:, bass.ds(b * HB, HB)], hi_lo[:, bass.ds(b * HB + T, HB)]
                    tt(hot(slot)[0], hi.unsqueeze(1).broadcast_to([P, P, HB]), iota_rep, ALU.is_equal)
                    tt(hot(slot)[1], lo.unsqueeze(1).broadcast_to([P, J, HB]), iota_rep[:, 0:J, :], ALU.is_equal)\
                        .then_inc(s_hot, 1)

                for slot in range(HSLOTS):
                    build(slot, slot)
                with dve.Fori(1, NHB // HSLOTS) as kk:
                    for slot in range(HSLOTS):
                        build(HSLOTS * kk + slot, slot)
                dve.wait_ge(s_hist, (turn + 1) * NHB)

            histogram(0, dst_f)
            link(dve.tensor_copy(deg, ps_misc[0:P, 0:J]))
            START, ENDP, HAS, PEND, CROSS, INCL, OWN, CNEG, RDEG, DEG1 = range(10)
            GATE, RS_DST, HN, RS_SRC = START, ENDP, PEND, INCL

            def ndc(r):
                return nd[:, r, :]

            link(dve.tensor_tensor_scan(ndc(INCL), cst("ones", P, J), deg, 0.0, ALU.mult, ALU.add))
            dve.tensor_copy(tot[:, 0:1], nd[:, INCL, J - 1:J]).then_inc(s_tot, 1)
            link(ts(ndc(HAS), deg, 1.0, None, ALU.min))
            link(ts(ndc(DEG1), deg, 1.0, None, ALU.max))
            link(dve.reciprocal(ndc(RDEG), ndc(DEG1)))
            link(tt(ndc(START), ndc(INCL), deg, ALU.subtract))
            dve.wait_ge(s_off, 1)
            link(ts(ndc(START), ndc(START), ps_misc[0:P, 64:65], None, ALU.add))

            SORT_LINKS = 7

            def sort_column(t):
                linked = [0]

                def link_sort(ins):
                    linked[0] += 1
                    ins.then_inc(s_sort_v, 1)
                    dve.wait_ge(s_sort_v, t * SORT_LINKS + linked[0])

                wait(dve, s_sort_moved, t * (3 * 16))
                one = bass.ds(t, 1)
                dve.tensor_copy(attr_c, edge_feat[:, one, :].rearrange("p t c -> p (t c)"))
                dve.tensor_copy(src_c, src_i[:, one])
                dve.tensor_copy(dst_c, dst_i[:, one])
                dve.tensor_copy(id_c, dst_f[:, one])
                dve.tensor_copy(hi_c, hi_f[:, one])
                link_sort(dve.tensor_copy(lo_c, hi_lo[:, bass.ds(t + T, 1)]))
                ts(hi_hot, iota_f[:, 0:P], hi_c, None, ALU.is_equal)
                ts(lo_hot, iota_f[:, 0:J], lo_c, None, ALU.is_equal)
                ts(id_diag, IDENT, id_c, None, ALU.mult).then_inc(s_sort_hot, 1)
                dve.wait_ge(s_sort_row, t + 1)
                link_sort(ts(earlier, bank[2][0:P, 0:P], id_c, None, ALU.is_equal))
                dve.tensor_copy(hi_hotT, bank[3][0:P, 0:P])
                tt(earlier, earlier, cst("tri", P, P), ALU.mult).then_inc(s_sort_rank, 1)
                dve.wait_ge(s_sort_sum, t + 1)
                link_sort(tt(base_lo, bank[5][0:P, 0:J], lo_hot, ALU.mult))
                link_sort(dve.tensor_reduce(base, base_lo, AX, ALU.add))
                link_sort(tt(place_f, base, bank[4][0:P, 0:1], ALU.add))
                link_sort(tt(node_next, node_next, bank[6][0:P, 0:J], ALU.add))
                link_sort(dve.tensor_copy(place_c, place_f))
                assert linked[0] == SORT_LINKS
                dve.sem_inc(s_sort_place, 1)

            link(dve.tensor_copy(node_next, ndc(START)))
            with dve.If(descents(dve) != 0):
                dve.wait_ge(s_idx_in, 32)
                dve.wait_ge(s_ef_in, 32)
                sort_column(0)
                with dve.Fori(1, T) as t:
                    sort_column(t)
            dve.wait_ge(s_order, 1)
            dve.tensor_copy(first_i[:, :], dst_i[:, 0:1])
            dve.tensor_copy(dst_f, dst_i[:, :])
            link(stt(ndc(ENDP), ndc(START), -1.0, deg, ALU.add, ALU.add))
            link(ts(ndc(PEND), ndc(ENDP), 1.0 / T, 0.5 / T - 0.5, ALU.mult, ALU.add))
            link(ts(ndc(PEND), ndc(PEND), MAGIC, MAGIC, ALU.add, ALU.subtract))
            link(ts(ndc(CROSS), ndc(PEND), float(T), None, ALU.mult))
            link(tt(ndc(CROSS), ndc(START), ndc(CROSS), ALU.is_lt))
            link(tt(ndc(CROSS), ndc(CROSS), ndc(HAS), ALU.mult))
            link(stt(ndc(OWN), ndc(PEND), 1.0, ndc(CROSS), ALU.add, ALU.mult))
            link(ts(ndc(OWN), ndc(OWN), -1.0, None, ALU.add))
            link(ts(ndc(CNEG), ndc(CROSS), -1.0, BIG, ALU.add, ALU.mult))
            link(ts(ndc(ENDP), ndc(ENDP), 0.0, None, ALU.max))
            link(dve.tensor_copy(end_i[:, :], ndc(ENDP)))
            link(ts(ndc(INCL), ndc(HAS), -1.0, -1.0e6, ALU.add, ALU.mult))
            link(tt(ndc(INCL), ndc(INCL), ndc(START), ALU.add))
            link(dve.tensor_copy(start_i[:, :], ndc(INCL)))
            link(ts(be2s[:, :], w("be2", P), 10.0, None, ALU.mult))
            dve.wait_ge(s_x_in, 16)
            dve.memset(nf[:, :, C:CW], 0.0)
            dve.tensor_copy(nf[:, :, 0:C], X[:, :, :]).then_inc(s_rows, 1)
            dve.tensor_copy(same_neg[:, 0:1], prev_i[:, :]).then_inc(s_place, 1)
            dve.wait_ge(s_place, 1)
            tt(same[:, 0:1], dst_f[:, 0:1], same_neg[:, 0:1], ALU.is_equal)
            link(tt(same[:, 1:T], dst_f[:, 1:T], dst_f[:, 0:T - 1], ALU.is_equal))
            link(ts(same_neg[:, :], same[:, :], -1.0, BIG, ALU.add, ALU.mult))
            ts(diag[:, 0:P], IDENT, dst_f[:, T - 1:T], None, ALU.mult)
            ts(diag[:, P:2 * P], IDENT, dst_f[:, 0:1], None, ALU.mult).then_inc(s_rowsd, 1)
            for l in range(3):
                dve.tensor_copy(att[:, l, 0:H], w("att")[:, l * H:(l + 1) * H])
                last = dve.tensor_copy(att[:, l, H:36], cst("mean", 128))
            link(last)
            ts(att_neg[:, :, :], att[:, :, :], -NEG_SLOPE, None, ALU.mult).then_inc(s_att, 1)
            dve.wait_ge(s_bcast, 1)
            link(ts(cont01[:, :], bank[2][0:P, P:2 * P], dst_f[:, T - 1:T], None, ALU.is_equal))
            link(tt(cont01[:, :], cont01[:, :], cst("tri", P, P), ALU.mult))
            ts(cont_neg[:, :], cont01[:, :], -1.0, 1.0e36, ALU.add, ALU.mult)
            link(ts(contT_neg[:, :], bank[2][0:P, 0:P], dst_f[:, 0:1], None, ALU.is_equal))
            link(tt(contT_neg[:, :], contT_neg[:, :], cst("triT", P, P), ALU.mult))
            link(ts(contT_neg[:, :], contT_neg[:, :], -1.0, BIG, ALU.add, ALU.mult))
            dve.sem_inc(s_setup, 1)
            dve.wait_ge(s_owner_r, 16)
            link(ts(owner[:, :], owner[:, :], cst("col", P), None, ALU.is_equal))

            def degree_terms():
                link(dve.tensor_reduce(tot[:, 0:1], ndc(DEG1), AX, ALU.add))
                dve.sem_inc(s_wlr, 1)
                dve.wait_ge(s_off, 2)
                link(ts(tot[:, 0:1], ps_misc[0:P, 64:65], 1.0 / N, None, ALU.mult))
                link(ts(ndc(HN), ndc(DEG1), tot[:, 0:1], None, ALU.subtract))
                link(tt(sm[:, 5, :], ndc(HN), ndc(HN), ALU.mult))
                dve.tensor_reduce(tot[:, 1:2], sm[:, 5, :], AX, ALU.add).then_inc(s_wlr, 1)
                dve.wait_ge(s_off, 3)
                ts(tot[:, 1:2], ps_misc[0:P, 65:66], 1.0 / (N - 1), None, ALU.mult)
                dve.tensor_copy(sm[:, 6, :], ndc(DEG1))
                ts(sm[:, 7, :], sdeg[:, :], 1.0, None, ALU.max).then_inc(s_sq, 1)
                dve.wait_ge(s_sqd, 1)
                link(ts(tot[:, 1:2], tot[:, 1:2], 1e-8, None, ALU.add))
                link(dve.reciprocal(tot[:, 1:2], tot[:, 1:2]))
                link(ts(ndc(HN), ndc(HN), tot[:, 1:2], None, ALU.mult))
                dve.reciprocal(ndc(RS_DST), sm[:, 6, :])
                link(dve.reciprocal(ndc(RS_SRC), sm[:, 7, :]))
                gw = dst_in_flat[:, 0:J * 16].rearrange("p (j c) -> p j c", c=16)

                def w16(name):
                    return w(name, P).unsqueeze(1).broadcast_to([P, J, 16])

                link(tt(gw, bc(ndc(HN), 16), w16("wn1"), ALU.mult))
                link(tt(gw, gw, w16("bn1"), ALU.add))
                link(ts(gw, gw, 0.0, None, ALU.max))
                link(tt(gw, gw, w16("wn2"), ALU.mult))
                link(dve.tensor_reduce(ndc(GATE), gw, AX, ALU.add))
                ts(ndc(GATE), ndc(GATE), w("bn2", P), None, ALU.add).then_inc(s_gate, 1)
                dve.wait_ge(s_gated, 1)
                link(ts(ndc(GATE), ndc(GATE), 1.0, None, ALU.add))
                link(dve.reciprocal(ndc(GATE), ndc(GATE)))

            for i in range(NP):
                kind = PASSES[i]
                k = KIND[kind]
                nh, wd, dw = k["heads"], width(i), k["dst_w"]
                plain = k["plain"]

                def msg3(slot):
                    return msg[:, slot, 0:TC * wd].rearrange("p (t c) -> p t c", c=wd)

                def fill(c, slot, turn):
                    dve.wait_ge(s_dstrow[slot], 16 * (before(i, lambda k: k["dst_w"]) * (NCH // 2) + turn + 1))
                    wait(dve, s_free, chunk_no(i, c) - 1)
                    first = isinstance(c, int) and c == 0
                    if first:
                        dve.wait_ge(s_first, 16 * (before(i, lambda k: k["dst_w"]) + 1))
                    if kind == "filter":
                        wait(dve, s_fsub, 2 * c - 1)
                    else:
                        wait(dve, s_filled, dst_chunk_no(i, c))
                    into = (filter_stage(slot)[0] if kind == "filter" else stage[:, slot, :, :])[:, :, k["dst_at"]:k["dst_at"] + dw]
                    for ch in range(dw):
                        init = dst_first[:, ch:ch + 1] if first else dst_last[:, ch:ch + 1]
                        last = dve.tensor_tensor_scan(into[:, :, ch], same[:, cols(c)], dst_in[:, slot, :, ch],
                                                      init, ALU.mult, ALU.add)
                    last.then_inc(s_fscan, 1)
                    dve.wait_ge(s_fscan, dst_chunk_no(i, c) + 1)
                    last = dve.tensor_copy(dst_last[:, 0:dw], into[:, TC - 1, :])
                    last.then_inc(s_fsub if kind == "filter" else s_filled, 1)

                def difference(c, slot):
                    dve.wait_ge(s_staged, (chunk_no(i, c) + 1) * NPT)
                    dve.wait_ge(s_fsub, 2 * c + 1)
                    d, rest = filter_stage(slot)[0][:, :, 0:C], filter_stage(slot)[1]
                    tt(d, d, rest[:, :, 0:C], ALU.subtract).then_inc(s_fsub, 1)
                    dve.wait_ge(s_fsub, 2 * c + 2)
                    stt(d, d, -1.0, d, ALU.mult, ALU.max).then_inc(s_filled, 1)

                def head_view(buf):
                    return buf.rearrange("p (t h) -> p t h", h=nh)

                def maxima(c, slot, turn):
                    first = isinstance(c, int) and c == 0
                    sc = soft_chunk_no(i, c)
                    lg = head_view(logits[:, slot, 0:TC * nh])
                    if first:
                        dve.memset(run_max[:, 0, 0:nh], -BIG).then_inc(s_mcar, 1)
                    else:
                        dve.tensor_copy(run_max[:, 0, 0:nh], run_max[:, TC, 0:nh]).then_inc(s_mcar, 1)
                    if kind == "gat":
                        dve.wait_ge(s_staged, (chunk_no(i, c) + 1) * NPT)
                        dve.wait_ge(s_filled, dst_chunk_no(i, c) + 1)
                        tt(head_view(w_arg[:, 0:TC * nh]), stage[:, slot, :, 33:37], stage[:, slot, :, 40:44], ALU.add)\
                            .then_inc(s_lg, 1)
                        dve.wait_ge(s_lg, 2 * c + 1)
                        stt(lg, head_view(w_arg[:, 0:TC * nh]), NEG_SLOPE, head_view(w_arg[:, 0:TC * nh]), ALU.mult, ALU.max)\
                            .then_inc(s_lg, 1)
                        dve.wait_ge(s_lg, 2 * c + 2)
                    else:
                        dve.wait_ge(s_lec, group_no(i, c, NG))
                    dve.wait_ge(s_mcar, sc + 1)
                    for h in range(nh):
                        last = dve.tensor_tensor_scan(run_max[:, 1:TC + 1, h], same_neg[:, cols(c)], lg[:, :, h],
                                                      run_max[:, 0, h:h + 1], ALU.add, ALU.max)
                    last.then_inc(s_max, 1)
                    dve.wait_ge(s_max, sc + 1)
                    wait(dve, s_exp, sc)
                    tt(head_view(w_arg[:, 0:TC * nh]), lg, run_max[:, 1:TC + 1, 0:nh], ALU.subtract)
                    tt(head_view(d_arg[:, 0:TC * nh]), run_max[:, 0:TC, 0:nh], run_max[:, 1:TC + 1, 0:nh], ALU.subtract)\
                        .then_inc(s_max2, 1)
                    dve.wait_ge(s_max2, sc + 1)
                    tt(head_view(d_arg[:, 0:TC * nh]), head_view(d_arg[:, 0:TC * nh]), bc(same_neg[:, cols(c)], nh), ALU.add)\
                        .then_inc(s_arg, 1)

                def weigh(c, slot, turn):
                    if not (isinstance(c, int) and i == 0 and c < 2):
                        dve.wait_ge(s_store[slot], 32 * (i * (NCH // 2) + turn))
                    m3 = msg3(slot)
                    if plain:
                        rest = filter_stage(slot)[1]
                        tt(m3[:, :, CW:CW + C], rest[:, :, 0:C], bc(rest[:, :, 33], C), ALU.mult)
                    dve.wait_ge(s_exp, soft_chunk_no(i, c) + 1)
                    dve.tensor_copy(m3[:, :, wd - nh:wd], run_max[:, 1:TC + 1, 0:nh])
                    if nh > 1:
                        o = m3[:, :, 0:nh * CW].rearrange("p t (h c) -> p t h c", c=CW)
                        wgt = bc(head_view(ps_w[0:P, 0:TC * nh]), CW)
                        row = stage[:, slot, :, 0:CW].unsqueeze(2).broadcast_to([P, TC, nh, CW])
                    else:
                        o = m3[:, :, 0:CW]
                        wgt = bc(ps_w[0:P, 0:TC], CW)
                        row = filter_stage(slot)[1][:, :, 0:CW]
                    tt(o, wgt, row, ALU.mult).then_inc(s_mult, 1)
                    if not plain:
                        dve.wait_ge(s_mult, soft_chunk_no(i, c) + 1)
                        dve.sem_inc(s_free, 1)

                def sums(c, slot, turn):
                    first = isinstance(c, int) and c == 0
                    m3, p3 = msg3(slot), msg3(1 - slot)
                    wait(dve, s_scan, chunk_no(i, c))
                    if nh:
                        dve.wait_ge(s_mult, soft_chunk_no(i, c) + 1)
                    else:
                        dve.wait_ge(s_staged, (chunk_no(i, c) + 1) * NPT)
                        if not (isinstance(c, int) and i == 0 and c < 2):
                            dve.wait_ge(s_store[slot], 32 * (i * (NCH // 2) + turn))
                    dv = head_view(decay[:, 0:TC * nh]) if nh else None
                    for h in range(nh):
                        for ch in range(CW):
                            q = h * CW + ch
                            last = dve.tensor_tensor_scan(m3[:, :, q], dv[:, :, h], m3[:, :, q],
                                                          0.0 if first else p3[:, TC - 1, q:q + 1], ALU.mult, ALU.add)
                    for ch in range(plain):
                        q = nh * CW + ch
                        last = dve.tensor_tensor_scan(m3[:, :, q], same[:, cols(c)],
                                                      m3[:, :, q] if nh else stage[:, slot, :, ch],
                                                      0.0 if first else p3[:, TC - 1, q:q + 1], ALU.mult, ALU.add)
                    last.then_inc(s_scan, 1)
                    if plain:
                        dve.wait_ge(s_scan, chunk_no(i, c) + 1)
                        dve.sem_inc(s_free, 1)

                if kind == "egat" and i:
                    link(dve.memset(stage[:, :, :, 32:33], 1.0))
                if nh:
                    def step(c, slot, turn, last=False):
                        if kind == "filter":
                            difference(c, slot)
                        if not (isinstance(c, int) and c == 0):
                            sums(c - 1, 1 - slot, turn - 1 + slot)
                        if not last:
                            fill(c + 1, 1 - slot, turn + slot)
                        maxima(c, slot, turn)
                        weigh(c, slot, turn)

                    fill(0, 0, 0)
                    step(0, 0, 0)
                    step(1, 1, 0)
                    with dve.Fori(1, NCH // 2 - 1) as kk:
                        for slot in range(2):
                            step(2 * kk + slot, slot, kk)
                    step(NCH - 2, 0, NCH // 2 - 1)
                    step(NCH - 1, 1, NCH // 2 - 1, last=True)
                    sums(NCH - 1, 1, NCH // 2 - 1)
                else:
                    if i == 3:
                        link(dve.tensor_copy(id_f, src_i[:, 0:T]))
                        histogram(1, id_f)
                        link(dve.tensor_copy(sdeg[:, :], ps_misc[0:P, 0:J]))
                    if i == 4:
                        degree_terms()
                    chunks(dve, sums)

                a = before(i, lambda k: k["heads"])
                if nh:
                    m0 = wd - nh
                    dve.wait_ge(s_scan, chunk_no(i, NCH))
                    link(dve.tensor_copy(tail[:, 0:wd], msg[:, 1, (TC - 1) * wd:TC * wd]))
                    for h in range(nh):
                        last = ts(diag[:, h * P:(h + 1) * P], IDENT, tail[:, m0 + h:m0 + h + 1], None, ALU.mult)
                    last.then_inc(s_diag, 1)
                    dve.wait_ge(s_bcast, 1 + 2 * a + 1)
                    v3 = seen[:, 0:nh * P].rearrange("p (h q) -> p h q", q=P)
                    b3 = bank[2][0:P, 0:nh * P].rearrange("p (h q) -> p h q", q=P)
                    link(tt(v3, b3, contT_neg[:, :].unsqueeze(1).broadcast_to([P, nh, P]), ALU.add))
                    link(dve.tensor_reduce(carry_max[:, 0:nh], v3, AX, ALU.max))
                    for h in range(nh):
                        last = ts(diag[:, h * P:(h + 1) * P], IDENT, carry_max[:, h:h + 1], None, ALU.mult)
                    last.then_inc(s_diag, 1)
                    dve.wait_ge(s_bcast, 1 + 2 * a + 2)
                    tt(v3, cont_neg[:, :].unsqueeze(1).broadcast_to([P, nh, P]), b3, ALU.subtract).then_inc(s_carg, 1)
                dve.wait_ge(s_carry_mm, i + 1)
                if nh:
                    dve.tensor_copy(carry[:, m0:wd], carry_max[:, 0:nh])
                dve.tensor_copy(carry[:, 0:nh * CW + plain], bank[3][0:P, 0:nh * CW + plain]).then_inc(s_carry, 1)
                dve.wait_ge(s_selc, (i + 1) * len(SEL))
                en, cv = ends_view(wd), carried_view(wd)
                if nh:
                    link(tt(cv[:, :, m0:wd], cv[:, :, m0:wd], bc(ndc(CNEG), nh), ALU.add))

                def aggregate_block(b):
                    j0, m = BLOCKS[b]
                    js = slice(j0, j0 + m)
                    dve.wait_ge(s_ends[b], 16 * m * (i + 1))
                    e, v = en[:, js, :], cv[:, js, :]
                    has, x = ndc(HAS)[:, js], X[:, js, :]
                    if not nh:
                        link(tt(e, e, bc(has, C), ALU.mult))
                        link(tt(e, e, v, ALU.add))
                        if i == 3:
                            tt(aggregate[:, js, 0:C], e, bc(ndc(RDEG)[:, js], C), ALU.mult)
                            dve.memset(aggregate[:, js, 64:65], 1.0)
                            dve.tensor_copy(aggregate[:, js, C:2 * C], x).then_inc(s_agg, 1)
                        else:
                            link(tt(e, e, bc(ndc(RDEG)[:, js], C), ALU.mult))
                        return

                    def hv(r):
                        return hw[:, r, j0 * nh:(j0 + m) * nh].rearrange("p (j h) -> p j h", h=nh)

                    link(tt(hv(4), e[:, :, m0:wd], v[:, :, m0:wd], ALU.max))
                    tt(hv(0), e[:, :, m0:wd], hv(4), ALU.subtract)
                    tt(hv(1), v[:, :, m0:wd], hv(4), ALU.subtract).then_inc(s_narg, 1)
                    dve.wait_ge(s_nexp, a * NBL + b + 1)
                    tt(hv(0), hv(2), e[:, :, C:nh * CW:CW], ALU.mult)
                    link(tt(hv(1), hv(3), v[:, :, C:nh * CW:CW], ALU.mult))
                    link(tt(hv(4), hv(0), hv(1), ALU.add))
                    if kind == "filter":
                        link(ts(hv(0), hv(4), 1e-16, None, ALU.add))
                        link(dve.reciprocal(hv(0), hv(0)))
                    elif kind == "gat":
                        link(ts(hv(4), hv(4), 1e-9, None, ALU.max))
                        link(dve.reciprocal(hv(0), hv(4)))
                    else:
                        link(dve.reciprocal(hv(0), hv(4)))
                    link(tt(hv(0), hv(0), bc(has, nh), ALU.mult))
                    tt(hv(2), hv(2), hv(0), ALU.mult)
                    link(tt(hv(3), hv(3), hv(0), ALU.mult))

                    def chans(t):
                        return t[:, :, 0:nh * CW].rearrange("p j (h c) -> p j h c", c=CW)[:, :, :, 0:C] if nh > 1 else t[:, :, 0:C]

                    def share(r):
                        return bc(hv(r), C) if nh > 1 else bc(hw[:, r, js], C)

                    ag = aggregate[:, js, 0:nh * C]
                    if nh > 1:
                        ag = ag.rearrange("p j (h c) -> p j h c", c=C)
                    tt(chans(v), chans(v), share(3), ALU.mult)
                    link(tt(ag, chans(e), share(2), ALU.mult))
                    last = tt(ag, ag, chans(v), ALU.add)
                    if kind == "filter":
                        link(last)
                    else:
                        last.then_inc(s_agg, 1)

                def layer_norm(b, r):
                    j0, m = BLOCKS[b]
                    js = slice(j0, j0 + m)
                    y, sq = yt[:, js, :], rr[:, js, :]
                    link(dve.tensor_reduce(sm[:, 0, js], y, AX, ALU.add))
                    link(ts(sm[:, 0, js], sm[:, 0, js], 1.0 / C, None, ALU.mult))
                    link(tt(y, y, bc(sm[:, 0, js], C), ALU.subtract))
                    link(tt(sq, y, y, ALU.mult))
                    link(dve.tensor_reduce(sm[:, 1, js], sq, AX, ALU.add))
                    ts(sm[:, 2, js], sm[:, 1, js], 1.0 / C, LN_EPS, ALU.mult, ALU.add).then_inc(s_var, 1)
                    dve.wait_ge(s_std, r * NBL + b + 1)
                    link(dve.reciprocal(sm[:, 3, js], sm[:, 2, js]))
                    return tt(X[:, js, :], y, bc(sm[:, 3, js], C), ALU.mult)

                def update_block(b):
                    j0, m = BLOCKS[b]
                    js = slice(j0, j0 + m)
                    x, y = X[:, js, :], yt[:, js, :]
                    if i in TPASS:
                        dve.wait_ge(s_no, prod_no(i) * NBL + b + 1)
                        out_w = PROD[kind]["m"]
                        prods = [(slice(j, j + n), n, bank[bk][0:P, at:at + n * out_w].rearrange("p (j c) -> p j c", c=out_w))
                                 for j, n, bk, at in product_at(j0, m, out_w)]
                    if kind == "egat":
                        for q, n, v in prods:
                            if i < 2:
                                ts(nf[:, q, 0:C], v, 1.0 / H, None, ALU.mult)
                                ts(yt[:, q, :], v, 1.0 / H, None, ALU.mult).then_inc(s_table, 1)
                            else:
                                link(stt(yt[:, q, :], v, 1.0 / H, X[:, q, :], ALU.mult, ALU.add))
                        if i == 2:
                            layer_norm(b, 0).then_inc(s_table, 1)
                    if i == 3:
                        for q, n, v in prods:
                            dve.tensor_copy(rr[:, q, :], v[:, :, C:2 * C])
                            last = dve.tensor_copy(yt[:, q, :], v[:, :, 0:C])
                        last.then_inc(s_table, 1)
                    if i == 4:
                        e = en[:, js, :]
                        link(tt(e, e, rr[:, js, :], ALU.add))
                        link(tt(e, e, w("b2", P).unsqueeze(1).broadcast_to([P, m, C]), ALU.add))
                        link(tt(y, e, x, ALU.add))
                        link(layer_norm(b, 1))
                        tb = pair[:, 0:J * 35].rearrange("p (j c) -> p j c", c=35)[:, js, :]
                        dve.tensor_copy(tb[:, :, 0:1], ndc(HN)[:, js].unsqueeze(2))
                        dve.tensor_copy(tb[:, :, 1:33], x)
                        dve.memset(tb[:, :, 33:34], 1.0)
                        dve.tensor_copy(tb[:, :, 34:35], ndc(RS_SRC)[:, js].unsqueeze(2))
                        dve.tensor_copy(nf[:, js, 0:C], x)
                        dve.tensor_copy(nf[:, js, C:CW], ndc(HN)[:, js].unsqueeze(2)).then_inc(s_table, 1)
                    if kind == "filter":
                        low, low_c = en[:, js, CW:CW + C], cv[:, js, CW:CW + C]
                        link(tt(low, low, bc(ndc(HAS)[:, js], C), ALU.mult))
                        link(tt(low, low, low_c, ALU.add))
                        link(tt(low, low, bc(ndc(RS_DST)[:, js], C), ALU.mult))
                        link(tt(hw[:, 4, js], hw[:, 4, js], hw[:, 0, js], ALU.mult))
                        link(tt(y, x, bc(hw[:, 4, js], C), ALU.mult))
                        link(tt(y, y, aggregate[:, js, 0:C], ALU.subtract))
                        link(tt(y, y, low, ALU.subtract))
                        link(tt(y, y, bc(ndc(GATE)[:, js], C), ALU.mult))
                        link(tt(y, y, low, ALU.add))
                        link(tt(y, y, x, ALU.add))
                        layer_norm(b, 2).then_inc(s_agg, 1)
                    if kind == "gat":
                        for q, n, v in prods:
                            link(tt(yt[:, q, :], v, w("bout", P).unsqueeze(1).broadcast_to([P, n, C]), ALU.add))
                        r = rr[:, js, :]
                        ts(r, y, 0.0, None, ALU.min).then_inc(s_elu, 1)
                        link(ts(y, y, 0.0, None, ALU.max))
                        dve.wait_ge(s_elud, b + 1)
                        link(stt(r, r, -1.0, y, ALU.add, ALU.add))
                        link(stt(y, x, 2.0, r, ALU.mult, ALU.add))
                        layer_norm(b, 3).then_inc(s_table, 1)

                def gat_rows(b):
                    if kind != "filter":
                        return
                    j0, m = BLOCKS[b]
                    js = slice(j0, j0 + m)
                    dve.wait_ge(s_lr, b + 1)
                    (_, _, bk, at), = product_at(j0, m, 2 * H)
                    lr = bank[bk][0:P, at:at + m * 2 * H].rearrange("p (j c) -> p j c", c=2 * H)
                    tb = pair[:, 0:J * 37].rearrange("p (j c) -> p j c", c=37)[:, js, :]
                    dve.tensor_copy(tb[:, :, 0:C], X[:, js, :])
                    dve.memset(tb[:, :, C:CW], 1.0)
                    dve.tensor_copy(tb[:, :, 33:37], lr[:, :, 0:H])
                    dve.tensor_copy(nf[:, js, 0:H], lr[:, :, H:2 * H]).then_inc(s_table, 1)

                if kind == "filter":
                    for s in range(2):
                        link(tt(lr_tmp, w("wfc_row", C), w("attn_lr", C)[:, s * 128:(s + 1) * 128], ALU.mult))
                        link(dve.tensor_reduce(wlr[:, s * H:(s + 1) * H], lr_tmp.rearrange("c (h d) -> c h d", d=C), AX, ALU.add))
                aggregate_block(0)
                aggregate_block(1)
                update_block(0)
                aggregate_block(2)
                update_block(1)
                gat_rows(0)
                update_block(2)
                gat_rows(1)
                gat_rows(2)


def pack_weights(np, a):
    wp = np.zeros((128, WCOLS), np.float32)

    def put(name, rows, block, col=0, row=0):
        wp[row:row + rows, W_OFF[name][0] + col:W_OFF[name][0] + col + block.shape[1]] = block

    for l in range(3):
        put("edge", C, a["L0_gnn_W_ni"][l], l * 128, 0)
        put("edge", 1, a["L0_gnn_bias"][l][None], l * 128, 32)
        put("edge", C, a["L0_gnn_W_fij"][l], l * 128, 33)
        put("edge", C, a["L0_gnn_W_nj"][l], l * 128, 65)
        for h in range(H):
            put("att", C, a["L0_gnn_attn"][l, h][:, None], l * H + h, h * C)
            put("node", C, a["L0_gnn_W_node"][l][:, h * C:(h + 1) * C], l * C, h * C)
    put("sage1", C, a["L1_gnn_W1_l"].T)
    put("sage1", C, a["L1_gnn_W1_r"].T, 0, C)
    put("sage1", 1, a["L1_gnn_b1"][None], 0, 2 * C)
    put("sage2", 128, a["L1_gnn_W2_l"].T)
    put("sage2", 128, a["L1_gnn_W2_r"].T, C)
    for u in range(2):
        put("filt1", C, a["L2_gnn_We1"][2:], u * 32, u * 34)
        put("filt1", 1, a["L2_gnn_We1"][1:2], u * 32, u * 34 + C)
        put("filt1", 1, a["L2_gnn_We1"][0:1], u * 32, u * 34 + C + 1)
        put("filt2", 32, a["L2_gnn_We2"], u, u * 32)
        put("be1", 32, a["L2_gnn_be1"][:, None], 0, u * 32)
    for h in range(H):
        put("wfc", C, a["L3_gnn_W_fc"][:, h * C:(h + 1) * C], h * C, h * C)
    put("wfc_row", C, a["L3_gnn_W_fc"])
    put("attn_lr", C, np.tile(a["L3_gnn_attn_l"].reshape(1, -1), (C, 1)))
    put("attn_lr", C, np.tile(a["L3_gnn_attn_r"].reshape(1, -1), (C, 1)), 128)
    put("wout", 128, a["L3_gnn_W_out"])
    put("bias_gat", 128, a["L3_gnn_bias_gat"][:, None])
    for name, v in (("be2", a["L2_gnn_be2"]), ("b2", a["L1_gnn_b2"]), ("bout", a["L3_gnn_b_out"]),
                    ("wn1", a["L2_gnn_Wn1"]), ("bn1", a["L2_gnn_bn1"]), ("wn2", a["L2_gnn_Wn2"]),
                    ("bn2", a["L2_gnn_bn2"])):
        put(name, 128, np.tile(v.reshape(1, -1), (128, 1)))
    return wp


def pack_constants(np):
    c = np.zeros((128, CCOLS + 128), np.float32)
    c[:, 0:128] = np.eye(128)
    c[:, 128:256] = 1.0
    c[:, 256:384] = np.triu(np.ones((128, 128)), 1)
    c[:, 384:512] = np.tril(np.ones((128, 128)), -1)
    c[:, 512:544] = np.tile(np.eye(C), (H, 1)) / H
    c[:, 544] = np.arange(128)
    c[:, 545:673] = np.arange(128)[None]
    return c


def build(nc):
    f32, i32 = mybir.dt.float32, mybir.dt.int32
    shapes = {"x": ((N, C), f32), "src": ((E,), i32), "dst": ((E,), i32), "edge_attr": ((E, C), f32),
              "wpack": ((128, WCOLS), f32), "cpack": ((128, CCOLS + 128), f32)}
    ins = [nc.dram_tensor(n, s, d, kind="ExternalInput").ap() for n, (s, d) in shapes.items()]
    out = nc.dram_tensor("out", (N, C), f32, kind="ExternalOutput").ap()
    graph_kernel(nc, *ins, out)


def kernel(**inputs):
    import numpy as np
    import concourse.bacc as bacc
    from concourse.bass_utils import run_bass_kernel_spmd

    a = {n: np.ascontiguousarray(v) for n, v in inputs.items()}
    nc = bacc.Bacc("TRN2", target_bir_lowering=False, num_devices=1)
    build(nc)
    arrays = {"x": a["x"], "src": a["src"], "dst": a["dst"], "edge_attr": a["edge_attr_32"],
              "wpack": pack_weights(np, a), "cpack": pack_constants(np)}
    r = run_bass_kernel_spmd(nc, [arrays], core_ids=[0])
    return r.results[0]["out"]
```
